# Optimizing a Trainium2 kernel written in Bass

```python
import numpy as np
import jax
import jax.numpy as jnp

def _softmax(x, axis=-1):
    return jax.nn.softmax(x, axis=axis)

def _gelu(x):
    return jax.nn.gelu(x, approximate=True)

def _silu(x):
    return jax.nn.silu(x)

def _sigmoid(x):
    return jax.nn.sigmoid(x)

def _layernorm(x, axis=-1, eps=1e-05):
    m = jnp.mean(x, axis=axis, keepdims=True)
    v = jnp.var(x, axis=axis, keepdims=True)
    return (x - m) / jnp.sqrt(v + eps)

def _scatter_add(tgt, idx, src, axis=0):
    return tgt.at[idx].add(src)

def _segment_sum(src, seg, n):
    return jax.ops.segment_sum(src, seg, n)
kernel_name = 'mk_adaln_attn_ffn_d1_seqx_r4_0b67e6'

def setup_inputs(seed: int=0):
    np.random.seed(seed)
    _w = jnp.asarray

    def _rec_inputs():
        import jax
        import jax.numpy as jnp
        _rk = jax.random.key(seed)
        x = -0.000125 + 0.9999 * jax.random.normal(jax.random.fold_in(_rk, 1), (32, 64, 512), jnp.float32)
        _lenS = 64 - jax.random.randint(jax.random.fold_in(_rk, 7), (32,), 0, max(1, 64 // 4) + 1, jnp.int32)
        _lenS2 = 64 - jax.random.randint(jax.random.fold_in(_rk, 8), (32,), 0, max(1, 64 // 4) + 1, jnp.int32)
        itok_B_0_7 = jax.random.randint(jax.random.fold_in(_rk, 11), (32,), 0, 8, jnp.int32)
        fside_8xS_0 = -0.00162727 + 0.0609077 * jax.random.normal(jax.random.fold_in(_rk, 12), (8, 64), jnp.float32)
        itok_B_0_6 = jax.random.randint(jax.random.fold_in(_rk, 13), (32,), 0, 7, jnp.int32)
        return (x, itok_B_0_7, fside_8xS_0, itok_B_0_6)
    x, itok_B_0_7, fside_8xS_0, itok_B_0_6 = _rec_inputs()

    def _L0_cond_setup():
        import jax, jax.numpy as jnp
        import numpy as np
        B, C, T = (64, 64, 512)
        D, N = (64, 8)
        key = jax.random.key(seed)
        k_x, k_s, k_w, k_b = jax.random.split(key, 4)
        scale = 1.0 / np.sqrt(C)
        x = jax.random.normal(k_x, (B, C, T), dtype=jnp.float32)
        subjects = jax.random.randint(k_s, (B,), 0, N, dtype=jnp.int64)
        weights = jax.random.normal(k_w, (N, C, D), dtype=jnp.float32) * scale
        bias = jax.random.normal(k_b, (N, D), dtype=jnp.float32) * scale
        return {'x': x, 'subjects': subjects, 'weights': weights, 'bias': bias}
    _L0_cond_all = _L0_cond_setup()
    _L0_cond_in = {k: v for k, v in _L0_cond_all.items() if k in ('weights',)}
    del _L0_cond_all

    def _L0_attn_setup():
        import jax, jax.numpy as jnp
        import numpy as np
        B, L, D = (2, 512, 512)
        DIN, N, R, K = (1024, 16, 128, 4)

        def _mamba_forward(hidden_states, in_proj_w, conv1d_w, x_proj_w, dt_proj_w, dt_proj_bias, A_log, D_param, out_proj_w):
            b, l, _ = hidden_states.shape
            xz = jnp.einsum('bld,ed->ble', hidden_states, in_proj_w)
            x, z = jnp.split(xz, 2, axis=-1)
            xp = jnp.pad(x, ((0, 0), (K - 1, 0), (0, 0)))
            xc = sum((conv1d_w[:, k] * xp[:, k:k + l, :] for k in range(K)))
            xc = jax.nn.silu(xc)
            x_dbl = jnp.einsum('bld,ed->ble', xc, x_proj_w)
            dt_r = x_dbl[..., :R]
            Bc = x_dbl[..., R:R + N]
            Cc = x_dbl[..., R + N:]
            delta = jax.nn.softplus(jnp.einsum('blr,dr->bld', dt_r, dt_proj_w) + dt_proj_bias)
            A = -jnp.exp(A_log)

            def step(h, inp):
                delta_t, B_t, C_t, x_t = inp
                dA = jnp.exp(delta_t[..., None] * A)
                h = h * dA + (delta_t * x_t)[..., None] * B_t[:, None, :]
                y_t = jnp.einsum('bdn,bn->bd', h, C_t)
                return (h, y_t)
            inputs = (jnp.swapaxes(delta, 0, 1), jnp.swapaxes(Bc, 0, 1), jnp.swapaxes(Cc, 0, 1), jnp.swapaxes(xc, 0, 1))
            h0 = jnp.zeros((b, DIN, N), dtype=xc.dtype)
            _, y = jax.lax.scan(step, h0, inputs)
            y = jnp.swapaxes(y, 0, 1)
            y = y + xc * D_param
            y = y * jax.nn.silu(z)
            return jnp.einsum('bld,ed->ble', y, out_proj_w)
        key = jax.random.key(seed)
        ks = jax.random.split(key, 9)
        hidden_states = jax.random.normal(ks[0], (B, L, D), dtype=jnp.float32) * 0.02
        in_proj_w = jax.random.normal(ks[1], (2 * DIN, D), dtype=jnp.float32) * (1.0 / np.sqrt(D))
        conv1d_w = jax.random.normal(ks[2], (DIN, K), dtype=jnp.float32) * (1.0 / np.sqrt(DIN))
        x_proj_w = jax.random.normal(ks[3], (R + 2 * N, DIN), dtype=jnp.float32) * (1.0 / np.sqrt(DIN))
        dt_proj_w = jax.random.normal(ks[4], (DIN, R), dtype=jnp.float32) * (1.0 / np.sqrt(R))
        dt = jnp.exp(jax.random.uniform(ks[5], (DIN,)) * (np.log(0.1) - np.log(0.001)) + np.log(0.001))
        dt = jnp.clip(dt, 0.0001, None)
        dt_proj_bias = dt + jnp.log(-jnp.expm1(-dt))
        A_log = jnp.broadcast_to(jnp.log(jnp.arange(1, N + 1, dtype=jnp.float32)), (DIN, N))
        D_param = jnp.ones((DIN,), dtype=jnp.float32)
        out_proj_w = jax.random.normal(ks[6], (D, DIN), dtype=jnp.float32) * (1.0 / np.sqrt(DIN))
        return {'hidden_states': hidden_states, 'in_proj_w': in_proj_w, 'conv1d_w': conv1d_w, 'x_proj_w': x_proj_w, 'dt_proj_w': dt_proj_w, 'dt_proj_bias': dt_proj_bias, 'A_log': A_log, 'D_param': D_param, 'out_proj_w': out_proj_w}
    _L0_attn_all = _L0_attn_setup()
    _L0_attn_in = {k: v for k, v in _L0_attn_all.items() if k in ('in_proj_w', 'conv1d_w', 'x_proj_w', 'dt_proj_w', 'dt_proj_bias', 'A_log', 'D_param', 'out_proj_w')}
    del _L0_attn_all

    def _L0_cond2_setup():
        import jax, jax.numpy as jnp
        import numpy as np
        B, T, D_IN, D_OUT = (16, 512, 512, 512)
        N_ADAPTERS, RANK = (8, 16)
        key = jax.random.key(seed)
        k_x, k_w, k_a, k_b, k_s, k_idx = jax.random.split(key, 6)
        x = jax.random.normal(k_x, (B, T, D_IN), dtype=jnp.float32)
        W = jax.random.normal(k_w, (D_OUT, D_IN), dtype=jnp.float32) * (1.0 / np.sqrt(D_IN))
        A = jax.random.normal(k_a, (N_ADAPTERS, RANK, D_IN), dtype=jnp.float32) * 0.02
        Bm = jax.random.normal(k_b, (N_ADAPTERS, D_OUT, RANK), dtype=jnp.float32) * 0.02
        scalings = jnp.ones((N_ADAPTERS,), dtype=jnp.float32)
        adapter_idx = jax.random.randint(k_idx, (B,), 0, N_ADAPTERS, dtype=jnp.int32)
        return {'x': x, 'W': W, 'A': A, 'Bm': Bm, 'scalings': scalings, 'adapter_idx': adapter_idx}
    _L0_cond2_all = _L0_cond2_setup()
    _L0_cond2_in = {k: v for k, v in _L0_cond2_all.items() if k in ('W', 'A', 'Bm', 'scalings')}
    del _L0_cond2_all

    def _L0_ffn_setup():
        import jax, jax.numpy as jnp
        import numpy as np
        H = 512
        I = 352
        E = 16
        G = 4
        TOPK_GROUP = 2
        K = 4
        SI = 2 * I
        SCALE = 1.0
        NORM = True
        B, S = (4, 128)

        def _swiglu(h):
            g, u = jnp.split(h, 2, axis=-1)
            return jax.nn.silu(g) * u

        def _combine_weights(xt, gate_w):
            T = xt.shape[0]
            scores = jax.nn.softmax(xt @ gate_w.T, axis=-1)
            group_scores = scores.reshape(T, G, E // G).max(axis=-1)
            _, gidx = jax.lax.top_k(group_scores, TOPK_GROUP)
            gmask = jnp.zeros((T, G), bool).at[jnp.arange(T)[:, None], gidx].set(True)
            emask = jnp.repeat(gmask, E // G, axis=1)
            masked = jnp.where(emask, scores, 0.0)
            w, eidx = jax.lax.top_k(masked, K)
            if NORM:
                w = w / (w.sum(-1, keepdims=True) + 1e-20)
            w = w * SCALE
            return jnp.zeros((T, E), xt.dtype).at[jnp.arange(T)[:, None], eidx].add(w)
        key = jax.random.key(seed)
        ks = jax.random.split(key, 6)
        sc = lambda fan_in: 1.0 / np.sqrt(fan_in)
        return {'x': jax.random.normal(ks[0], (B, S, H), jnp.float32), 'gate_w': jax.random.normal(ks[1], (E, H), jnp.float32) * sc(H), 'expert_up_w': jax.random.normal(ks[2], (E, 2 * I, H), jnp.float32) * sc(H), 'expert_down_w': jax.random.normal(ks[3], (E, H, I), jnp.float32) * sc(I), 'shared_up_w': jax.random.normal(ks[4], (2 * SI, H), jnp.float32) * sc(H), 'shared_down_w': jax.random.normal(ks[5], (H, SI), jnp.float32) * sc(SI)}
    _L0_ffn_all = _L0_ffn_setup()
    _L0_ffn_in = {k: v for k, v in _L0_ffn_all.items() if k in ('gate_w', 'expert_up_w', 'expert_down_w', 'shared_up_w', 'shared_down_w')}
    del _L0_ffn_all
    return {'x': x, 'itok_B_0_7': itok_B_0_7, 'fside_8xS_0': fside_8xS_0, 'itok_B_0_6': itok_B_0_6, 'L0_cond_weights': _L0_cond_in['weights'], 'L0_attn_in_proj_w': _L0_attn_in['in_proj_w'], 'L0_attn_conv1d_w': _L0_attn_in['conv1d_w'], 'L0_attn_x_proj_w': _L0_attn_in['x_proj_w'], 'L0_attn_dt_proj_w': _L0_attn_in['dt_proj_w'], 'L0_attn_dt_proj_bias': _L0_attn_in['dt_proj_bias'], 'L0_attn_A_log': _L0_attn_in['A_log'], 'L0_attn_D_param': _L0_attn_in['D_param'], 'L0_attn_out_proj_w': _L0_attn_in['out_proj_w'], 'L0_cond2_W': _L0_cond2_in['W'], 'L0_cond2_A': _L0_cond2_in['A'], 'L0_cond2_Bm': _L0_cond2_in['Bm'], 'L0_cond2_scalings': _L0_cond2_in['scalings'], 'L0_ffn_gate_w': _L0_ffn_in['gate_w'], 'L0_ffn_expert_up_w': _L0_ffn_in['expert_up_w'], 'L0_ffn_expert_down_w': _L0_ffn_in['expert_down_w'], 'L0_ffn_shared_up_w': _L0_ffn_in['shared_up_w'], 'L0_ffn_shared_down_w': _L0_ffn_in['shared_down_w']}

def reference(x, itok_B_0_7, fside_8xS_0, itok_B_0_6, L0_cond_weights, L0_attn_in_proj_w, L0_attn_conv1d_w, L0_attn_x_proj_w, L0_attn_dt_proj_w, L0_attn_dt_proj_bias, L0_attn_A_log, L0_attn_D_param, L0_attn_out_proj_w, L0_cond2_W, L0_cond2_A, L0_cond2_Bm, L0_cond2_scalings, L0_ffn_gate_w, L0_ffn_expert_up_w, L0_ffn_expert_down_w, L0_ffn_shared_up_w, L0_ffn_shared_down_w):
    import jax
    import jax.numpy as jnp

    def _L0_cond_ref(x, subjects, weights, bias):
        import jax, jax.numpy as jnp
        import numpy as np
        B, C, T = (64, 64, 512)
        D, N = (64, 8)
        w = weights[subjects]
        b = bias[subjects]
        out = jnp.einsum('bct,bcd->bdt', x, w)
        out = out + b[:, :, None]
        return out

    def _L0_attn_ref(hidden_states, in_proj_w, conv1d_w, x_proj_w, dt_proj_w, dt_proj_bias, A_log, D_param, out_proj_w):
        import jax, jax.numpy as jnp
        import numpy as np
        B, L, D = (2, 512, 512)
        DIN, N, R, K = (1024, 16, 128, 4)

        def _mamba_forward(hidden_states, in_proj_w, conv1d_w, x_proj_w, dt_proj_w, dt_proj_bias, A_log, D_param, out_proj_w):
            b, l, _ = hidden_states.shape
            xz = jnp.einsum('bld,ed->ble', hidden_states, in_proj_w)
            x, z = jnp.split(xz, 2, axis=-1)
            xp = jnp.pad(x, ((0, 0), (K - 1, 0), (0, 0)))
            xc = sum((conv1d_w[:, k] * xp[:, k:k + l, :] for k in range(K)))
            xc = jax.nn.silu(xc)
            x_dbl = jnp.einsum('bld,ed->ble', xc, x_proj_w)
            dt_r = x_dbl[..., :R]
            Bc = x_dbl[..., R:R + N]
            Cc = x_dbl[..., R + N:]
            delta = jax.nn.softplus(jnp.einsum('blr,dr->bld', dt_r, dt_proj_w) + dt_proj_bias)
            A = -jnp.exp(A_log)

            def step(h, inp):
                delta_t, B_t, C_t, x_t = inp
                dA = jnp.exp(delta_t[..., None] * A)
                h = h * dA + (delta_t * x_t)[..., None] * B_t[:, None, :]
                y_t = jnp.einsum('bdn,bn->bd', h, C_t)
                return (h, y_t)
            inputs = (jnp.swapaxes(delta, 0, 1), jnp.swapaxes(Bc, 0, 1), jnp.swapaxes(Cc, 0, 1), jnp.swapaxes(xc, 0, 1))
            h0 = jnp.zeros((b, DIN, N), dtype=xc.dtype)
            _, y = jax.lax.scan(step, h0, inputs)
            y = jnp.swapaxes(y, 0, 1)
            y = y + xc * D_param
            y = y * jax.nn.silu(z)
            return jnp.einsum('bld,ed->ble', y, out_proj_w)
        return _mamba_forward(hidden_states, in_proj_w, conv1d_w, x_proj_w, dt_proj_w, dt_proj_bias, A_log, D_param, out_proj_w)

    def _L0_cond2_ref(x, W, A, Bm, scalings, adapter_idx):
        import jax, jax.numpy as jnp
        import numpy as np
        B, T, D_IN, D_OUT = (16, 512, 512, 512)
        N_ADAPTERS, RANK = (8, 16)
        H = jnp.einsum('btd,od->bto', x, W)
        A_b = A[adapter_idx]
        B_b = Bm[adapter_idx]
        s_b = scalings[adapter_idx]
        xa = jnp.einsum('btd,brd->btr', x, A_b)
        delta = jnp.einsum('btr,bor->bto', xa, B_b)
        delta = jax.lax.stop_gradient(delta * s_b[:, None, None])
        return H + delta

    def _L0_ffn_ref(x, gate_w, expert_up_w, expert_down_w, shared_up_w, shared_down_w):
        import jax, jax.numpy as jnp
        import numpy as np
        H = 512
        I = 352
        E = 16
        G = 4
        TOPK_GROUP = 2
        K = 4
        SI = 2 * I
        SCALE = 1.0
        NORM = True
        B, S = (4, 128)

        def _swiglu(h):
            g, u = jnp.split(h, 2, axis=-1)
            return jax.nn.silu(g) * u

        def _combine_weights(xt, gate_w):
            T = xt.shape[0]
            scores = jax.nn.softmax(xt @ gate_w.T, axis=-1)
            group_scores = scores.reshape(T, G, E // G).max(axis=-1)
            _, gidx = jax.lax.top_k(group_scores, TOPK_GROUP)
            gmask = jnp.zeros((T, G), bool).at[jnp.arange(T)[:, None], gidx].set(True)
            emask = jnp.repeat(gmask, E // G, axis=1)
            masked = jnp.where(emask, scores, 0.0)
            w, eidx = jax.lax.top_k(masked, K)
            if NORM:
                w = w / (w.sum(-1, keepdims=True) + 1e-20)
            w = w * SCALE
            return jnp.zeros((T, E), xt.dtype).at[jnp.arange(T)[:, None], eidx].add(w)
        Bq, Sq, _ = x.shape
        xt = x.reshape(-1, H)
        cw = _combine_weights(xt, gate_w)
        out = jnp.zeros_like(xt)
        for e in range(E):
            a = _swiglu(xt @ expert_up_w[e].T)
            out = out + cw[:, e:e + 1] * (a @ expert_down_w[e].T)
        out = out + _swiglu(xt @ shared_up_w.T) @ shared_down_w.T
        return out.reshape(Bq, Sq, H)
    x = x + _L0_attn_ref(_L0_cond_ref(x, itok_B_0_7, L0_cond_weights, fside_8xS_0), L0_attn_in_proj_w, L0_attn_conv1d_w, L0_attn_x_proj_w, L0_attn_dt_proj_w, L0_attn_dt_proj_bias, L0_attn_A_log, L0_attn_D_param, L0_attn_out_proj_w)
    x = x + _L0_ffn_ref(_L0_cond2_ref(x, L0_cond2_W, L0_cond2_A, L0_cond2_Bm, L0_cond2_scalings, itok_B_0_6), L0_ffn_gate_w, L0_ffn_expert_up_w, L0_ffn_expert_down_w, L0_ffn_shared_up_w, L0_ffn_shared_down_w)
    return x

_drawn_inputs = setup_inputs


def setup_inputs(seed=0):
    import zlib

    import numpy as np

    out = dict(_drawn_inputs(seed))
    spreads = {'L0_attn_D_param': (1.0, 0.6), 'L0_cond2_scalings': (1.0, 0.6)}
    factors = {'fside_8xS_0': 5.988,
     'L0_attn_x_proj_w': 8.0,
     'L0_attn_dt_proj_w': 8.0,
     'L0_attn_dt_proj_bias': 8.0,
     'L0_attn_A_log': 8.0}
    for name, (base, spread) in spreads.items():
        noise = np.random.default_rng([zlib.crc32(name.encode()), seed]).standard_normal(out[name].shape)
        drawn = base * np.exp(spread * noise) if base else spread * noise
        out[name] = jnp.asarray(drawn.astype(out[name].dtype))
    for name, factor in factors.items():
        out[name] = (out[name] * factor).astype(out[name].dtype)
    return out
```

```python
from contextlib import ExitStack

import numpy as np
import concourse.bass as bass
from concourse import mybir
from concourse.alu_op_type import AluOpType as ALU

F32, I32 = mybir.dt.float32, mybir.dt.int32
ACT = mybir.ActivationFunctionType
AX = mybir.AxisListType

P = 128
LOG_EXP = "natural_log_exp_and_others"
BATCH, SEQ, DM = 32, 64, 512
TOK = BATCH * SEQ
DIN, NST, RANK, TAPS, SUBJ = 1024, 16, 128, 4, 8
BLK = 512
NBLK = TOK // BLK
BB = BLK // SEQ
TB = BLK // P
KM = DM // P
DT = DIN // P
HALVES = 2
HT = DT // HALVES
STEPS = HALVES * NST
SCANS = STEPS * HT
SUMS = STEPS * TB
RING = 2

BESIDE = [
    [["turn1", "gate1"], ["dt4"], ["dt5"], ["dt6", "z4"],
     ["dt7", "out0"], ["out1", "z5"], ["out2"], ["out3", "z6"],
     ["z7", "out4"], ["out5", "cond0", "cond1"], ["out6", "cond2", "cond3"],
     ["out7", "cond4", "cond5"], ["cond6", "cond7", "skip0"],
     ["skip1", "x0"], ["skip2", "x1"], ["skip3", "x2"]],
    [["x3", "turn0"], ["x4"], ["x5"], ["x6"],
     ["x7"], ["silu_x", "silu_z", "gate0", "rank0"], ["rank1"], ["bt0"],
     ["bt1"], ["ct", "dt0"], ["dt1"], ["dt2"],
     ["dt3"], ["z0"], ["z1", "z2"], ["z3"]],
]
AHEAD = [f"cond{b}" for b in range(BB)] + [f"x{e}" for e in range(DT)] + [
    "silu_x", "rank0", "rank1", "bt0", "bt1", "ct", "dt0", "dt1", "dt2", "dt3", "z0", "z1", "z2", "z3"]
AFTER = ["turn1", "gate1"] + [f"out{i}" for i in range(2 * TB)]
NEXT = {f"cond{b}" for b in range(BB)} | {f"x{e}" for e in range(DT)} | {
    "silu_x", "rank0", "rank1", "bt0", "bt1", "ct", "dt0", "dt1", "dt2", "dt3", "z0", "z1", "z2", "z3"}


def name_and_number(piece):
    name = piece.rstrip("0123456789")
    return name, int(piece[len(name):] or 0)


def uses_of(pieces, names, halved):
    at, n = {}, 0
    for piece in pieces:
        name, i = name_and_number(piece)
        if name not in names:
            continue
        if name in halved and i % 2:
            at[piece] = n - 1
            continue
        at[piece] = n
        n += HT if name == "turn" else 1
    return at, n


STORE_AT = [BESIDE[0].index(step) + 1 for step in BESIDE[0] if any(p in ("out1", "out3", "out5", "out7") for p in step)]

BODY = [piece for half in BESIDE for step in half for piece in step]
PP_NAMES, PP_HALVED = {"cond", "x", "rank", "bt", "dt", "z"}, {"rank", "bt"}
Q_NAMES, Q_HALVED = {"turn", "out", "ct"}, {"out"}
PP_AHEAD, N_PP_AHEAD = uses_of(AHEAD, PP_NAMES, PP_HALVED)
PP_BODY, N_PP_BODY = uses_of(BODY, PP_NAMES, PP_HALVED)
Q_AHEAD, N_Q_AHEAD = uses_of(AHEAD, Q_NAMES, Q_HALVED)
Q_BODY, N_Q_BODY = uses_of(BODY, Q_NAMES, Q_HALVED)
Q_AFTER, _ = uses_of(AFTER, Q_NAMES, Q_HALVED)


class Place:

    def __init__(self, section, j, piece):
        ahead = section == "ahead"
        self.block = 0 if ahead else j + 1 if piece in NEXT else j
        if piece in ("turn1", "gate1") or piece.startswith("out"):
            self.block = j
        pp, q = {"ahead": (PP_AHEAD, Q_AHEAD), "body": (PP_BODY, Q_BODY), "after": ({}, Q_AFTER)}[section]
        if piece in pp:
            self.pp = pp[piece] if ahead else j * N_PP_BODY + N_PP_AHEAD + pp[piece]
        if piece in q:
            self.q = q[piece] if ahead else j * N_Q_BODY + N_Q_AHEAD + q[piece]


def mamba(nc, ctx, x_pad, itok, cond_w, in_wT, xp_wT, dt_wT, out_wT, chan, ident_d, bt_d, x1_d):
    NCH = NST + TAPS + 2
    A0, W0, DTB, DSK = 0, NST, NST + TAPS, NST + TAPS + 1

    def sb(name, shape, dt=F32):
        return ctx.enter_context(nc.sbuf_tensor(name, shape, dt))

    def ps(name, shape):
        return ctx.enter_context(nc.psum_tensor(name, shape, F32))

    def sem(name):
        return ctx.enter_context(nc.semaphore(name))

    w_in = sb("w_in", [P, KM, 2 * DIN])
    w_xp = sb("w_xp", [P, DT, RANK + 2 * NST])
    w_dt = sb("w_dt", [RANK, DIN])
    w_out = sb("w_out", [P, DT, DM])
    ch = sb("ch", [P, DT, NCH])
    a_neg = sb("a_neg", [P, DT, NST])
    ident = sb("ident", [P, P])
    itok_sb = sb("itok_sb", [1, BATCH + BB], I32)
    x_in = sb("x_in", [SEQ + 1, RING, DM])
    w_sel = sb("w_sel", [SEQ + 1, RING, SEQ])
    hid = sb("hid", [P, KM, BLK])
    xpad = sb("xpad", [P, RING, BB, SEQ + TAPS - 1])
    xc = sb("xc", [P, DT, BLK])
    skip = sb("skip", [P, DT, BLK])
    zs = sb("zs", [P, DT, BLK])
    rank = sb("rank", [RANK, BLK])
    bt = sb("bt", [NST, BLK])
    c_next = sb("c_next", [P, TB, NST])
    c_now = sb("c_now", [P, TB, NST])
    b_all = sb("b_all", [P, RING, BLK])
    sp_e = sb("sp_e", [P, BLK])
    sp_w = sb("sp_w", [P, BLK])
    sp_l = sb("sp_l", [P, BLK])
    delta = sb("delta", [P, DT, BLK])
    u = sb("u", [P, DT, BLK])
    dbx = sb("dbx", [P, RING, BLK])
    h = sb("h", [P, RING, HT, BLK])
    yacc = sb("yacc", [P, TB, HT * P])
    res = sb("res", [P, RING, DM])

    da = [ps(f"da{i}", [P, BLK]) for i in range(RING)]
    hT = [ps(f"hT{t}", [P, HT * P]) for t in range(TB)]
    pp = ps("pp", [P, BLK])
    q = ps("q", [P, BLK])

    const_in = sem("const_in")
    w_in_full = sem("w_in_full")
    w_more_full = sem("w_more_full")
    x_full = [sem(f"x_full{s}") for s in range(RING)]
    b_full = [sem(f"b_full{s}") for s in range(RING)]
    res_full = [sem(f"res_full{s}") for s in range(RING)]
    x1_stored = [sem(f"x1_stored{s}") for s in range(RING)]
    bt_stored = sem("bt_stored")
    set_up = sem("set_up")
    a_step = sem("a_step")
    pp_full = sem("pp_full")
    pp_free = sem("pp_free")
    q_full = sem("q_full")
    q_free = sem("q_free")
    conv_step = sem("conv_step")
    xc_ready = sem("xc_ready")
    zs_ready = sem("zs_ready")
    skip_ready = sem("skip_ready")
    sp_step = sem("sp_step")
    sp_ready = sem("sp_ready")
    corr_ready = sem("corr_ready")
    u_step = sem("u_step")
    da_full = sem("da_full")
    dbx_made = sem("dbx_made")
    scan_done = sem("scan_done")
    hT_full = sem("hT_full")
    sum_done = sem("sum_done")
    c_copied = sem("c_copied")
    y_ready = sem("y_ready")
    DBX0, SCAN0, SUM0 = RING * HT, RING, TB
    N_SET = 7

    x_blk = x_pad.rearrange("(k b) c f -> k b c f", b=BB)
    x_rows = x_pad.rearrange("b c f -> (b c) f").rearrange("(k t p) f -> k t p f", t=TB, p=P)
    x1_rows = x1_d.rearrange("(k t p) f -> k t p f", t=TB, p=P)

    with nc.Block() as block:
        @block.sync
        def _(sp):
            def load_x(section, j, b):
                at, s = Place(section, j, f"cond{b}"), b % RING
                if section == "ahead" and b >= RING:
                    sp.wait_ge(pp_free, b - RING + 1)
                if section == "body":
                    last = f"cond{b - RING}" if b >= RING else None
                    if last:
                        sp.wait_ge(pp_free, Place(section, j, last).pp + 1)
                    else:
                        sp.wait_ge(pp_free, j * N_PP_BODY + N_PP_AHEAD)
                sp.dma_start(x_in[0:SEQ, s, :], x_blk[bass.ds(at.block + 1, 1), b].rearrange("o c f -> (o c) f")) \
                    .then_inc(x_full[s], 16)
                which = sp.value_load(itok_sb[0:1, bass.ds(at.block * BB + b, 1)], min_val=0, max_val=SUBJ - 1)
                sp.dma_start(w_sel[:, s, :], cond_w[bass.ds(which, 1)].rearrange("o c l -> (o c) l")) \
                    .then_inc(x_full[s], 16)

            def load_b(j, m):
                if m == 0:
                    sp.wait_ge(bt_stored, 16 * (j + 1))
                sp.wait_ge(dbx_made, j * SCANS + HT * (m + 1))
                row = bt_d[bass.ds(j, 1), m % NST, :]
                sp.dma_start(b_all[:, m % RING, :], row.broadcast_to([P, BLK])).then_inc(b_full[m % RING], 16)

            def load_res(j, t):
                sp.wait_ge(x1_stored[t % RING], j * 32 + 16 * (t // RING))
                sp.dma_start(res[:, t % RING, :], x_rows[bass.ds(j, 1), t].rearrange("o p f -> (o p) f")) \
                    .then_inc(res_full[t % RING], 16)

            def store_x1(section, j, t):
                sp.wait_ge(q_free, Place(section, j, f"out{2 * t}").q + 1)
                sp.dma_start(x1_rows[bass.ds(j, 1), t].rearrange("o p f -> (o p) f"), res[:, t % RING, :]) \
                    .then_inc(x1_stored[t % RING], 16)

            sp.dma_start(itok_sb[:], itok).then_inc(const_in, 16)
            sp.dma_start(ch[:], chan).then_inc(const_in, 16)
            sp.dma_start(ident[:], ident_d).then_inc(const_in, 16)
            sp.wait_ge(const_in, 48)
            for b in range(RING):
                load_x("ahead", 0, b)
            sp.dma_start(w_in[:], in_wT).then_inc(w_in_full, 16)
            for b in range(RING, BB):
                load_x("ahead", 0, b)
            sp.dma_start(w_xp[:], xp_wT).then_inc(w_more_full, 16)
            sp.dma_start(w_dt[:], dt_wT).then_inc(w_more_full, 16)
            sp.dma_start(w_out[:], out_wT).then_inc(w_more_full, 16)
            with sp.Fori(0, NBLK) as j:
                for g in range(HALVES):
                    for n in range(NST):
                        load_b(j, g * NST + n)
                        for piece in BESIDE[g][n]:
                            name, i = name_and_number(piece)
                            if name == "cond" and i >= RING:
                                load_x("body", j, i)
                        if g == 0 and n == 3:
                            for i in range(RING):
                                load_res(j, i)
                        if g == 0 and n == 6:
                            for i in range(RING):
                                load_x("body", j, i)
                        if g == 0 and n in STORE_AT:
                            store_x1("body", j, STORE_AT.index(n))
                        if g == 0 and n - 1 in STORE_AT[:TB - RING]:
                            load_res(j, STORE_AT.index(n - 1) + RING)
            for t in range(RING):
                load_res(NBLK, t)
            for t in range(TB):
                store_x1("after", NBLK, t)
                if t + RING < TB:
                    load_res(NBLK, t + RING)
            for s in range(RING):
                sp.wait_ge(x1_stored[s], 32 * (NBLK + 1))

        @block.tensor
        def _(pe):
            def cond(at, b):
                s = b % RING
                pe.wait_ge(x_full[s], at.block * (16 * BB) + 32 * (b // RING + 1))
                pe.wait_ge(pp_free, at.pp)
                for k in range(KM):
                    mm = nc.tensor.matmul(pp[:, k * SEQ:(k + 1) * SEQ], x_in[:, s, k * P:(k + 1) * P],
                                          w_sel[:, s, :], start=True, stop=True)
                mm.then_inc(pp_full, 1)

            def in_proj(at, e):
                pe.wait_ge(pp_free, at.pp)
                for k in range(KM):
                    mm = nc.tensor.matmul(pp[:], w_in[:, k, e * P:(e + 1) * P], hid[:, k, :],
                                          start=(k == 0), stop=(k == KM - 1))
                mm.then_inc(pp_full, 1)

            def x_proj(at, lo, n, part):
                if part == 0:
                    pe.wait_ge(xc_ready, at.block + 1)
                    pe.wait_ge(pp_free, at.pp)
                for d in range(part * HT, part * HT + HT):
                    mm = nc.tensor.matmul(pp[0:n, :], w_xp[:, d, lo:lo + n], xc[:, d, :],
                                          start=(d == 0), stop=(d == DT - 1))
                if part == 1:
                    mm.then_inc(pp_full, 1)

            def c_tiles(at):
                pe.wait_ge(q_free, at.q)
                for t in range(TB):
                    for d in range(DT):
                        mm = nc.tensor.matmul(q[:, t * NST:(t + 1) * NST], xc[:, d, t * P:(t + 1) * P],
                                              w_xp[:, d, RANK + NST:RANK + 2 * NST],
                                              start=(d == 0), stop=(d == DT - 1))
                mm.then_inc(q_full, 1)

            def dt_proj(at, d):
                pe.wait_ge(pp_free, at.pp)
                nc.tensor.matmul(pp[:], w_dt[:, d * P:(d + 1) * P], rank[:], start=True, stop=True) \
                    .then_inc(pp_full, 1)

            def turn(at, half):
                pe.wait_ge(sum_done, at.block * SUMS + SUM0 + (0 if half else SUMS // HALVES))
                for d in range(HT):
                    pe.wait_ge(q_free, at.q + d)
                    for t in range(TB):
                        mm = nc.tensor.transpose(q[:, t * P:(t + 1) * P], yacc[:, t, d * P:(d + 1) * P], ident[:])
                    mm.then_inc(q_full, 1)

            def out_proj(at, i):
                t, part = divmod(i, 2)
                if part == 0:
                    pe.wait_ge(y_ready, at.block * DT + HT)
                    pe.wait_ge(q_free, at.q)
                for d in range(part * HT, part * HT + HT):
                    mm = nc.tensor.matmul(q[:], skip[:, d, t * P:(t + 1) * P], w_out[:, d, :],
                                          start=(d == 0), stop=(d == DT - 1))
                if part == 1:
                    mm.then_inc(q_full, 1)

            def piece_of(section, j, piece):
                at = Place(section, j, piece)
                name, i = name_and_number(piece)
                if name == "cond":
                    cond(at, i)
                elif name == "x":
                    in_proj(at, i)
                elif name == "z":
                    in_proj(at, DT + i)
                elif name == "rank":
                    x_proj(at, 0, RANK, i)
                elif name == "bt":
                    x_proj(at, RANK, NST, i)
                elif name == "ct":
                    c_tiles(at)
                elif name == "dt":
                    dt_proj(at, i)
                elif name == "turn":
                    turn(at, i)
                elif name == "out":
                    out_proj(at, i)

            def turn_h(j, g, n):
                m = g * NST + n
                pe.wait_ge(scan_done, j * SCANS + SCAN0 + HT * (m + 1))
                for t in range(TB):
                    pe.wait_ge(sum_done, j * SUMS + TB * m + t + 1)
                    for d in range(HT):
                        mm = nc.tensor.transpose(hT[t][:, d * P:(d + 1) * P], h[:, n % RING, d, t * P:(t + 1) * P],
                                                 ident[:])
                    mm.then_inc(hT_full, 1)

            pe.wait_ge(const_in, 48)
            pe.wait_ge(set_up, N_SET)
            for piece in AHEAD:
                if piece == "x0":
                    pe.wait_ge(w_in_full, 16)
                if piece == "rank0":
                    pe.wait_ge(w_more_full, 48)
                piece_of("ahead", 0, piece)
            with pe.Fori(0, NBLK) as j:
                for g in range(HALVES):
                    for n in range(NST):
                        for piece in BESIDE[g][n]:
                            piece_of("body", j, piece)
                        turn_h(j, g, n)
            for piece in AFTER:
                piece_of("after", NBLK, piece)

        @block.scalar
        def _(act):
            def cond(at, b):
                act.wait_ge(pp_full, at.pp + 1)
                nc.scalar.copy(hid[:, :, b * SEQ:(b + 1) * SEQ],
                               pp[:, 0:KM * SEQ].rearrange("p (k l) -> p k l", k=KM)).then_inc(pp_free, 1)

            def conv_in(section, at, e):
                act.wait_ge(pp_full, at.pp + 1)
                if section == "ahead":
                    if e >= RING:
                        act.wait_ge(conv_step, (TAPS - 1) * (e - RING + 1))
                else:
                    act.wait_ge(conv_step, at.block * ((TAPS - 1) * DT) + (TAPS - 1) * (e - RING + 1))
                    act.wait_ge(u_step, at.block * (3 * DT))
                    act.wait_ge(skip_ready, (at.block - 1) * DT + e + 1)
                rows = pp[:].rearrange("p (b l) -> p b l", b=BB)
                nc.scalar.copy(xpad[:, e % RING, :, TAPS - 1:], rows)
                nc.scalar.mul(xc[:, e, :], pp[:], ch[:, e, W0 + TAPS - 1:W0 + TAPS]).then_inc(pp_free, 1)

            def silu_x(section, at):
                act.wait_ge(conv_step, (at.block + 1) * ((TAPS - 1) * DT))
                nc.scalar.activation(xc[:], xc[:], ACT.Silu).then_inc(xc_ready, 1)
                if section == "ahead":
                    nc.scalar.preload_act_table_set(LOG_EXP)

            def silu_z(at):
                act.wait_ge(pp_free, at.block * N_PP_BODY + N_PP_AHEAD + PP_BODY["z7"] + 1)
                nc.scalar.activation(zs[:], zs[:], ACT.Silu).then_inc(zs_ready, 1)
                nc.scalar.preload_act_table_set(LOG_EXP)

            def skips(at, i):
                for e in (2 * i, 2 * i + 1):
                    if i == 0:
                        act.wait_ge(q_full, at.block * N_Q_BODY + N_Q_AHEAD + Q_BODY["out7"] + 1)
                        act.wait_ge(xc_ready, at.block + 1)
                    nc.scalar.mul(skip[:, e, :], xc[:, e, :], ch[:, e, DSK:DSK + 1]).then_inc(skip_ready, 1)

            def rank_out(at):
                act.wait_ge(pp_full, at.pp + 1)
                nc.scalar.copy(rank[:], pp[:]).then_inc(pp_free, 1)

            def b_out(at, section):
                act.wait_ge(pp_full, at.pp + 1)
                if section == "body":
                    act.wait_ge(bt_stored, 16 * at.block)
                nc.scalar.copy(bt[:], pp[0:NST, :]).then_inc(pp_free, 1)
                act.wait_ge(pp_free, at.pp + 1)
                act.dma_start(bt_d[bass.ds(at.block, 1)].rearrange("o n t -> (o n) t"), bt[:]).then_inc(bt_stored, 16)

            def softplus(section, at, d):
                bias = ch[:, d, DTB:DTB + 1]
                act.wait_ge(pp_full, at.pp + 1)
                if section == "body" or d >= 1:
                    act.wait_ge(u_step, at.block * (3 * DT) + 3 * (d - 1) + 2)
                if section == "body":
                    act.wait_ge(da_full, at.block * SCANS - (SCANS // HALVES if d < HT else 0))
                nc.scalar.activation(sp_e[:], pp[:], ACT.Abs, bias=bias).then_inc(sp_step, 1)
                nc.scalar.activation(delta[:, d, :], pp[:], ACT.Relu, bias=bias).then_inc(pp_free, 1)
                act.wait_ge(sp_step, at.block * (2 * DT) + 2 * d + 1)
                nc.scalar.activation(sp_e[:], sp_e[:], ACT.Exp, scale=-1.0).then_inc(sp_step, 1)
                act.wait_ge(sp_step, at.block * (2 * DT) + 2 * d + 2)
                nc.scalar.activation(sp_w[:], sp_e[:], ACT.Identity, bias=1.0)
                nc.scalar.activation(sp_l[:], sp_e[:], ACT.Ln, bias=1.0).then_inc(sp_ready, 1)

            def z_out(section, at, e):
                act.wait_ge(pp_full, at.pp + 1)
                if section == "body":
                    act.wait_ge(y_ready, at.block * DT + (HT if e >= HT else 0))
                nc.scalar.copy(zs[:, e, :], pp[:]).then_inc(pp_free, 1)

            def piece_of(section, j, piece):
                at = Place(section, j, piece)
                name, i = name_and_number(piece)
                if name == "cond":
                    cond(at, i)
                elif name == "x":
                    conv_in(section, at, i)
                elif name == "silu_x":
                    silu_x(section, at)
                elif name == "silu_z":
                    silu_z(at)
                elif name == "skip":
                    skips(at, i)
                elif name == "rank" and i == 1:
                    rank_out(at)
                elif name == "bt" and i == 1:
                    b_out(at, section)
                elif name == "dt":
                    softplus(section, at, i)
                elif name == "z":
                    z_out(section, at, i)

            def decay(j, g, n, i):
                m = g * NST + n
                d = g * HT + i
                if n == 0:
                    act.wait_ge(u_step, j * (3 * DT) + 3 * d + 2)
                act.wait_ge(scan_done, j * SCANS + HT * m + i + 1)
                rows = delta[:, d, :].rearrange("p (b l) -> p b l", b=BB)
                out = da[i % RING][:].rearrange("p (b l) -> p b l", b=BB)
                nc.scalar.activation(out[:, :, 1:], rows[:, :, 1:], ACT.Exp, scale=a_neg[:, d, n:n + 1]) \
                    .then_inc(da_full, 1)

            nc.scalar.preload_act_table_set(LOG_EXP)
            act.wait_ge(const_in, 48)
            nc.scalar.activation(a_neg[:], ch[:, :, A0:A0 + NST], ACT.Exp).then_inc(a_step, 1)
            act.wait_ge(a_step, 1)
            nc.scalar.mul(a_neg[:], a_neg[:], -1.0).then_inc(a_step, 1)
            act.wait_ge(set_up, N_SET)
            act.wait_ge(a_step, 2)
            for piece in AHEAD:
                piece_of("ahead", 0, piece)
            with act.Fori(0, NBLK) as j:
                nc.scalar.preload_act_table_set(LOG_EXP)
                for g in range(HALVES):
                    for n in range(NST):
                        for i in range(HT):
                            decay(j, g, n, i)
                            if i == HT - 1:
                                for piece in BESIDE[g][n]:
                                    piece_of("body", j, piece)
            act.wait_ge(bt_stored, 16 * (NBLK + 1))

        @block.vector
        def _(dve):
            def conv(at, e):
                dve.wait_ge(pp_free, at.pp + 1)
                out = xc[:, e, :].rearrange("p (b l) -> p b l", b=BB)
                for k in range(TAPS - 1):
                    if k:
                        dve.wait_ge(conv_step, at.block * ((TAPS - 1) * DT) + (TAPS - 1) * e + k)
                    nc.vector.scalar_tensor_tensor(out=out, in0=xpad[:, e % RING, :, k:k + SEQ],
                                                   scalar=ch[:, e, W0 + k:W0 + k + 1], in1=out,
                                                   op0=ALU.mult, op1=ALU.add).then_inc(conv_step, 1)

            def correct(at, d):
                dve.wait_ge(sp_ready, at.block * DT + d + 1)
                nc.vector.scalar_tensor_tensor(out=sp_w[:], in0=sp_w[:], scalar=-1.0, in1=sp_e[:],
                                               op0=ALU.add, op1=ALU.subtract, reverse1=True).then_inc(corr_ready, 1)

            def c_in(section, at):
                dve.wait_ge(q_full, at.q + 1)
                if section == "body":
                    dve.wait_ge(c_copied, at.block)
                nc.vector.tensor_copy(c_next[:], q[:, 0:TB * NST].rearrange("p (t n) -> p t n", t=TB)) \
                    .then_inc(q_free, 1)

            def add_skip(at, half):
                for i in range(HT):
                    d = half * HT + i
                    dve.wait_ge(skip_ready, at.block * DT + (0 if half else d + 1))
                    dve.wait_ge(q_full, at.q + i + 1)
                    nc.vector.tensor_tensor(skip[:, d, :], q[:], skip[:, d, :], ALU.add).then_inc(q_free, 1)

            def residual(at, j, t):
                s = t % RING
                dve.wait_ge(res_full[s], j * 32 + 16 * (t // RING + 1))
                dve.wait_ge(q_full, at.q + 1)
                nc.vector.tensor_tensor(res[:, s, :], q[:], res[:, s, :], ALU.add).then_inc(q_free, 1)

            def piece_of(section, j, piece):
                at = Place(section, j, piece)
                name, i = name_and_number(piece)
                if name == "x":
                    conv(at, i)
                elif name == "dt":
                    correct(at, i)
                elif name == "ct":
                    c_in(section, at)
                elif name == "turn":
                    add_skip(at, i)
                elif name == "out" and i % 2:
                    residual(at, j, i // 2)

            def scan(j, g, n, i):
                m = g * NST + n
                at = j * SCANS + HT * m + i
                dve.wait_ge(da_full, at + 1)
                dve.wait_ge(dbx_made, at + DBX0 + 1)
                nc.vector.tensor_tensor_scan(h[:, n % RING, i, :], da[i % RING][:], dbx[:, i % RING, :], 0.0,
                                             ALU.mult, ALU.add).then_inc(scan_done, 1)

            def add_state(j, g, n, t):
                at = j * SUMS + TB * (g * NST + n) + t
                scalar = c_now[:, t, n:n + 1]
                dve.wait_ge(hT_full, at + 1)
                if n == 0:
                    dve.wait_ge(c_copied, j + 1)
                    nc.vector.tensor_scalar(yacc[:, t, :], hT[t][:], scalar, None, ALU.mult).then_inc(sum_done, 1)
                else:
                    dve.wait_ge(sum_done, at + SUM0 - TB + 1)
                    nc.vector.scalar_tensor_tensor(out=yacc[:, t, :], in0=hT[t][:], scalar=scalar, in1=yacc[:, t, :],
                                                   op0=ALU.mult, op1=ALU.add).then_inc(sum_done, 1)

            dve.sem_inc(scan_done, SCAN0)
            dve.sem_inc(sum_done, SUM0)
            for s in range(RING):
                nc.vector.memset(da[s][:].rearrange("p (b l) -> p b l", b=BB)[:, :, 0:1], 0.0).then_inc(set_up, 1)
            nc.vector.memset(xpad[:, :, :, 0:TAPS - 1], 0.0).then_inc(set_up, 1)
            nc.vector.memset(x_in[SEQ:SEQ + 1, :, :], 1.0).then_inc(set_up, 1)
            nc.vector.memset(yacc[:], 0.0).then_inc(set_up, 1)
            dve.wait_ge(set_up, N_SET)
            for piece in AHEAD:
                piece_of("ahead", 0, piece)
            with dve.Fori(0, NBLK) as j:
                dve.wait_ge(q_free, j * N_Q_BODY + N_Q_AHEAD)
                dve.wait_ge(sum_done, j * SUMS + SUM0)
                nc.vector.tensor_copy(c_now[:], c_next[:]).then_inc(c_copied, 1)
                for g in range(HALVES):
                    for n in range(NST):
                        for i in range(HT):
                            scan(j, g, n, i)
                            if n:
                                add_state(j, g, n - 1, i)
                        for piece in BESIDE[g][n]:
                            piece_of("body", j, piece)
                    for t in range(TB):
                        add_state(j, g, NST - 1, t)
            for piece in AFTER:
                piece_of("after", NBLK, piece)

        @block.gpsimd
        def _(pool):
            def finish_delta(section, at, d):
                step = at.block * (3 * DT) + 3 * d
                pool.wait_ge(corr_ready, at.block * DT + d + 1)
                nc.gpsimd.tensor_tensor(sp_l[:], sp_l[:], sp_w[:], ALU.add).then_inc(u_step, 1)
                pool.wait_ge(u_step, step + 1)
                nc.gpsimd.tensor_tensor(delta[:, d, :], delta[:, d, :], sp_l[:], ALU.add).then_inc(u_step, 1)
                pool.wait_ge(u_step, step + 2)
                pool.wait_ge(xc_ready, at.block + 1)
                if section == "body":
                    pool.wait_ge(dbx_made, at.block * SCANS + DBX0 - (SCANS // HALVES if d < HT else 0))
                nc.gpsimd.tensor_tensor(u[:, d, :], delta[:, d, :], xc[:, d, :], ALU.mult).then_inc(u_step, 1)

            def gate(section, j, half):
                at = Place(section, j, f"turn{half}")
                pool.wait_ge(zs_ready, at.block + (0 if half else 1))
                for i in range(HT):
                    d = half * HT + i
                    pool.wait_ge(q_free, at.q + i + 1)
                    nc.gpsimd.tensor_tensor(skip[:, d, :], skip[:, d, :], zs[:, d, :], ALU.mult).then_inc(y_ready, 1)

            def piece_of(section, j, piece):
                name, i = name_and_number(piece)
                if name == "dt":
                    finish_delta(section, Place(section, j, piece), i)
                elif name == "gate":
                    gate(section, j, i)

            def inflow(j, g, n, i):
                m = g * NST + n
                d = g * HT + i
                if n == 0:
                    pool.wait_ge(u_step, j * (3 * DT) + 3 * (d + 1))
                if i == 0:
                    pool.wait_ge(b_full[m % RING], j * (16 * STEPS // RING) + 16 * (m // RING + 1))
                pool.wait_ge(scan_done, j * SCANS + HT * m + i + 1)
                nc.gpsimd.tensor_tensor(dbx[:, i % RING, :], u[:, d, :], b_all[:, m % RING, :], ALU.mult) \
                    .then_inc(dbx_made, 1)

            pool.sem_inc(dbx_made, DBX0)
            nc.gpsimd.memset(skip[:], 0.0).then_inc(set_up, 1)
            nc.gpsimd.memset(zs[:], 0.0).then_inc(set_up, 1)
            pool.wait_ge(set_up, N_SET)
            for piece in AHEAD:
                piece_of("ahead", 0, piece)
            with pool.Fori(0, NBLK) as j:
                for g in range(HALVES):
                    for n in range(NST):
                        for i in range(HT):
                            inflow(j, g, n, i)
                        for piece in BESIDE[g][n]:
                            piece_of("body", j, piece)
            for piece in AFTER:
                piece_of("after", NBLK, piece)


NADAPT, LRANK = 8, 16
EXP, GROUPS, TOP_GROUPS, TOP = 16, 4, 2, 4
PER_GROUP = EXP // GROUPS
INNER = 352
SINNER = 2 * INNER
KI = -(-INNER // P)
KS = -(-SINNER // P)
SPAD = KS * P
TILES = TOK // P
SLOT_TILES = (TOK * TOP - EXP) // P + EXP
TURN = 8
TURNS = -(-SLOT_TILES // TURN)
RUN_TILES = TURNS * TURN
LISTS, YS, WSEMS = TURN, 4, 4
LAG = 3
LIST_TILES = RUN_TILES + LISTS - LAG


def width(chunk, total):
    return min(P, total - chunk * P)


def mix(nc, keep, x1_d, adapter_ids, d, x2_d):
    ctx = ExitStack()

    def sb(name, shape, dt=F32):
        return ctx.enter_context(nc.sbuf_tensor(name, shape, dt))

    def ps(name, shape):
        return ctx.enter_context(nc.psum_tensor(name, shape, F32))

    def sem(name):
        return ctx.enter_context(nc.semaphore(name))

    RANKS = 24
    ident, x2T, sel, cw = keep["ident"], keep["x2T"], keep["sel"], keep["cw"]
    w_T = sb("w_T", [P, KM, DM])
    a_T = sb("a_T", [P, KM, NADAPT * LRANK])
    b_T = sb("b_T", [NADAPT * LRANK, DM])
    gate_T = sb("gate_T", [P, KM, EXP])
    ids_i = sb("ids_i", [P, BATCH], I32)
    ids_f = sb("ids_f", [P, BATCH])
    row_scale = sb("row_scale", [P, 2])
    mask = sb("mask", [P, BATCH])
    tri_g = sb("tri_g", [P, GROUPS, GROUPS])
    tri_e = sb("tri_e", [P, EXP, EXP])
    x1_in = sb("x1_in", [P, TB, DM])
    x1T = sb("x1T", [P, KM, BLK])
    xam = sb("xam", [P, BLK])
    x2_sb = sb("x2_sb", [P, TB, DM])
    lgT = sb("lgT", [EXP, BLK])
    zero_rows = sb("zero_rows", [P, DM])
    top = sb("top", [P, TB])
    sc = sb("sc", [P, TB, EXP])
    total = sb("total", [P, TB])
    rc = sb("rc", [P, TB])
    g_top = sb("g_top", [P, TB, GROUPS])
    g_more = sb("g_more", [P, TB, GROUPS, GROUPS])
    g_tie = sb("g_tie", [P, TB, GROUPS, GROUPS])
    g_rank = sb("g_rank", [P, TB, GROUPS])
    e_more = sb("e_more", [P, TB, EXP, EXP])
    e_tie = sb("e_tie", [P, TB, EXP, EXP])
    e_rank = sb("e_rank", [P, TB, EXP])
    w_top = sb("w_top", [P, TB, EXP])

    tr = [ps(f"tr{i}", [P, BLK]) for i in range(RING)]
    xa = ps("xa", [P, BLK])
    x2p = [ps(f"x2p{i}", [P, DM]) for i in range(RING)]
    lg = ps("lg", [EXP, BLK])
    lgt = ps("lgt", [P, TB, EXP])

    consts_in = sem("consts_in")
    w_in = sem("w_in")
    x1_full = sem("x1_full")
    zero_set = sem("zero_set")
    zero_stored = sem("zero_stored")
    mask_step = sem("mask_step")
    x1T_full = sem("x1T_full")
    x1T_out = sem("x1T_out")
    xa_full = sem("xa_full")
    xa_out = sem("xa_out")
    x2_full = sem("x2_full")
    x2_out = sem("x2_out")
    x2_stored = sem("x2_stored")
    x2T_full = sem("x2T_full")
    x2T_out = sem("x2T_out")
    lg_full = sem("lg_full")
    lg_out = sem("lg_out")
    lgt_full = sem("lgt_full")
    rank_step = sem("rank_step")
    exp_done = sem("exp_done")

    x1_blk = x1_d.rearrange("(k t p) f -> k p t f", t=TB, p=P)
    x2_blk = x2_d[0:TOK].rearrange("(k t p) f -> k p t f", t=TB, p=P)

    with ctx, nc.Block() as block:
        @block.sync
        def _(sp):
            def load_x1(j):
                sp.dma_start(x1_in[:], x1_blk[bass.ds(j + 1, 1)].rearrange("o p t f -> (o p) t f")).then_inc(x1_full, 16)

            load_x1(0)
            sp.dma_start(ident[:], d["ident"]).then_inc(consts_in, 16)
            sp.dma_start(ids_i[:], adapter_ids.broadcast_to([P, BATCH])).then_inc(consts_in, 16)
            sp.dma_start(row_scale[:], d["row_scale"]).then_inc(consts_in, 16)
            sp.dma_start(tri_g[:], d["tri_g"]).then_inc(consts_in, 16)
            sp.dma_start(tri_e[:], d["tri_e"]).then_inc(consts_in, 16)
            sp.dma_start(a_T[:], d["a_T"]).then_inc(w_in, 16)
            sp.dma_start(w_T[:], d["w_T"]).then_inc(w_in, 16)
            sp.dma_start(b_T[:], d["b_T"]).then_inc(w_in, 16)
            sp.dma_start(gate_T[:], d["gate_T"]).then_inc(w_in, 16)
            sp.wait_ge(zero_set, 1)
            sp.dma_start(x2_d[TOK:TOK + P], zero_rows[:]).then_inc(zero_stored, 16)
            with sp.Fori(0, NBLK - 1) as j:
                sp.wait_ge(x1T_full, KM * (j + 1))
                load_x1(j + 1)
                sp.wait_ge(x2_out, TB * (j + 1))
                sp.dma_start(x2_blk[bass.ds(j, 1)].rearrange("o p t f -> (o p) t f"), x2_sb[:]).then_inc(x2_stored, 16)
            sp.wait_ge(x2_out, TB * NBLK)
            sp.dma_start(x2_blk[NBLK - 1], x2_sb[:]).then_inc(x2_stored, 16)
            sp.wait_ge(x2_stored, 16 * NBLK)
            sp.wait_ge(zero_stored, 16)

        @block.tensor
        def _(pe):
            pe.wait_ge(consts_in, 16 * 5)
            with pe.Fori(0, NBLK) as j:
                pe.wait_ge(x1_full, 16 * (j + 1))
                for k in range(KM):
                    if k < RING:
                        pe.wait_ge(x2T_out, KM * j)
                    else:
                        pe.wait_ge(x1T_out, KM * j + k - RING + 1)
                    for t in range(TB):
                        mm = nc.tensor.transpose(tr[k % RING][:, t * P:(t + 1) * P], x1_in[:, t, k * P:(k + 1) * P], ident[:])
                    mm.then_inc(x1T_full, 1)
                pe.wait_ge(w_in, 64)
                for k in range(KM):
                    pe.wait_ge(x1T_out, KM * j + k + 1)
                    mm = nc.tensor.matmul(xa[:], a_T[:, k, :], x1T[:, k, :], start=(k == 0), stop=(k == KM - 1))
                mm.then_inc(xa_full, 1)
                for t in range(TB):
                    pe.wait_ge(x2_out, TB * j + (t - RING + 1 if t >= RING else 0))
                    for k in range(KM):
                        nc.tensor.matmul(x2p[t % RING][:], x1T[:, k, t * P:(t + 1) * P], w_T[:, k, :], start=(k == 0), stop=False)
                    pe.wait_ge(xa_out, j + 1)
                    nc.tensor.matmul(x2p[t % RING][:], xam[:, t * P:(t + 1) * P], b_T[:], start=False, stop=True) \
                        .then_inc(x2_full, 1)
                pe.wait_ge(x2_out, TB * (j + 1))
                for k in range(KM):
                    if k < RING:
                        pe.wait_ge(x1T_out, KM * (j + 1))
                    else:
                        pe.wait_ge(x2T_out, KM * j + k - RING + 1)
                    for t in range(TB):
                        mm = nc.tensor.transpose(tr[k % RING][:, t * P:(t + 1) * P], x2_sb[:, t, k * P:(k + 1) * P], ident[:])
                    mm.then_inc(x2T_full, 1)
                for k in range(KM):
                    pe.wait_ge(x2T_out, KM * j + k + 1)
                    mm = nc.tensor.matmul(lg[:], gate_T[:, k, :], x2T[:, k, bass.ds(j * BLK, BLK)],
                                          start=(k == 0), stop=(k == KM - 1))
                mm.then_inc(lg_full, 1)
                pe.wait_ge(rank_step, j * RANKS + 2)
                pe.wait_ge(lg_out, j + 1)
                for t in range(TB):
                    mm = nc.tensor.matmul(lgt[:, t, :], lgT[:, t * P:(t + 1) * P], ident[0:EXP, 0:EXP], start=True, stop=True)
                mm.then_inc(lgt_full, 1)

        @block.scalar
        def _(act):
            def exps(j):
                act.wait_ge(rank_step, (j + 1) * RANKS + 2)
                nc.scalar.activation(sc[:], sc[:], ACT.Exp).then_inc(exp_done, 1)

            def block_out(j, ranked):
                for k in range(KM):
                    act.wait_ge(x1T_full, KM * j + k + 1)
                    nc.scalar.copy(x1T[:, k, :], tr[k % RING][:]).then_inc(x1T_out, 1)
                for t in range(TB):
                    act.wait_ge(x2_full, TB * j + t + 1)
                    if t == 0:
                        act.wait_ge(x2_stored, 16 * j)
                    nc.scalar.copy(x2_sb[:, t, :], x2p[t % RING][:]).then_inc(x2_out, 1)
                    if t == 0 and ranked is not None:
                        exps(ranked)
                for k in range(KM):
                    act.wait_ge(x2T_full, KM * j + k + 1)
                    nc.scalar.copy(x2T[:, k, bass.ds(j * BLK, BLK)], tr[k % RING][:]).then_inc(x2T_out, 1)

            def logits_out(j):
                act.wait_ge(lg_full, j + 1)
                nc.scalar.copy(lgT[:], lg[:]).then_inc(lg_out, 1)

            block_out(0, None)
            logits_out(0)
            with act.Fori(1, NBLK) as j:
                block_out(j, j - 1)
                logits_out(j)
            exps(NBLK - 1)

        @block.vector
        def _(dve):
            def adapt(j):
                dve.wait_ge(xa_full, j + 1)
                nc.vector.tensor_tensor(xam[:].rearrange("p (b l) -> p b l", b=BB), xa[:].rearrange("p (b l) -> p b l", b=BB),
                                        mask[:, bass.ds(j * BB, BB)].unsqueeze(2).broadcast_to([P, BB, SEQ]),
                                        ALU.mult).then_inc(xa_out, 1)

            def rank(j):
                base = (j + 1) * RANKS
                done = 0

                def step(op):
                    nonlocal done
                    op.then_inc(rank_step, 1)
                    done += 1
                    dve.wait_ge(rank_step, base + done)

                def spread(x, n):
                    return x.unsqueeze(2).broadcast_to([P, TB, n])

                dve.wait_ge(lgt_full, j + 1)
                step(nc.vector.tensor_reduce(top[:], lgt[:], AX.X, ALU.max))
                step(nc.vector.tensor_tensor(sc[:], lgt[:], spread(top[:], EXP), ALU.subtract))
                dve.wait_ge(exp_done, j + 1)
                step(nc.vector.tensor_reduce(total[:], sc[:], AX.X, ALU.add))
                step(nc.vector.reciprocal(rc[:], total[:]))
                step(nc.vector.tensor_tensor(sc[:], sc[:], spread(rc[:], EXP), ALU.mult))
                step(nc.vector.tensor_reduce(g_top[:], sc[:].rearrange("p t (g i) -> p t g i", g=GROUPS), AX.X, ALU.max))
                other = g_top[:].unsqueeze(2).broadcast_to([P, TB, GROUPS, GROUPS])
                own = g_top[:].unsqueeze(3).broadcast_to([P, TB, GROUPS, GROUPS])
                step(nc.vector.tensor_tensor(g_more[:], other, own, ALU.is_gt))
                step(nc.vector.tensor_tensor(g_tie[:], other, own, ALU.is_equal))
                step(nc.vector.tensor_tensor(g_tie[:], g_tie[:], tri_g[:].unsqueeze(1).broadcast_to([P, TB, GROUPS, GROUPS]), ALU.mult))
                step(nc.vector.tensor_tensor(g_more[:], g_more[:], g_tie[:], ALU.add))
                step(nc.vector.tensor_reduce(g_rank[:], g_more[:], AX.X, ALU.add))
                step(nc.vector.tensor_scalar(g_rank[:], g_rank[:], float(TOP_GROUPS), None, ALU.is_lt))
                step(nc.vector.tensor_tensor(sc[:].rearrange("p t (g i) -> p t g i", g=GROUPS),
                                             sc[:].rearrange("p t (g i) -> p t g i", g=GROUPS),
                                             g_rank[:].unsqueeze(3).broadcast_to([P, TB, GROUPS, PER_GROUP]), ALU.mult))
                other = sc[:].unsqueeze(2).broadcast_to([P, TB, EXP, EXP])
                own = sc[:].unsqueeze(3).broadcast_to([P, TB, EXP, EXP])
                step(nc.vector.tensor_tensor(e_more[:], other, own, ALU.is_gt))
                step(nc.vector.tensor_tensor(e_tie[:], other, own, ALU.is_equal))
                step(nc.vector.tensor_tensor(e_tie[:], e_tie[:], tri_e[:].unsqueeze(1).broadcast_to([P, TB, EXP, EXP]), ALU.mult))
                step(nc.vector.tensor_tensor(e_more[:], e_more[:], e_tie[:], ALU.add))
                step(nc.vector.tensor_reduce(e_rank[:], e_more[:], AX.X, ALU.add))
                chosen = sel[:, bass.ds(j * TB, TB), :]
                step(nc.vector.tensor_scalar(chosen, e_rank[:], float(TOP), None, ALU.is_lt))
                step(nc.vector.tensor_tensor(w_top[:], sc[:], chosen, ALU.mult))
                step(nc.vector.tensor_reduce(total[:], w_top[:], AX.X, ALU.add))
                step(nc.vector.tensor_scalar(total[:], total[:], 1e-20, None, ALU.add))
                step(nc.vector.reciprocal(rc[:], total[:]))
                step(nc.vector.tensor_tensor(cw[:, bass.ds(j * TB, TB), :], w_top[:], spread(rc[:], EXP), ALU.mult))
                assert done == RANKS

            dve.sem_inc(rank_step, RANKS)
            nc.vector.memset(zero_rows[:], 0.0).then_inc(zero_set, 1)
            dve.wait_ge(consts_in, 16 * 5)
            nc.vector.tensor_copy(ids_f[:], ids_i[:]).then_inc(mask_step, 1)
            dve.wait_ge(mask_step, 1)
            nc.vector.tensor_scalar(mask[:], ids_f[:], row_scale[:, 0:1], row_scale[:, 1:2], ALU.is_equal, ALU.mult) \
                .then_inc(mask_step, 1)
            dve.wait_ge(mask_step, 2)
            adapt(0)
            with dve.Fori(1, NBLK) as j:
                adapt(j)
                rank(j - 1)
            rank(NBLK - 1)


def shared(nc, keep, x1_d, d, list_d, out_d):
    ctx = ExitStack()

    def sb(name, shape, dt=F32):
        return ctx.enter_context(nc.sbuf_tensor(name, shape, dt))

    def ps(name, shape):
        return ctx.enter_context(nc.psum_tensor(name, shape, F32))

    def sem(name):
        return ctx.enter_context(nc.semaphore(name))

    x2T, sel, cw, table = keep["x2T"], keep["sel"], keep["cw"], keep["table"]
    sup_T = sb("sup_T", [P, KM, 2 * SPAD])
    sdn_T = sb("sdn_T", [P, KS, DM])
    res = sb("res2", [P, TB, DM])
    gs = sb("sgs", [P, RING, BLK])
    a = sb("sa", [P, KS, BLK])
    pad_list = sb("pad_list", [P, LIST_TILES, 2], I32)
    pad_rows = sb("pad_rows", [P, DM])
    tokens = sb("tokens", [P, TILES], I32)
    strict = sb("strict", [P, P])
    ones = sb("ones", [P, P])
    restart = sb("restart", [P, EXP, TILES])
    steps = sb("steps", [P, TILES])
    numbers = sb("numbers", [1, LIST_TILES])
    before = sb("before", [P, EXP, TILES])
    upto = sb("upto", [P, EXP, TILES])
    more = sb("more", [P, EXP, TILES])
    tiles = sb("tiles", [P, EXP])
    ends = sb("ends", [P, EXP])
    starts = sb("starts", [P, EXP])
    place = sb("place", [P, TILES, EXP])
    best = sb("best", [P, TILES, 8])
    match = sb("match", [P, TILES, TOP, EXP])
    pairs = sb("pairs", [P, TILES, TOP, 2], I32)
    slot_i = sb("slot_i", [P, TILES, TOP], I32)
    t_cmp = sb("t_cmp", [1, LIST_TILES, EXP])
    t_exp = sb("t_exp", [1, 1 + LIST_TILES])
    t_new = sb("t_new", [1, LIST_TILES])
    t_flip = sb("t_flip", [1, LIST_TILES])
    t_slot = sb("t_slot", [1, LIST_TILES])
    t_first = sb("t_first", [1, 1 + LIST_TILES])
    t_tmp = sb("t_tmp", [1, LIST_TILES])

    gp = [ps(f"gp{i}", [P, BLK]) for i in range(RING)]
    up = [ps(f"up{i}", [P, BLK]) for i in range(RING)]
    yp = [ps(f"yp{i}", [P, DM]) for i in range(RING)]
    within = ps("within", [P, TILES, EXP])
    totals = ps("totals", [P, TILES, EXP])

    w_up_in = sem("w_up_in")
    w_dn_in = sem("w_dn_in")
    consts2 = sem("consts2")
    res_full = sem("res2_full")
    out_stored = sem("out_stored")
    pads_stored = sem("pads_stored")
    pads_set = sem("pads_set")
    g_full = sem("g_full")
    u_full = sem("u_full")
    silu_done = sem("silu_done")
    a_done = sem("a_done")
    y_full = sem("y_full")
    y_out = sem("y_out")
    counts_full = sem("counts_full")
    slot_step = sem("slot_step")
    slots_ready = sem("slots_ready")
    listed = sem("listed")

    x1_blk = x1_d.rearrange("(k t p) f -> k p t f", t=TB, p=P)
    out_blk = out_d[0:TOK].rearrange("(k t p) f -> k p t f", t=TB, p=P)
    list_rows = list_d.rearrange("(i p) c -> p i c", p=P)
    N_CONST = 7

    with ctx, nc.Block() as block:
        @block.sync
        def _(sp):
            sp.dma_start(sup_T[:], d["sup_T"]).then_inc(w_up_in, 16)
            sp.dma_start(sdn_T[:], d["sdn_T"]).then_inc(w_dn_in, 16)
            sp.dma_start(pad_list[:], d["pad_list"]).then_inc(consts2, 16)
            sp.dma_start(tokens[:], d["tokens"]).then_inc(consts2, 16)
            sp.dma_start(strict[:], d["strict"]).then_inc(consts2, 16)
            sp.dma_start(ones[:], d["ones"]).then_inc(consts2, 16)
            sp.dma_start(restart[:], d["restart"]).then_inc(consts2, 16)
            sp.dma_start(steps[:], d["steps"]).then_inc(consts2, 16)
            sp.dma_start(numbers[:], d["numbers"]).then_inc(consts2, 16)
            sp.wait_ge(consts2, 16 * N_CONST)
            sp.dma_start(list_rows, pad_list[:]).then_inc(pads_stored, 16)
            sp.wait_ge(pads_set, 1)
            sp.dma_start(out_d[TOK:TOK + P], pad_rows[:]).then_inc(pads_stored, 16)
            with sp.Fori(0, NBLK) as j:
                sp.wait_ge(out_stored, 16 * j)
                sp.dma_start(res[:], x1_blk[bass.ds(j + 1, 1)].rearrange("o p t f -> (o p) t f")).then_inc(res_full, 16)
                sp.wait_ge(y_out, TB * (j + 1))
                sp.dma_start(out_blk[bass.ds(j, 1)].rearrange("o p t f -> (o p) t f"), res[:]).then_inc(out_stored, 16)
            sp.wait_ge(out_stored, 16 * NBLK)
            sp.wait_ge(pads_stored, 32)

        @block.tensor
        def _(pe):
            def expert(j):
                for f in range(KS):
                    at = j * KS + f
                    tokens_j = bass.ds(j * BLK, BLK)
                    if f >= RING:
                        pe.wait_ge(a_done, at - RING + 1)
                    else:
                        pe.wait_ge(a_done, j * KS)
                    for k in range(KM):
                        mm = nc.tensor.matmul(gp[f % RING][:], sup_T[:, k, f * P:(f + 1) * P], x2T[:, k, tokens_j],
                                              start=(k == 0), stop=(k == KM - 1))
                    mm.then_inc(g_full, 1)
                    for k in range(KM):
                        mm = nc.tensor.matmul(up[f % RING][:], sup_T[:, k, SPAD + f * P:SPAD + (f + 1) * P],
                                              x2T[:, k, tokens_j], start=(k == 0), stop=(k == KM - 1))
                    mm.then_inc(u_full, 1)
                pe.wait_ge(w_dn_in, 16)
                for t in range(TB):
                    pe.wait_ge(y_out, j * TB + (t - RING + 1 if t >= RING else 0))
                    for f in range(KS):
                        if t == 0:
                            pe.wait_ge(a_done, j * KS + f + 1)
                        mm = nc.tensor.matmul(yp[t % RING][:], a[:, f, t * P:(t + 1) * P], sdn_T[:, f, :],
                                              start=(f == 0), stop=(f == KS - 1))
                    mm.then_inc(y_full, 1)

            pe.wait_ge(w_up_in, 16)
            expert(0)
            pe.wait_ge(consts2, 16 * N_CONST)
            nc.tensor.matmul(within[:], strict[:], sel[:], start=True, stop=True).then_inc(counts_full, 1)
            nc.tensor.matmul(totals[:], ones[:], sel[:], start=True, stop=True).then_inc(counts_full, 1)
            with pe.Fori(1, NBLK) as j:
                expert(j)

        @block.scalar
        def _(act):
            with act.Fori(0, NBLK) as j:
                for f in range(KS):
                    at = j * KS + f
                    act.wait_ge(g_full, at + 1)
                    if f >= RING:
                        act.wait_ge(a_done, at - RING + 1)
                    else:
                        act.wait_ge(a_done, j * KS)
                    nc.scalar.activation(gs[:, f % RING, :], gp[f % RING][:], ACT.Silu).then_inc(silu_done, 1)

        @block.vector
        def _(dve):
            def expert(j):
                for f in range(KS):
                    at = j * KS + f
                    dve.wait_ge(silu_done, at + 1)
                    dve.wait_ge(u_full, at + 1)
                    nc.vector.tensor_tensor(a[:, f, :], gs[:, f % RING, :], up[f % RING][:], ALU.mult) \
                        .then_inc(a_done, 1)
                dve.wait_ge(res_full, 16 * (j + 1))
                for t in range(TB):
                    dve.wait_ge(y_full, j * TB + t + 1)
                    nc.vector.tensor_tensor(res[:, t, :], yp[t % RING][:], res[:, t, :], ALU.add).then_inc(y_out, 1)

            def slots():
                done = 0

                def step(op):
                    nonlocal done
                    op.then_inc(slot_step, 1)
                    done += 1
                    dve.wait_ge(slot_step, done)

                dve.wait_ge(consts2, 16 * N_CONST)
                dve.wait_ge(counts_full, 2)
                by_expert = totals[:].rearrange("p t e -> p e t")
                step(nc.vector.tensor_copy(before[:], by_expert))
                step(nc.vector.tensor_tensor_scan(upto[:].rearrange("p e t -> p (e t)"), restart[:].rearrange("p e t -> p (e t)"),
                                                  before[:].rearrange("p e t -> p (e t)"), 0.0, ALU.mult, ALU.add))
                step(nc.vector.tensor_tensor(before[:], upto[:], before[:], ALU.subtract))
                step(nc.vector.tensor_tensor(more[:], upto[:, :, TILES - 1:TILES].broadcast_to([P, EXP, TILES]),
                                             steps[:].unsqueeze(1).broadcast_to([P, EXP, TILES]), ALU.is_gt))
                step(nc.vector.tensor_reduce(tiles[:], more[:], AX.X, ALU.add))
                step(nc.vector.tensor_tensor_scan(ends[:], ones[:, 0:EXP], tiles[:], 0.0, ALU.mult, ALU.add))
                step(nc.vector.tensor_tensor(starts[:], ends[:], tiles[:], ALU.subtract))
                step(nc.vector.tensor_tensor(place[:], within[:], before[:].rearrange("p e t -> p t e"), ALU.add))
                step(nc.vector.scalar_tensor_tensor(out=place[:], in0=starts[:].unsqueeze(1).broadcast_to([P, TILES, EXP]),
                                                    scalar=float(P), in1=place[:], op0=ALU.mult, op1=ALU.add))
                step(nc.vector.scalar_tensor_tensor(out=place[:], in0=place[:], scalar=1.0, in1=sel[:],
                                                    op0=ALU.add, op1=ALU.mult))
                for t in range(TILES):
                    step(nc.vector.max(best[:, t, :], place[:, t, :]))
                step(nc.vector.tensor_tensor(match[:], place[:].unsqueeze(2).broadcast_to([P, TILES, TOP, EXP]),
                                             best[:, :, 0:TOP].unsqueeze(3).broadcast_to([P, TILES, TOP, EXP]), ALU.is_equal))
                step(nc.vector.tensor_tensor(match[:], match[:], cw[:].unsqueeze(2).broadcast_to([P, TILES, TOP, EXP]), ALU.mult))
                step(nc.vector.tensor_reduce(pairs[:, :, :, 1].bitcast(F32), match[:], AX.X, ALU.add))
                step(nc.vector.tensor_copy(pairs[:, :, :, 0], tokens[:].unsqueeze(2).broadcast_to([P, TILES, TOP])))
                nc.vector.tensor_scalar(slot_i[:], best[:, :, 0:TOP], -1.0, None, ALU.add).then_inc(slots_ready, 1)
                step(nc.vector.tensor_tensor(t_cmp[:], ends[0:1, :].unsqueeze(1).broadcast_to([1, LIST_TILES, EXP]),
                                             numbers[:].unsqueeze(2).broadcast_to([1, LIST_TILES, EXP]), ALU.is_le))
                step(nc.vector.memset(t_exp[:, 0:1], -1.0))
                step(nc.vector.tensor_reduce(t_exp[:, 1:], t_cmp[:], AX.X, ALU.add))
                step(nc.vector.tensor_scalar(t_exp[:, 1:], t_exp[:, 1:], float(EXP - 1), None, ALU.min))
                step(nc.vector.tensor_tensor(t_new[:], t_exp[:, 1:], t_exp[:, 0:LIST_TILES], ALU.not_equal))
                step(nc.vector.tensor_scalar(t_flip[:], t_new[:], -2.0, 1.0, ALU.mult, ALU.add))
                step(nc.vector.tensor_tensor_scan(t_slot[:], t_flip[:], t_new[:], 1.0, ALU.mult, ALU.add))
                step(nc.vector.tensor_tensor(t_tmp[:], t_new[:], numbers[:], ALU.mult))
                step(nc.vector.memset(t_first[:, 0:1], 0.0))
                step(nc.vector.tensor_tensor_scan(t_first[:, 1:], ones[0:1, 0:LIST_TILES], t_tmp[:], 0.0, ALU.mult, ALU.max))
                step(nc.vector.tensor_tensor(t_tmp[:], t_new[:], t_first[:, 0:LIST_TILES], ALU.mult))
                step(nc.vector.tensor_tensor_scan(t_flip[:], ones[0:1, 0:LIST_TILES], t_tmp[:], 0.0, ALU.mult, ALU.max))
                step(nc.vector.tensor_copy(table[:, 0, :], t_exp[:, 1:]))
                step(nc.vector.tensor_copy(table[:, 1, :], t_new[:]))
                step(nc.vector.tensor_copy(table[:, 2, :], t_slot[:]))
                step(nc.vector.tensor_copy(table[:, 3, :], t_flip[:]))

            nc.vector.memset(pad_rows[:], 0.0).then_inc(pads_set, 1)
            expert(0)
            slots()
            with dve.Fori(1, NBLK) as j:
                expert(j)

        @block.gpsimd
        def _(pool):
            pool.wait_ge(pads_stored, 32)
            pool.wait_ge(slots_ready, 1)
            for t in range(TILES):
                for k in range(TOP):
                    nc.gpsimd.indirect_dma_start(
                        out=list_d, out_offset=bass.IndirectOffsetOnAxis(ap=slot_i[:, t, k:k + 1], axis=0),
                        in_=pairs[:, t, k, :], in_offset=None).then_inc(listed, 16)
            pool.wait_ge(listed, 16 * TILES * TOP)


def experts(nc, keep, up_d, dn_d, x2_d, list_d, out_d):
    ctx = ExitStack()

    def sb(name, shape, dt=F32):
        return ctx.enter_context(nc.sbuf_tensor(name, shape, dt))

    def ps(name, shape):
        return ctx.enter_context(nc.psum_tensor(name, shape, F32))

    def sem(name):
        return ctx.enter_context(nc.semaphore(name))

    ident, table = keep["ident"], keep["table"]
    w_up = sb("w_up", [P, RING, KM, 2 * INNER])
    w_dn = sb("w_dn", [P, RING, KI, DM])
    slots = sb("slots", [P, LISTS, 2], I32)
    xg = sb("xg", [P, RING, DM])
    xT = sb("xT", [P, RING, DM])
    gs = sb("gs", [P, RING, INNER])
    a = sb("a", [P, RING, INNER])
    aT = sb("aT", [P, RING, KI * P])
    y = sb("y", [P, YS, DM])

    xT_ps = ps("xT_ps", [P, DM])
    gp = [ps(f"egp{i}", [P, INNER]) for i in range(RING)]
    up = [ps(f"eup{i}", [P, INNER]) for i in range(RING)]
    aT_ps = ps("aT_ps", [P, KI * P])
    yp = [ps(f"eyp{i}", [P, DM]) for i in range(RING)]

    w_full = [sem(f"w_full{s}") for s in range(WSEMS)]
    slots_full = [sem(f"slots_full{s}") for s in range(LISTS)]
    xg_full = [sem(f"xg_full{s}") for s in range(RING)]
    y_zero = sem("y_zero")
    gathers = sem("gathers")
    scatters = sem("scatters")
    added = sem("added")
    xT_full = sem("xT_full")
    xT_out = sem("xT_out")
    up_full = sem("up_full")
    silu_done = sem("esilu_done")
    a_done = sem("ea_done")
    aT_full = sem("aT_full")
    aT_out = sem("aT_out")
    y_full = sem("ey_full")
    y_out = sem("ey_out")
    Y0 = RING

    list_tiles = list_d.rearrange("(i p) c -> i p c", p=P)

    with ctx, nc.Block() as block:
        @block.sync
        def _(sp):
            def load_slots(i, r):
                sp.dma_start(slots[:, r % LISTS, :], list_tiles[bass.ds(i, 1)].rearrange("o p c -> (o p) c")) \
                    .then_inc(slots_full[r % LISTS], 16)

            def load_weights(i, r):
                at = bass.ds(i, 1)
                expert = sp.value_load(table[0:1, 0, at], min_val=0, max_val=EXP - 1)
                starts = sp.value_load(table[0:1, 1, at], min_val=0, max_val=1)
                slot = sp.value_load(table[0:1, 2, at], min_val=0, max_val=RING - 1)
                last_run = sp.value_load(table[0:1, 3, at], min_val=0, max_val=LIST_TILES)
                sp.wait_ge(y_full, last_run)
                sp.dma_start(w_up[:, bass.ds(slot, 1)].rearrange("p o k f -> p (o k f)"),
                             up_d[bass.ds(expert, 1)].rearrange("o p k f -> (o p) (k f)"), cond=starts) \
                    .then_inc(w_full[r % WSEMS], 16)
                sp.dma_start(w_dn[:, bass.ds(slot, 1)].rearrange("p o k f -> p (o k f)"),
                             dn_d[bass.ds(expert, 1)].rearrange("o p k f -> (o p) (k f)"), cond=starts) \
                    .then_inc(w_full[r % WSEMS], 16)

            for r in range(LISTS - LAG, LISTS):
                load_slots(RUN_TILES + r - (LISTS - LAG), r)
            for r in range(LISTS - LAG):
                load_slots(r, r)
            for r in range(WSEMS):
                load_weights(r, r)
            with sp.Fori(0, TURNS) as j:
                for r in range(TURN):
                    i = j * TURN + r
                    sp.wait_ge(added, 16 * (i + 1))
                    load_slots(i + LISTS - LAG, r + LISTS - LAG)
                    sp.wait_ge(up_full, i + 1)
                    load_weights(i + WSEMS, r + WSEMS)
            sp.wait_ge(added, 16 * (RUN_TILES + LAG))
            for r in range(LISTS):
                sp.wait_ge(slots_full[r], 16 * (TURNS + 1))
            for r in range(WSEMS):
                sp.wait_ge(w_full[r], 32 * (RUN_TILES // WSEMS + 1))

        @block.tensor
        def _(pe):
            def x_turned(s, gathered, before):
                pe.wait_ge(xg_full[s], 16 * gathered)
                if before is not None:
                    pe.wait_ge(xT_out, before)
                for k in range(KM):
                    mm = nc.tensor.transpose(xT_ps[:, k * P:(k + 1) * P], xg[:, s, k * P:(k + 1) * P], ident[:])
                mm.then_inc(xT_full, 1)

            def go_up(i, r, s):
                slot = bass.ds(pe.value_load(table[0:1, 2, bass.ds(i, 1)], min_val=0, max_val=RING - 1), 1)
                pe.wait_ge(xT_out, i + 1)
                for half, bank in ((0, gp), (1, up)):
                    for k in range(KM):
                        mm = nc.tensor.matmul(bank[s][:], xT[:, s, k * P:(k + 1) * P],
                                              w_up[:, slot, k, half * INNER:(half + 1) * INNER].rearrange("p o f -> p (o f)"),
                                              start=(k == 0), stop=(k == KM - 1))
                mm.then_inc(up_full, 1)

            def a_turned(i, s):
                pe.wait_ge(a_done, i + 1)
                pe.wait_ge(aT_out, i)
                for c in range(KI):
                    n = width(c, INNER)
                    mm = nc.tensor.transpose(aT_ps[0:n, c * P:(c + 1) * P], a[:, s, c * P:c * P + n], ident[:])
                mm.then_inc(aT_full, 1)

            def go_down(i, s):
                slot = bass.ds(pe.value_load(table[0:1, 2, bass.ds(i, 1)], min_val=0, max_val=RING - 1), 1)
                pe.wait_ge(y_out, i + 1)
                pe.wait_ge(aT_out, i + 1)
                for c in range(KI):
                    n = width(c, INNER)
                    mm = nc.tensor.matmul(yp[s][:], aT[0:n, s, c * P:(c + 1) * P],
                                          w_dn[0:n, slot, c, :].rearrange("p o f -> p (o f)"),
                                          start=(c == 0), stop=(c == KI - 1))
                mm.then_inc(y_full, 1)

            x_turned(0, 1, None)
            x_turned(1, 1, 1)
            pe.wait_ge(w_full[0], 32)
            go_up(0, 0, 0)
            with pe.Fori(0, TURNS) as j:
                for r in range(TURN):
                    i = j * TURN + r
                    s = r % RING
                    a_turned(i, s)
                    x_turned(s, j * (TURN // RING) + r // RING + 2, i + 2)
                    pe.wait_ge(w_full[(r + 1) % WSEMS], j * (32 * TURN // WSEMS) + 32 * ((r + 1) // WSEMS + 1))
                    pe.wait_ge(silu_done, i)
                    pe.wait_ge(a_done, i)
                    go_up(i + 1, r + 1, (r + 1) % RING)
                    go_down(i, s)

        @block.scalar
        def _(act):
            def silu(i, s):
                act.wait_ge(up_full, i + 1)
                if not isinstance(i, int):
                    act.wait_ge(a_done, i - 1)
                nc.scalar.activation(gs[:, s, :], gp[s][:], ACT.Silu).then_inc(silu_done, 1)

            act.sem_inc(y_out, Y0)
            silu(0, 0)
            with act.Fori(0, TURNS) as j:
                for r in range(TURN):
                    i = j * TURN + r
                    silu(i + 1, (r + 1) % RING)
                    act.wait_ge(y_full, i + 1)
                    act.wait_ge(added, 16 * i)
                    nc.scalar.mul(y[:, r % YS, :], yp[r % RING][:], slots[:, r, 1:2].bitcast(F32)).then_inc(y_out, 1)

        @block.vector
        def _(dve):
            def x_out(i, s):
                dve.wait_ge(xT_full, i + 1)
                nc.vector.tensor_copy(xT[:, s, :], xT_ps[:]).then_inc(xT_out, 1)

            def swiglu(i, s):
                dve.wait_ge(silu_done, i + 1)
                nc.vector.tensor_tensor(a[:, s, :], gs[:, s, :], up[s][:], ALU.mult).then_inc(a_done, 1)

            for s in range(YS - LAG, YS):
                nc.vector.memset(y[:, s, :], 0.0).then_inc(y_zero, 1)
            x_out(0, 0)
            x_out(1, 1)
            swiglu(0, 0)
            with dve.Fori(0, TURNS) as j:
                for r in range(TURN):
                    i = j * TURN + r
                    s = r % RING
                    dve.wait_ge(aT_full, i + 1)
                    whole, n = (KI - 1) * P, width(KI - 1, INNER)
                    nc.vector.tensor_copy(aT[:, s, 0:whole], aT_ps[:, 0:whole])
                    nc.vector.tensor_copy(aT[0:n, s, whole:], aT_ps[0:n, whole:]).then_inc(aT_out, 1)
                    x_out(i + 2, s)
                    swiglu(i + 1, (r + 1) % RING)

        @block.gpsimd
        def _(pool):
            def gather(s, r, loaded, turned):
                pool.wait_ge(slots_full[r], loaded)
                if turned is not None:
                    pool.wait_ge(xT_full, turned)
                pool.sem_inc(gathers, 1)
                nc.gpsimd.indirect_dma_start(out=xg[:, s, :], out_offset=None, in_=x2_d,
                                             in_offset=bass.IndirectOffsetOnAxis(ap=slots[:, r, 0:1], axis=0)) \
                    .then_inc(xg_full[s], 16)

            def add(i, r):
                pool.wait_ge(y_out, i + Y0 - LAG + 1)
                pool.wait_ge(added, i * 16)
                pool.sem_inc(scatters, 1)
                nc.gpsimd.indirect_dma_start(out=out_d, out_offset=bass.IndirectOffsetOnAxis(ap=slots[:, r % LISTS, 0:1], axis=0),
                                             in_=y[:, r % YS, :], in_offset=None, compute_op=ALU.add).then_inc(added, 16)

            pool.wait_ge(y_zero, LAG)
            for r in range(LISTS - LAG, LISTS):
                pool.wait_ge(slots_full[r], 16)
            for s in range(RING):
                gather(s, s, 16, None)
            with pool.Fori(0, TURNS) as j:
                for r in range(TURN):
                    i = j * TURN + r
                    ahead = r + RING
                    loads = 1 + ahead // LISTS + (1 if ahead % LISTS >= LISTS - LAG else 0)
                    gather(r % RING, ahead % LISTS, 16 * (j + loads), i + 1)
                    add(i, r + LISTS - LAG)
            for r in range(LAG):
                add(RUN_TILES + r, r + LISTS - LAG)


def layer(nc, d, out_d):
    bt_d = nc.dram_tensor("bt_scratch", [NBLK + 1, NST, BLK], F32, kind="Internal").ap()
    x1_d = nc.dram_tensor("x1_scratch", [BLK + TOK, DM], F32, kind="Internal").ap()
    x2_d = nc.dram_tensor("x2_scratch", [TOK + P, DM], F32, kind="Internal").ap()
    list_d = nc.dram_tensor("list_scratch", [LIST_TILES * P, 2], I32, kind="Internal").ap()
    with ExitStack() as ctx:
        mamba(nc, ctx, d["x_pad"], d["subjects"], d["cond_w"], d["in_T"], d["xp_T"], d["dt_T"], d["out_T"], d["chan"],
              d["ident"], bt_d, x1_d)
    with ExitStack() as ctx:
        keep = {name: ctx.enter_context(nc.sbuf_tensor(name + "_kept", shape, dt)) for name, shape, dt in (
            ("ident", [P, P], F32), ("x2T", [P, KM, TOK], F32), ("sel", [P, TILES, EXP], F32),
            ("cw", [P, TILES, EXP], F32), ("table", [1, 4, LIST_TILES], I32))}
        mix(nc, keep, x1_d, d["adapters"], d, x2_d)
        shared(nc, keep, x1_d, d, list_d, out_d)
        experts(nc, keep, d["up_T"], d["dn_T"], x2_d, list_d, out_d)


def layouts(inputs):
    def get(name):
        return np.asarray(inputs[name])

    def turned(w):
        chunks = -(-w.shape[1] // P)
        padded = np.zeros((chunks * P, w.shape[0]), w.dtype)
        padded[:w.shape[1]] = w.T
        return padded.reshape(chunks, P, w.shape[0]).transpose(1, 0, 2)

    def lower(n):
        return np.broadcast_to(np.tril(np.ones((n, n), np.float32), -1), (P, n, n))

    x = get("x")
    no_rows = np.zeros((BB,) + x.shape[1:], x.dtype)
    subjects = get("itok_B_0_7")
    per_channel = np.concatenate([get("L0_attn_A_log"), get("L0_attn_conv1d_w"), get("L0_attn_dt_proj_bias")[:, None],
                                  get("L0_attn_D_param")[:, None]], 1)
    gate, up = np.split(get("L0_ffn_shared_up_w"), 2)
    rows = np.zeros((SPAD - SINNER, DM), gate.dtype)
    row_adapter = np.repeat(np.arange(NADAPT, dtype=np.float32), LRANK)
    pad_list = np.zeros((P, LIST_TILES, 2), np.int32)
    pad_list[:, :, 0] = TOK + np.arange(P)[:, None]
    restart = np.ones((P, EXP, TILES), np.float32)
    restart[:, :, 0] = 0
    arrays = {
        "x_pad": np.concatenate([no_rows, x, no_rows]),
        "subjects": np.concatenate([subjects, np.zeros(BB, subjects.dtype)])[None],
        "cond_w": np.concatenate([get("L0_cond_weights"), get("fside_8xS_0")[:, None, :]], 1),
        "in_T": turned(get("L0_attn_in_proj_w")),
        "xp_T": turned(get("L0_attn_x_proj_w")),
        "dt_T": get("L0_attn_dt_proj_w").T,
        "out_T": turned(get("L0_attn_out_proj_w")),
        "chan": per_channel.reshape(DT, P, -1).transpose(1, 0, 2),
        "ident": np.eye(P, dtype=np.float32),
        "adapters": get("itok_B_0_6")[None],
        "row_scale": np.stack([row_adapter, np.repeat(get("L0_cond2_scalings"), LRANK)], 1),
        "tri_g": lower(GROUPS),
        "tri_e": lower(EXP),
        "a_T": turned(get("L0_cond2_A").reshape(NADAPT * LRANK, DM)),
        "w_T": turned(get("L0_cond2_W")),
        "b_T": get("L0_cond2_Bm").transpose(0, 2, 1).reshape(NADAPT * LRANK, DM),
        "gate_T": turned(get("L0_ffn_gate_w")),
        "sup_T": np.concatenate([turned(np.concatenate([gate, rows])), turned(np.concatenate([up, rows]))], 2),
        "sdn_T": turned(get("L0_ffn_shared_down_w")),
        "pad_list": pad_list,
        "tokens": np.arange(TOK, dtype=np.int32).reshape(TILES, P).T,
        "strict": np.triu(np.ones((P, P), np.float32), 1),
        "ones": np.ones((P, P), np.float32),
        "restart": restart,
        "steps": np.broadcast_to(P * np.arange(TILES, dtype=np.float32), (P, TILES)),
        "numbers": np.arange(LIST_TILES, dtype=np.float32)[None],
        "up_T": np.stack([turned(w) for w in get("L0_ffn_expert_up_w")]),
        "dn_T": np.stack([turned(w) for w in get("L0_ffn_expert_down_w")]),
    }
    return {f"in_{name}": np.ascontiguousarray(a) for name, a in arrays.items()}


def kernel(**inputs):
    import concourse.bacc as bacc
    from concourse.bass_utils import run_bass_kernel_spmd

    nc = bacc.Bacc("TRN2", target_bir_lowering=False, num_devices=1)
    arrays = layouts(inputs)
    d = {name[3:]: nc.dram_tensor(name, a.shape, mybir.dt.from_np(a.dtype), kind="ExternalInput").ap()
         for name, a in arrays.items()}
    out_d = nc.dram_tensor("out", [TOK + P, DM], F32, kind="ExternalOutput").ap()
    layer(nc, d, out_d)
    r = run_bass_kernel_spmd(nc, [arrays], core_ids=[0])
    return r.results[0]["out"][:TOK].reshape(BATCH, SEQ, DM)
```

```python
from contextlib import ExitStack

import numpy as np
import concourse.bass as bass
from concourse import mybir
from concourse.alu_op_type import AluOpType as ALU

F32, I32 = mybir.dt.float32, mybir.dt.int32
ACT = mybir.ActivationFunctionType
AX = mybir.AxisListType

P = 128
LOG_EXP = "natural_log_exp_and_others"
BATCH, SEQ, DM = 32, 64, 512
TOK = BATCH * SEQ
DIN, NST, RANK, TAPS, SUBJ = 1024, 16, 128, 4, 8
BLK = 512
NBLK = TOK // BLK
BB = BLK // SEQ
TB = BLK // P
KM = DM // P
DT = DIN // P
HALVES = 2
HT = DT // HALVES
STEPS = HALVES * NST
SCANS = STEPS * HT
SUMS = STEPS * TB
RING = 2

BESIDE = [
    [["turn1"], ["z4"], ["z5", "dt4"], ["z6", "ln4"],
     ["z7", "dt5"], ["out0", "ln5"], ["out1", "cond0"], ["out2", "dt6"],
     ["out3", "cond1", "ln6"], ["out4"], ["out5", "cond2", "dt7"], ["out6", "ln7"],
     ["out7", "cond3", "skip0"], ["x0", "skip1"], ["x1", "skip2"], ["x2", "skip3"]],
    [["turn0", "x3"], ["x4"], ["x5"], ["x6"],
     ["x7"], ["silu"], ["rank0", "gate0"], ["rank1", "gate1"],
     ["dt0", "bc0", "gate2"], ["bc1", "ln0", "gate3"], ["ct", "dt1"], ["ln1", "z0"],
     ["dt2", "z1"], ["ln2", "dt3", "z2"], ["ln3", "z3"], []],
]
LINE = [pieces for half in BESIDE for pieces in half]
ROWS = BATCH + 2 * BB
CONDS = BB // RING
AHEAD = [f"cond{c}" for c in range(CONDS)] + [f"x{e}" for e in range(DT)] + [
    "silu", "rank0", "rank1", "dt0", "ln0", "bc0", "bc1", "dt1", "ln1", "ct", "dt2", "ln2", "dt3", "ln3"] + [
    f"z{e}" for e in range(HT)]
AFTER = ["turn1"] + [f"out{i}" for i in range(2 * TB)]
NEXT = set(AHEAD)


def name_and_number(piece):
    name = piece.rstrip("0123456789")
    return name, int(piece[len(name):] or 0)


EMPTIED_BY_ACT = {"cond", "x", "rank", "bc", "dt", "z"}
EMPTIED_BY_DVE = {"turn", "out", "ct"}
HALVED = {"rank", "bc", "out"}
BANKS = 2


class Use:

    def __init__(self, uses, by_act):
        self.number = len(uses)
        self.by_act = by_act
        self.place = sum(use.by_act == by_act for use in uses)
        self.bank = self.number % BANKS
        self.last = uses[-BANKS] if len(uses) >= BANKS else None


def uses_of(pieces):
    uses, of = [], {}
    for piece in pieces:
        name, i = name_and_number(piece)
        if name not in EMPTIED_BY_ACT | EMPTIED_BY_DVE:
            continue
        if name in HALVED and i % 2:
            of[piece] = of[f"{name}{i - 1}"]
            continue
        of[piece] = []
        for _ in range(HT if name == "turn" else 1):
            uses.append(Use(uses, name in EMPTIED_BY_ACT))
            of[piece].append(uses[-1])
    return uses, of


def count(uses, by_act):
    return sum(use.by_act == by_act for use in uses)


def step_of(piece):
    return next(m for m, pieces in enumerate(LINE) if piece in pieces)


BODY = [piece for pieces in LINE for piece in pieces]
USES_AHEAD, AHEAD_USE = uses_of(AHEAD)
USES_BODY, BODY_USE = uses_of(BODY)
_, AFTER_USE = uses_of(AFTER)


class Place:

    def __init__(self, section, j, piece):
        ahead = section == "ahead"
        self.block = 0 if ahead else j + 1 if piece in NEXT else j
        self.uses = {"ahead": AHEAD_USE, "body": BODY_USE, "after": AFTER_USE}[section].get(piece, [])

        def before(in_body, in_front):
            return 0 if ahead else j * in_body + in_front

        self.full_before = before(len(USES_BODY), len(USES_AHEAD))
        self.act_before = before(count(USES_BODY, True), count(USES_AHEAD, True))
        self.dve_before = before(count(USES_BODY, False), count(USES_AHEAD, False))
        if self.uses:
            use = self.uses[0]
            self.bank = use.bank
            self.full = self.full_before + use.number
            if use.by_act:
                self.act = self.act_before + use.place
            else:
                self.dve = self.dve_before + use.place


def mamba(nc, ctx, x_pad, itok, cond_w, cond_b, rows_d, in_wT, xp_wT, dt_wT, out_wT, chan, ident_d, bt_d, x1_d):
    NCH = NST + TAPS + 2
    W_PARTS = 8
    A0, W0, DTB, DSK = 0, NST, NST + TAPS, NST + TAPS + 1

    def sb(name, shape, dt=F32):
        return ctx.enter_context(nc.sbuf_tensor(name, shape, dt))

    def ps(name, shape):
        return ctx.enter_context(nc.psum_tensor(name, shape, F32))

    def sem(name):
        return ctx.enter_context(nc.semaphore(name))

    w_in = sb("w_in", [P, KM, 2 * DIN])
    w_xp = sb("w_xp", [P, DT, RANK + 2 * NST])
    w_dt = sb("w_dt", [RANK, DIN])
    w_out = sb("w_out", [P, DT, DM])
    ch = sb("ch", [P, DT, NCH])
    a_neg = sb("a_neg", [P, DT, NST])
    ident = sb("ident", [P, P])
    itok_sb = sb("itok_sb", [ROWS, 1], I32)
    row_b = sb("row_b", [ROWS, SEQ])
    x_in = sb("x_in", [SEQ + 1, RING, DM])
    w_sel = sb("w_sel", [SEQ + 1, RING, SEQ])
    hid = sb("hid", [P, KM, BLK])
    xpad = sb("xpad", [P, RING, BB, SEQ + TAPS - 1])
    xc = sb("xc", [P, DT, BLK])
    skip = sb("skip", [P, DT, BLK])
    zs = sb("zs", [P, DT, BLK])
    rank = sb("rank", [RANK, BLK])
    c_next = sb("c_next", [P, TB, NST])
    c_now = sb("c_now", [P, TB, NST])
    b_all = sb("b_all", [P, RING, BLK])
    sp_e = sb("sp_e", [P, RING, BLK])
    sp_w = sb("sp_w", [P, RING, BLK])
    delta = sb("delta", [P, DT, BLK])
    u = sb("u", [P, DT, BLK])
    dbx = sb("dbx", [P, HT, BLK])
    h = sb("h", [P, RING, HT, BLK])
    yacc = sb("yacc", [P, TB, HT * P])
    res = sb("res", [P, RING, DM])
    bc = res[0:2 * NST, 0, :]

    da = [ps(f"da{i}", [P, BLK]) for i in range(RING)]
    hT = [ps(f"hT{t}", [P, HT * P]) for t in range(TB)]
    banks = [ps(f"bank{i}", [P, BLK]) for i in range(BANKS)]

    const_in = sem("const_in")
    w_in_full = [sem(f"w_in_full{part}") for part in range(W_PARTS)]
    w_more_full = sem("w_more_full")
    x_full = sem("x_full")
    itok_in = sem("itok_in")
    row_w_full = sem("row_w_full")
    rows_stored = sem("rows_stored")
    b_full = [sem(f"b_full{s}") for s in range(RING)]
    res_full = [sem(f"res_full{s}") for s in range(RING)]
    x1_stored = [sem(f"x1_stored{s}") for s in range(RING)]
    bt_stored = sem("bt_stored")
    set_up = sem("set_up")
    ones_set = sem("ones_set")
    a_step = sem("a_step")
    bank_full = sem("bank_full")
    act_emptied = sem("act_emptied")
    dve_emptied = sem("dve_emptied")
    conv_step = sem("conv_step")
    xc_ready = sem("xc_ready")
    zs_ready = sem("zs_ready")
    skip_ready = sem("skip_ready")
    sp_step = sem("sp_step")
    sp_ready = sem("sp_ready")
    corr_ready = sem("corr_ready")
    delta_step = sem("delta_step")
    u_ready = sem("u_ready")
    da_full = sem("da_full")
    dbx_made = sem("dbx_made")
    scan_done = sem("scan_done")
    hT_full = sem("hT_full")
    sum_done = sem("sum_done")
    c_copied = sem("c_copied")
    y_ready = [sem(f"y_ready{half}") for half in range(HALVES)]
    DBX0, SCAN0, SUM0 = RING * HT, HT, TB
    X10, SKIP0, Z0, Y0 = 16, 1, 1, HT
    N_SET = 6
    row_w = u[0:ROWS].rearrange("p d t -> p (d t)")[:, 0:SEQ * SEQ]

    x_blk = x_pad.rearrange("(k b) c f -> k b c f", b=BB)
    x_rows = x_pad.rearrange("b c f -> (b c) f").rearrange("(k t p) f -> k t p f", t=TB, p=P)
    x1_rows = x1_d.rearrange("(k t p) f -> k t p f", t=TB, p=P)

    with nc.Block() as block:
        @block.sync
        def _(sp):
            def load_b(j, m):
                if m == 0:
                    sp.wait_ge(bt_stored, 16 * (j + 1))
                sp.wait_ge(dbx_made, j * SCANS + HT * (m + 1))
                row = bt_d[bass.ds(j, 1), m % NST, :]
                sp.dma_start(b_all[:, m % RING, :], row.broadcast_to([P, BLK])).then_inc(b_full[m % RING], 16)

            def load_res(j, t):
                sp.wait_ge(x1_stored[t % RING], j * 32 + 16 * (t // RING) + X10)
                if t == 0:
                    sp.wait_ge(bt_stored, 16 * (j + 1))
                    sp.wait_ge(dve_emptied, Place("body", j, "turn1").dve_before)
                sp.dma_start(res[:, t % RING, :], x_rows[bass.ds(j, 1), t].rearrange("o p f -> (o p) f")) \
                    .then_inc(res_full[t % RING], 16)

            def store_x1(section, j, t):
                sp.wait_ge(dve_emptied, Place(section, j, f"out{2 * t}").dve + 1)
                sp.dma_start(x1_rows[bass.ds(j, 1), t].rearrange("o p f -> (o p) f"), res[:, t % RING, :]) \
                    .then_inc(x1_stored[t % RING], 16)

            for s in range(RING):
                sp.sem_inc(x1_stored[s], X10)
            sp.dma_start(itok_sb[:], itok).then_inc(itok_in, 16)
            sp.dma_start(ch[:], chan).then_inc(const_in, 16)
            sp.dma_start(ident[:], ident_d).then_inc(const_in, 16)
            sp.wait_ge(row_w_full, 32)
            sp.dma_start(rows_d[:, 0:SEQ * SEQ], row_w).then_inc(rows_stored, 16)
            sp.dma_start(rows_d[:, SEQ * SEQ:], row_b[:]).then_inc(rows_stored, 16)
            for part in range(W_PARTS):
                columns = slice(part * 2 * DIN // W_PARTS, (part + 1) * 2 * DIN // W_PARTS)
                if part < CONDS:
                    sp.wait_ge(x_full, 32 * (part + 1))
                sp.dma_start(w_in[:, :, columns], in_wT[:, :, columns]).then_inc(w_in_full[part], 16)
            sp.dma_start(w_xp[:], xp_wT).then_inc(w_more_full, 16)
            sp.dma_start(w_dt[:], dt_wT).then_inc(w_more_full, 16)
            sp.dma_start(w_out[:], out_wT).then_inc(w_more_full, 16)
            with sp.Fori(0, NBLK) as j:
                for m in range(STEPS):
                    load_b(j, m)
                    for t in range(TB):
                        if m == step_of(f"out{2 * t + 1}") + 3:
                            store_x1("body", j, t)
                        if m == (step_of(f"out{2 * (t - RING) + 1}") + 4 if t >= RING else step_of("out0") - 2):
                            load_res(j, t)
            for t in range(RING):
                load_res(NBLK, t)
            for t in range(TB):
                store_x1("after", NBLK, t)
                if t + RING < TB:
                    load_res(NBLK, t + RING)
            for s in range(RING):
                sp.wait_ge(x1_stored[s], 32 * (NBLK + 1) + X10)

        @block.tensor
        def _(pe):
            def take(at, i=0):
                use = at.uses[i]
                if use.last is None:
                    pe.wait_ge(act_emptied, at.act_before)
                    pe.wait_ge(dve_emptied, at.dve_before)
                elif use.last.by_act:
                    pe.wait_ge(act_emptied, at.act_before + use.last.place + 1)
                else:
                    pe.wait_ge(dve_emptied, at.dve_before + use.last.place + 1)
                return banks[use.bank]

            def cond(at, c):
                bank = take(at)
                pe.wait_ge(x_full, at.block * (32 * CONDS) + 32 * (c + 1))
                for s in range(RING):
                    for k in range(KM):
                        mm = nc.tensor.matmul(bank[:, (s * KM + k) * SEQ:(s * KM + k + 1) * SEQ],
                                              x_in[:, s, k * P:(k + 1) * P], w_sel[:, s, :], start=True, stop=True)
                mm.then_inc(bank_full, 1)

            def in_proj(section, j, at, e):
                bank = take(at)
                if e == 0:
                    pe.wait_ge(act_emptied, Place(section, j, f"cond{CONDS - 1}").act + 1)
                for k in range(KM):
                    mm = nc.tensor.matmul(bank[:], w_in[:, k, e * P:(e + 1) * P], hid[:, k, :],
                                          start=(k == 0), stop=(k == KM - 1))
                mm.then_inc(bank_full, 1)

            def rank_proj(at, part):
                bank = banks[at.bank]
                if part == 0:
                    pe.wait_ge(xc_ready, at.block + 1)
                    take(at)
                for d in range(part * HT, part * HT + HT):
                    mm = nc.tensor.matmul(bank[:], w_xp[:, d, 0:RANK], xc[:, d, :], start=(d == 0), stop=(d == DT - 1))
                if part == 1:
                    mm.then_inc(bank_full, 1)

            def bc_proj(at, part):
                bank = banks[at.bank]
                if part == 0:
                    take(at)
                for d in range(part * HT, part * HT + HT):
                    mm = nc.tensor.matmul(bank[0:2 * NST, :], w_xp[:, d, RANK:], xc[:, d, :],
                                          start=(d == 0), stop=(d == DT - 1))
                if part == 1:
                    mm.then_inc(bank_full, 1)

            def turn_bc(section, j, at):
                bank = take(at)
                pe.wait_ge(act_emptied, Place(section, j, "bc0").act + 1)
                for t in range(TB):
                    mm = nc.tensor.matmul(bank[:, t * 2 * NST:(t + 1) * 2 * NST], bc[:, t * P:(t + 1) * P],
                                          ident[0:2 * NST, 0:2 * NST], start=True, stop=True)
                mm.then_inc(bank_full, 1)

            def dt_proj(section, j, at, d):
                bank = take(at)
                if d == 0:
                    pe.wait_ge(act_emptied, Place(section, j, "rank0").act + 1)
                nc.tensor.matmul(bank[:], w_dt[:, d * P:(d + 1) * P], rank[:], start=True, stop=True) \
                    .then_inc(bank_full, 1)

            def turn(at, half):
                pe.wait_ge(sum_done, at.block * SUMS + SUM0 + (0 if half else SUMS // HALVES))
                for d in range(HT):
                    bank = take(at, d)
                    for t in range(TB):
                        mm = nc.tensor.transpose(bank[:, t * P:(t + 1) * P], yacc[:, t, d * P:(d + 1) * P], ident[:])
                    mm.then_inc(bank_full, 1)

            def out_proj(at, i):
                t, part = divmod(i, 2)
                bank = banks[at.bank]
                if part == 0:
                    pe.wait_ge(y_ready[0], at.block * HT + Y0)
                    pe.wait_ge(y_ready[1], at.block * HT + HT)
                    take(at)
                for d in range(part * HT, part * HT + HT):
                    mm = nc.tensor.matmul(bank[:], skip[:, d, t * P:(t + 1) * P], w_out[:, d, :],
                                          start=(d == 0), stop=(d == DT - 1))
                if part == 1:
                    mm.then_inc(bank_full, 1)

            def piece_of(section, j, piece):
                at = Place(section, j, piece)
                name, i = name_and_number(piece)
                if name == "cond":
                    cond(at, i)
                elif name == "x":
                    in_proj(section, j, at, i)
                elif name == "z":
                    in_proj(section, j, at, DT + i)
                elif name == "rank":
                    rank_proj(at, i)
                elif name == "bc":
                    bc_proj(at, i)
                elif name == "ct":
                    turn_bc(section, j, at)
                elif name == "dt":
                    dt_proj(section, j, at, i)
                elif name == "turn":
                    turn(at, i)
                elif name == "out":
                    out_proj(at, i)

            def turn_h(j, m, tiles):
                pe.wait_ge(scan_done, j * SCANS + SCAN0 + HT * (m + 1))
                for t in tiles:
                    pe.wait_ge(sum_done, j * SUMS + TB * m + t + 1)
                    for d in range(HT):
                        mm = nc.tensor.transpose(hT[t][:, d * P:(d + 1) * P], h[:, m % RING, d, t * P:(t + 1) * P],
                                                 ident[:])
                    mm.then_inc(hT_full, 1)

            pe.wait_ge(const_in, 32)
            pe.wait_ge(ones_set, 1)
            for piece in AHEAD:
                name, i = name_and_number(piece)
                if name == "x" and i % (2 * DT // W_PARTS) == 0:
                    pe.wait_ge(w_in_full[i * W_PARTS // (2 * DT)], 16)
                if piece == "rank0":
                    for part in range(W_PARTS // 2, W_PARTS):
                        pe.wait_ge(w_in_full[part], 16)
                    pe.wait_ge(w_more_full, 48)
                piece_of("ahead", 0, piece)
            with pe.Fori(0, NBLK) as j:
                for m in range(STEPS):
                    mine = [piece for piece in LINE[m] if name_and_number(piece)[0] in EMPTIED_BY_ACT | EMPTIED_BY_DVE]
                    for piece in mine[:1]:
                        piece_of("body", j, piece)
                    turn_h(j, m, range(0, TB // 2))
                    for piece in mine[1:]:
                        piece_of("body", j, piece)
                    turn_h(j, m, range(TB // 2, TB))
            for piece in AFTER:
                piece_of("after", NBLK, piece)

        @block.scalar
        def _(act):
            def load_x(block, c):
                x_rows = x_blk[bass.ds(block + 1, 1), c * RING:(c + 1) * RING].rearrange("o s c f -> c (o s) f")
                act.dma_start(x_in[0:SEQ, :, :], x_rows).then_inc(x_full, 16)
                w_rows = rows_d[bass.ds(block * BB + c * RING, RING)].rearrange("s (c l) -> c s l", l=SEQ)
                act.dma_start(w_sel[:], w_rows).then_inc(x_full, 16)

            def cond(at, c):
                act.wait_ge(bank_full, at.full + 1)
                rows = slice(c * RING * SEQ, (c + 1) * RING * SEQ)
                nc.scalar.copy(hid[:, :, rows].rearrange("p k (s l) -> p s k l", s=RING),
                               banks[at.bank][:].rearrange("p (s k l) -> p s k l", s=RING, k=KM)).then_inc(act_emptied, 1)
                if c + 1 < CONDS:
                    load_x(at.block, c + 1)
                else:
                    load_x(at.block + 1, 0)

            def conv_in(section, at, e):
                act.wait_ge(bank_full, at.full + 1)
                if section == "ahead":
                    if e >= RING:
                        act.wait_ge(conv_step, (TAPS - 1) * (e - RING + 1))
                else:
                    act.wait_ge(conv_step, at.block * ((TAPS - 1) * DT) + (TAPS - 1) * (e - RING + 1))
                    act.wait_ge(u_ready, at.block * DT)
                    act.wait_ge(skip_ready, (at.block - 1) * DT + e + 1 + SKIP0)
                rows = banks[at.bank][:].rearrange("p (b l) -> p b l", b=BB)
                nc.scalar.copy(xpad[:, e % RING, :, TAPS - 1:], rows)
                nc.scalar.mul(xc[:, e, :], banks[at.bank][:], ch[:, e, W0 + TAPS - 1:W0 + TAPS]).then_inc(act_emptied, 1)

            def silus(section, j, at):
                act.wait_ge(conv_step, (at.block + 1) * ((TAPS - 1) * DT))
                nc.scalar.activation(xc[:], xc[:], ACT.Silu).then_inc(xc_ready, 1)
                if section == "body":
                    act.wait_ge(act_emptied, Place("body", j, "z7").act + 1)
                    nc.scalar.activation(zs[:], zs[:], ACT.Silu).then_inc(zs_ready, 1)
                nc.scalar.preload_act_table_set(LOG_EXP)

            def skips(j, at, i):
                for e in (2 * i, 2 * i + 1):
                    if i == 0:
                        act.wait_ge(bank_full, Place("body", j, "out7").full + 1)
                        act.wait_ge(xc_ready, at.block + 1)
                    nc.scalar.mul(skip[:, e, :], xc[:, e, :], ch[:, e, DSK:DSK + 1]).then_inc(skip_ready, 1)

            def rank_out(at):
                act.wait_ge(bank_full, at.full + 1)
                nc.scalar.copy(rank[:], banks[at.bank][:]).then_inc(act_emptied, 1)

            def bc_out(at):
                act.wait_ge(bank_full, at.full + 1)
                act.wait_ge(x1_stored[0], at.block * 32 + X10)
                nc.scalar.copy(bc, banks[at.bank][0:2 * NST, :]).then_inc(act_emptied, 1)
                act.wait_ge(act_emptied, at.act + 1)
                act.dma_start(bt_d[bass.ds(at.block, 1)].rearrange("o n t -> (o n) t"), bc[0:NST, :]).then_inc(bt_stored, 16)

            def softplus(section, at, d):
                bias = ch[:, d, DTB:DTB + 1]
                s = d % RING
                act.wait_ge(bank_full, at.full + 1)
                if section == "body" or d >= RING:
                    act.wait_ge(corr_ready, at.block * DT + d - RING + 1)
                if section == "body":
                    act.wait_ge(da_full, at.block * SCANS - (SCANS // HALVES if d < HT else 0) + 1)
                nc.scalar.activation(sp_e[:, s, :], banks[at.bank][:], ACT.Abs, bias=bias).then_inc(sp_step, 1)
                nc.scalar.activation(delta[:, d, :], banks[at.bank][:], ACT.Relu, bias=bias).then_inc(act_emptied, 1)
                act.wait_ge(sp_step, at.block * (2 * DT) + 2 * d + 1)
                nc.scalar.activation(sp_e[:, s, :], sp_e[:, s, :], ACT.Exp, scale=-1.0).then_inc(sp_step, 1)

            def log1p(section, at, d):
                s = d % RING
                act.wait_ge(sp_step, at.block * (2 * DT) + 2 * d + 2)
                if section == "body" or d >= RING:
                    act.wait_ge(delta_step, at.block * (2 * DT) + 2 * (d - RING) + 1)
                if section == "body":
                    act.wait_ge(dbx_made, at.block * SCANS + DBX0 - (SCANS // HALVES if d < HT else 0))
                nc.scalar.activation(sp_w[:, s, :], sp_e[:, s, :], ACT.Identity, bias=1.0)
                nc.scalar.activation(u[:, d, :], sp_e[:, s, :], ACT.Ln, bias=1.0).then_inc(sp_ready, 1)

            def z_out(section, at, e):
                act.wait_ge(bank_full, at.full + 1)
                if section == "body":
                    if e < HT:
                        act.wait_ge(y_ready[0], (at.block - 1) * HT + e + 1 + Y0)
                    else:
                        act.wait_ge(y_ready[1], at.block * HT + e - HT + 1)
                nc.scalar.copy(zs[:, e, :], banks[at.bank][:]).then_inc(act_emptied, 1)

            def piece_of(section, j, piece):
                at = Place(section, j, piece)
                name, i = name_and_number(piece)
                if name == "cond":
                    cond(at, i)
                elif name == "x":
                    conv_in(section, at, i)
                elif name == "silu":
                    silus(section, j, at)
                elif name == "skip":
                    skips(j, at, i)
                elif name == "rank" and i == 1:
                    rank_out(at)
                elif name == "bc" and i == 1:
                    bc_out(at)
                elif name == "dt":
                    softplus(section, at, i)
                elif name == "ln":
                    log1p(section, at, i)
                elif name == "z":
                    z_out(section, at, i)

            def decay(j, g, n, i):
                m = g * NST + n
                d = g * HT + i
                if n == 0:
                    act.wait_ge(delta_step, j * (2 * DT) + 2 * d + 2)
                act.wait_ge(scan_done, j * SCANS + HT * m + i + 1 + SCAN0 - RING)
                rows = delta[:, d, :].rearrange("p (b l) -> p b l", b=BB)
                out = da[i % RING][:].rearrange("p (b l) -> p b l", b=BB)
                nc.scalar.activation(out[:, :, 1:], rows[:, :, 1:], ACT.Exp, scale=a_neg[:, d, n:n + 1]) \
                    .then_inc(da_full, 1)

            act.sem_inc(skip_ready, SKIP0)
            act.sem_inc(zs_ready, Z0)
            nc.scalar.preload_act_table_set(LOG_EXP)
            act.wait_ge(const_in, 32)
            nc.scalar.activation(a_neg[:], ch[:, :, A0:A0 + NST], ACT.Exp).then_inc(a_step, 1)
            act.wait_ge(a_step, 1)
            nc.scalar.mul(a_neg[:], a_neg[:], -1.0).then_inc(a_step, 1)
            act.wait_ge(rows_stored, 32)
            load_x(0, 0)
            act.wait_ge(set_up, N_SET)
            act.wait_ge(a_step, 2)
            for piece in AHEAD:
                piece_of("ahead", 0, piece)
            with act.Fori(0, NBLK) as j:
                nc.scalar.preload_act_table_set(LOG_EXP)
                for m in range(STEPS):
                    for i in range(HT):
                        decay(j, *divmod(m, NST), i)
                        if m and i % RING == RING - 1:
                            mine = [piece for piece in LINE[m - 1] if name_and_number(piece)[0] not in EMPTIED_BY_DVE | {"gate"}]
                            for piece in (mine[:1] if i == RING - 1 else mine[1:]):
                                piece_of("body", j, piece)
            act.wait_ge(bt_stored, 16 * (NBLK + 1))
            act.wait_ge(x_full, 32 * (CONDS * (NBLK + 1) + 1))

        @block.vector
        def _(dve):
            def conv(at, e):
                dve.wait_ge(act_emptied, at.act + 1)
                out = xc[:, e, :].rearrange("p (b l) -> p b l", b=BB)
                for k in range(TAPS - 1):
                    if k:
                        dve.wait_ge(conv_step, at.block * ((TAPS - 1) * DT) + (TAPS - 1) * e + k)
                    nc.vector.scalar_tensor_tensor(out=out, in0=xpad[:, e % RING, :, k:k + SEQ],
                                                   scalar=ch[:, e, W0 + k:W0 + k + 1], in1=out,
                                                   op0=ALU.mult, op1=ALU.add).then_inc(conv_step, 1)

            def correct(at, d):
                s = d % RING
                dve.wait_ge(sp_ready, at.block * DT + d + 1)
                nc.vector.scalar_tensor_tensor(out=sp_w[:, s, :], in0=sp_w[:, s, :], scalar=-1.0, in1=sp_e[:, s, :],
                                               op0=ALU.add, op1=ALU.subtract, reverse1=True).then_inc(corr_ready, 1)

            def c_out(section, at):
                dve.wait_ge(bank_full, at.full + 1)
                if section == "body":
                    dve.wait_ge(c_copied, at.block)
                both = banks[at.bank][:, 0:TB * 2 * NST].rearrange("p (t n) -> p t n", t=TB)
                nc.vector.tensor_copy(c_next[:], both[:, :, NST:]).then_inc(dve_emptied, 1)

            def make_u(at, d):
                dve.wait_ge(delta_step, at.block * (2 * DT) + 2 * d + 2)
                dve.wait_ge(xc_ready, at.block + 1)
                nc.vector.tensor_tensor(u[:, d, :], delta[:, d, :], xc[:, d, :], ALU.mult).then_inc(u_ready, 1)

            def add_skip(at, half, i):
                d = half * HT + i
                dve.wait_ge(skip_ready, at.block * DT + (0 if half else d + 1) + SKIP0)
                dve.wait_ge(bank_full, at.full + i + 1)
                nc.vector.tensor_tensor(skip[:, d, :], banks[at.uses[i].bank][:], skip[:, d, :], ALU.add).then_inc(dve_emptied, 1)
                if half:
                    dve.wait_ge(zs_ready, at.block + Z0)
                    dve.wait_ge(dve_emptied, at.dve + i + 1)
                    nc.vector.tensor_tensor(skip[:, d, :], skip[:, d, :], zs[:, d, :], ALU.mult).then_inc(y_ready[1], 1)

            def residual(at, j, t):
                s = t % RING
                dve.wait_ge(res_full[s], j * 32 + 16 * (t // RING + 1))
                dve.wait_ge(bank_full, at.full + 1)
                nc.vector.tensor_tensor(res[:, s, :], banks[at.bank][:], res[:, s, :], ALU.add).then_inc(dve_emptied, 1)

            def piece_of(section, j, piece):
                at = Place(section, j, piece)
                name, i = name_and_number(piece)
                if name == "x":
                    conv(at, i)
                elif name == "ln":
                    correct(at, i)
                elif name == "ct":
                    c_out(section, at)
                elif name == "out" and i % 2:
                    residual(at, j, i // 2)

            def scan(j, g, n, i):
                m = g * NST + n
                at = j * SCANS + HT * m + i
                dve.wait_ge(da_full, at + 1)
                dve.wait_ge(dbx_made, at + DBX0 + 1)
                nc.vector.tensor_tensor_scan(h[:, n % RING, i, :], da[i % RING][:], dbx[:, i, :], 0.0,
                                             ALU.mult, ALU.add).then_inc(scan_done, 1)

            def add_state(j, g, n, t):
                at = j * SUMS + TB * (g * NST + n) + t
                scalar = c_now[:, t, n:n + 1]
                dve.wait_ge(hT_full, at + 1)
                if n == 0:
                    dve.wait_ge(c_copied, j + 1)
                    nc.vector.tensor_scalar(yacc[:, t, :], hT[t][:], scalar, None, ALU.mult).then_inc(sum_done, 1)
                else:
                    dve.wait_ge(sum_done, at + SUM0 - TB + 1)
                    nc.vector.scalar_tensor_tensor(out=yacc[:, t, :], in0=hT[t][:], scalar=scalar, in1=yacc[:, t, :],
                                                   op0=ALU.mult, op1=ALU.add).then_inc(sum_done, 1)

            dve.sem_inc(scan_done, SCAN0)
            dve.sem_inc(sum_done, SUM0)
            for s in range(RING):
                nc.vector.memset(da[s][:].rearrange("p (b l) -> p b l", b=BB)[:, :, 0:1], 0.0).then_inc(set_up, 1)
            nc.vector.memset(xpad[:, :, :, 0:TAPS - 1], 0.0).then_inc(set_up, 1)
            nc.vector.memset(x_in[SEQ:SEQ + 1, :, :], 1.0).then_inc(ones_set, 1)
            nc.vector.memset(yacc[:], 0.0).then_inc(set_up, 1)
            dve.wait_ge(set_up, N_SET)
            for piece in AHEAD:
                piece_of("ahead", 0, piece)
                if piece.startswith("ln"):
                    make_u(Place("ahead", 0, piece), name_and_number(piece)[1])
            with dve.Fori(0, NBLK) as j:
                dve.wait_ge(dve_emptied, Place("body", j, "turn1").dve_before)
                dve.wait_ge(sum_done, j * SUMS + SUM0)
                nc.vector.tensor_copy(c_now[:], c_next[:]).then_inc(c_copied, 1)
                for m in range(STEPS):
                    g, n = divmod(m, NST)
                    for i in range(HT):
                        scan(j, g, n, i)
                        if n == 0:
                            turned = f"turn{1 - g}"
                            if i == RING - 1:
                                add_skip(Place("body", j, turned), 1 - g, 0)
                            if i >= RING:
                                add_skip(Place("body", j, turned), 1 - g, i - 1)
                        elif i % RING == RING - 1:
                            for t in range(i - RING + 1, i + 1):
                                add_state(j, g, n - 1, t)
                    if n == 0:
                        add_skip(Place("body", j, turned), 1 - g, HT - 1)
                    for piece in LINE[m]:
                        if name_and_number(piece)[0] in ("out", "ct"):
                            piece_of("body", j, piece)
                    if m:
                        for piece in LINE[m - 1]:
                            if name_and_number(piece)[0] in ("x", "ln"):
                                piece_of("body", j, piece)
                    if m >= 2:
                        for piece in LINE[m - 2]:
                            if piece.startswith("ln"):
                                make_u(Place("body", j, piece), name_and_number(piece)[1])
                    if n == NST - 1:
                        for t in range(TB):
                            add_state(j, g, n, t)
                for piece in LINE[STEPS - 2]:
                    if piece.startswith("ln"):
                        make_u(Place("body", j, piece), name_and_number(piece)[1])
            for i in range(HT):
                add_skip(Place("after", NBLK, "turn1"), 1, i)
            for piece in AFTER:
                piece_of("after", NBLK, piece)

        @block.gpsimd
        def _(pool):
            def finish_delta(at, d):
                pool.wait_ge(corr_ready, at.block * DT + d + 1)
                nc.gpsimd.tensor_tensor(u[:, d, :], u[:, d, :], sp_w[:, d % RING, :], ALU.add).then_inc(delta_step, 1)
                pool.wait_ge(delta_step, at.block * (2 * DT) + 2 * d + 1)
                nc.gpsimd.tensor_tensor(delta[:, d, :], delta[:, d, :], u[:, d, :], ALU.add).then_inc(delta_step, 1)

            def gate(j, d):
                at = Place("body", j, "turn0")
                pool.wait_ge(zs_ready, at.block + 1 + Z0)
                pool.wait_ge(dve_emptied, at.dve + d + 1)
                nc.gpsimd.tensor_tensor(skip[:, d, :], skip[:, d, :], zs[:, d, :], ALU.mult).then_inc(y_ready[0], 1)

            def piece_of(section, j, piece):
                name, i = name_and_number(piece)
                if name == "ln":
                    finish_delta(Place(section, j, piece), i)
                elif name == "gate":
                    gate(j, i)

            def inflow(j, g, n, i):
                m = g * NST + n
                d = g * HT + i
                if n == 0:
                    pool.wait_ge(u_ready, j * DT + d + 1)
                if i == 0:
                    pool.wait_ge(b_full[m % RING], j * (16 * STEPS // RING) + 16 * (m // RING + 1))
                pool.wait_ge(scan_done, j * SCANS + HT * m + i + 1)
                nc.gpsimd.tensor_tensor(dbx[:, i, :], u[:, d, :], b_all[:, m % RING, :], ALU.mult) \
                    .then_inc(dbx_made, 1)

            pool.wait_ge(itok_in, 16)
            for table, rows in ((cond_w, row_w), (cond_b, row_b[:])):
                nc.gpsimd.indirect_dma_start(out=rows, out_offset=None, in_=table,
                                             in_offset=bass.IndirectOffsetOnAxis(ap=itok_sb[:, 0:1], axis=0)) \
                    .then_inc(row_w_full, 16)
            pool.sem_inc(dbx_made, DBX0)
            pool.sem_inc(y_ready[0], Y0)
            nc.gpsimd.memset(skip[:], 0.0).then_inc(set_up, 1)
            nc.gpsimd.memset(zs[:], 0.0).then_inc(set_up, 1)
            pool.wait_ge(set_up, N_SET)
            for piece in AHEAD:
                piece_of("ahead", 0, piece)
            with pool.Fori(0, NBLK) as j:
                for m in range(STEPS):
                    for i in range(HT):
                        inflow(j, *divmod(m, NST), i)
                    for behind, name in ((1, "gate"), (2, "ln")):
                        due = LINE[m - behind] if m >= behind else []
                        if m == STEPS - 1:
                            due = due + [piece for pieces in LINE[m - behind + 1:] for piece in pieces]
                        for piece in due:
                            if piece.startswith(name):
                                piece_of("body", j, piece)


NADAPT, LRANK = 8, 16
EXP, GROUPS, TOP_GROUPS, TOP = 16, 4, 2, 4
PER_GROUP = EXP // GROUPS
INNER = 352
SINNER = 2 * INNER
KI = -(-INNER // P)
KS = -(-SINNER // P)
SPAD = KS * P
TILES = TOK // P
SLOT_TILES = (TOK * TOP - EXP) // P + EXP
TURN = 8
SURE_TURNS = TOK * TOP // P // TURN
GROUP = 4
RUN_TILES = -(-SLOT_TILES // GROUP) * GROUP
GROUPS_MORE = range(SURE_TURNS * TURN, RUN_TILES, GROUP)
LISTS, YS, WSEMS = TURN, 4, 4
LAG = 3
LIST_TILES = RUN_TILES + LISTS - LAG


def width(chunk, total):
    return min(P, total - chunk * P)


def mix(nc, keep, x1_d, adapter_ids, d, x2_d):
    ctx = ExitStack()

    def sb(name, shape, dt=F32):
        return ctx.enter_context(nc.sbuf_tensor(name, shape, dt))

    def ps(name, shape):
        return ctx.enter_context(nc.psum_tensor(name, shape, F32))

    def sem(name):
        return ctx.enter_context(nc.semaphore(name))

    RANKS = 24
    ident, x2T, sel, cw = keep["ident"], keep["x2T"], keep["sel"], keep["cw"]
    w_T = sb("w_T", [P, KM, DM])
    a_T = sb("a_T", [P, KM, NADAPT * LRANK])
    b_T = sb("b_T", [NADAPT * LRANK, DM])
    gate_T = sb("gate_T", [P, KM, EXP])
    ids_i = sb("ids_i", [P, BATCH], I32)
    ids_f = sb("ids_f", [P, BATCH])
    row_scale = sb("row_scale", [P, 2])
    mask = sb("mask", [P, BATCH])
    tri_g = sb("tri_g", [P, GROUPS, GROUPS])
    tri_e = sb("tri_e", [P, EXP, EXP])
    x1_in = sb("x1_in", [P, TB, DM])
    x1T = sb("x1T", [P, KM, BLK])
    xam = sb("xam", [P, BLK])
    x2_sb = sb("x2_sb", [P, TB, DM])
    lgT = sb("lgT", [EXP, BLK])
    zero_rows = sb("zero_rows", [P, DM])
    top = sb("top", [P, TB])
    sc = sb("sc", [P, TB, EXP])
    total = sb("total", [P, TB])
    rc = sb("rc", [P, TB])
    g_top = sb("g_top", [P, TB, GROUPS])
    g_more = sb("g_more", [P, TB, GROUPS, GROUPS])
    g_tie = sb("g_tie", [P, TB, GROUPS, GROUPS])
    g_rank = sb("g_rank", [P, TB, GROUPS])
    e_more = sb("e_more", [P, TB, EXP, EXP])
    e_tie = sb("e_tie", [P, TB, EXP, EXP])
    e_rank = sb("e_rank", [P, TB, EXP])
    w_top = sb("w_top", [P, TB, EXP])

    tr = [ps(f"tr{i}", [P, BLK]) for i in range(RING)]
    xa = ps("xa", [P, BLK])
    x2p = [ps(f"x2p{i}", [P, DM]) for i in range(RING)]
    lg = ps("lg", [EXP, BLK])
    lgt = ps("lgt", [P, TB, EXP])

    consts_in = sem("consts_in")
    w_in = sem("w_in")
    ahead_in = sem("ahead_in")
    x1_full = sem("x1_full")
    zero_set = sem("zero_set")
    zero_stored = sem("zero_stored")
    mask_step = sem("mask_step")
    x1T_full = sem("x1T_full")
    x1T_out = sem("x1T_out")
    xa_full = sem("xa_full")
    xa_out = sem("xa_out")
    x2_full = sem("x2_full")
    x2_out = sem("x2_out")
    x2_stored = sem("x2_stored")
    x2T_full = sem("x2T_full")
    x2T_out = sem("x2T_out")
    lg_full = sem("lg_full")
    lg_out = sem("lg_out")
    lgt_full = sem("lgt_full")
    rank_step = sem("rank_step")
    exp_done = sem("exp_done")

    x1_blk = x1_d.rearrange("(k t p) f -> k p t f", t=TB, p=P)
    x2_blk = x2_d[0:TOK].rearrange("(k t p) f -> k p t f", t=TB, p=P)

    with ctx, nc.Block() as block:
        @block.sync
        def _(sp):
            def load_x1(j):
                sp.dma_start(x1_in[:], x1_blk[bass.ds(j + 1, 1)].rearrange("o p t f -> (o p) t f")).then_inc(x1_full, 16)

            load_x1(0)
            sp.dma_start(ident[:], d["ident"]).then_inc(consts_in, 16)
            sp.dma_start(ids_i[:], adapter_ids.broadcast_to([P, BATCH])).then_inc(consts_in, 16)
            sp.dma_start(row_scale[:], d["row_scale"]).then_inc(consts_in, 16)
            sp.dma_start(tri_g[:], d["tri_g"]).then_inc(consts_in, 16)
            sp.dma_start(tri_e[:], d["tri_e"]).then_inc(consts_in, 16)
            sp.dma_start(a_T[:], d["a_T"]).then_inc(w_in, 16)
            sp.dma_start(w_T[:], d["w_T"]).then_inc(w_in, 16)
            sp.dma_start(b_T[:], d["b_T"]).then_inc(w_in, 16)
            sp.dma_start(gate_T[:], d["gate_T"]).then_inc(w_in, 16)
            sp.dma_start(keep["sup_T"][:], d["sup_T"]).then_inc(ahead_in, 16)
            sp.dma_start(keep["sdn_T"][:], d["sdn_T"]).then_inc(ahead_in, 16)
            sp.wait_ge(zero_set, 1)
            sp.dma_start(x2_d[TOK:TOK + P], zero_rows[:]).then_inc(zero_stored, 16)
            with sp.Fori(0, NBLK - 1) as j:
                sp.wait_ge(x1T_full, KM * (j + 1))
                load_x1(j + 1)
                sp.wait_ge(x2_out, TB * (j + 1) + 1)
                sp.dma_start(x2_blk[bass.ds(j, 1)].rearrange("o p t f -> (o p) t f"), x2_sb[:]).then_inc(x2_stored, 16)
            sp.wait_ge(x2_out, TB * NBLK + 1)
            sp.dma_start(x2_blk[NBLK - 1], x2_sb[:]).then_inc(x2_stored, 16)
            sp.wait_ge(x2_stored, 16 * NBLK)
            sp.wait_ge(ahead_in, 32)
            sp.wait_ge(zero_stored, 16)

        @block.tensor
        def _(pe):
            pe.wait_ge(consts_in, 16 * 5)
            with pe.Fori(0, NBLK) as j:
                pe.wait_ge(x1_full, 16 * (j + 1))
                for k in range(KM):
                    if k < RING:
                        pe.wait_ge(x2T_out, KM * j + 1)
                    else:
                        pe.wait_ge(x1T_out, KM * j + k - RING + 1)
                    for t in range(TB):
                        mm = nc.tensor.transpose(tr[k % RING][:, t * P:(t + 1) * P], x1_in[:, t, k * P:(k + 1) * P], ident[:])
                    mm.then_inc(x1T_full, 1)
                pe.wait_ge(w_in, 64)
                for k in range(KM):
                    pe.wait_ge(x1T_out, KM * j + k + 1)
                    mm = nc.tensor.matmul(xa[:], a_T[:, k, :], x1T[:, k, :], start=(k == 0), stop=(k == KM - 1))
                mm.then_inc(xa_full, 1)
                for t in range(TB):
                    pe.wait_ge(x2_out, TB * j + (t - RING + 1 if t >= RING else 0) + 1)
                    for k in range(KM):
                        nc.tensor.matmul(x2p[t % RING][:], x1T[:, k, t * P:(t + 1) * P], w_T[:, k, :], start=(k == 0), stop=False)
                    pe.wait_ge(xa_out, j + 1)
                    nc.tensor.matmul(x2p[t % RING][:], xam[:, t * P:(t + 1) * P], b_T[:], start=False, stop=True) \
                        .then_inc(x2_full, 1)
                pe.wait_ge(x2_out, TB * (j + 1) + 1)
                for k in range(KM):
                    if k < RING:
                        pe.wait_ge(x1T_out, KM * (j + 1))
                    else:
                        pe.wait_ge(x2T_out, KM * j + k - RING + 2)
                    for t in range(TB):
                        mm = nc.tensor.transpose(tr[k % RING][:, t * P:(t + 1) * P], x2_sb[:, t, k * P:(k + 1) * P], ident[:])
                    mm.then_inc(x2T_full, 1)
                for k in range(KM):
                    pe.wait_ge(x2T_out, KM * j + k + 2)
                    mm = nc.tensor.matmul(lg[:], gate_T[:, k, :], x2T[:, k, bass.ds(j * BLK, BLK)],
                                          start=(k == 0), stop=(k == KM - 1))
                mm.then_inc(lg_full, 1)
                pe.wait_ge(rank_step, j * RANKS + 2)
                pe.wait_ge(lg_out, j + 1)
                for t in range(TB):
                    mm = nc.tensor.matmul(lgt[:, t, :], lgT[:, t * P:(t + 1) * P], ident[0:EXP, 0:EXP], start=True, stop=True)
                mm.then_inc(lgt_full, 1)

        @block.scalar
        def _(act):
            def exps(j):
                act.wait_ge(rank_step, (j + 1) * RANKS + 2)
                nc.scalar.activation(sc[:], sc[:], ACT.Exp).then_inc(exp_done, 1)

            def block_out(j, ranked):
                for k in range(KM):
                    act.wait_ge(x1T_full, KM * j + k + 1)
                    nc.scalar.copy(x1T[:, k, :], tr[k % RING][:]).then_inc(x1T_out, 1)
                for t in range(TB):
                    act.wait_ge(x2_full, TB * j + t + 1)
                    if t == 0:
                        act.wait_ge(x2_stored, 16 * j)
                    nc.scalar.copy(x2_sb[:, t, :], x2p[t % RING][:]).then_inc(x2_out, 1)
                    if t == 0 and ranked is not None:
                        exps(ranked)
                for k in range(KM):
                    act.wait_ge(x2T_full, KM * j + k + 1)
                    nc.scalar.copy(x2T[:, k, bass.ds(j * BLK, BLK)], tr[k % RING][:]).then_inc(x2T_out, 1)

            def logits_out(j):
                act.wait_ge(lg_full, j + 1)
                nc.scalar.copy(lgT[:], lg[:]).then_inc(lg_out, 1)

            act.sem_inc(x2_out, 1)
            act.sem_inc(x2T_out, 1)
            block_out(0, None)
            logits_out(0)
            with act.Fori(1, NBLK) as j:
                block_out(j, j - 1)
                logits_out(j)
            exps(NBLK - 1)

        @block.vector
        def _(dve):
            def adapt(j):
                dve.wait_ge(xa_full, j + 1)
                nc.vector.tensor_tensor(xam[:].rearrange("p (b l) -> p b l", b=BB), xa[:].rearrange("p (b l) -> p b l", b=BB),
                                        mask[:, bass.ds(j * BB, BB)].unsqueeze(2).broadcast_to([P, BB, SEQ]),
                                        ALU.mult).then_inc(xa_out, 1)

            def rank(j):
                base = (j + 1) * RANKS
                done = 0

                def step(op):
                    nonlocal done
                    op.then_inc(rank_step, 1)
                    done += 1
                    dve.wait_ge(rank_step, base + done)

                def spread(x, n):
                    return x.unsqueeze(2).broadcast_to([P, TB, n])

                dve.wait_ge(lgt_full, j + 1)
                step(nc.vector.tensor_reduce(top[:], lgt[:], AX.X, ALU.max))
                step(nc.vector.tensor_tensor(sc[:], lgt[:], spread(top[:], EXP), ALU.subtract))
                dve.wait_ge(exp_done, j + 1)
                step(nc.vector.tensor_reduce(total[:], sc[:], AX.X, ALU.add))
                step(nc.vector.reciprocal(rc[:], total[:]))
                step(nc.vector.tensor_tensor(sc[:], sc[:], spread(rc[:], EXP), ALU.mult))
                step(nc.vector.tensor_reduce(g_top[:], sc[:].rearrange("p t (g i) -> p t g i", g=GROUPS), AX.X, ALU.max))
                other = g_top[:].unsqueeze(2).broadcast_to([P, TB, GROUPS, GROUPS])
                own = g_top[:].unsqueeze(3).broadcast_to([P, TB, GROUPS, GROUPS])
                step(nc.vector.tensor_tensor(g_more[:], other, own, ALU.is_gt))
                step(nc.vector.tensor_tensor(g_tie[:], other, own, ALU.is_equal))
                step(nc.vector.tensor_tensor(g_tie[:], g_tie[:], tri_g[:].unsqueeze(1).broadcast_to([P, TB, GROUPS, GROUPS]), ALU.mult))
                step(nc.vector.tensor_tensor(g_more[:], g_more[:], g_tie[:], ALU.add))
                step(nc.vector.tensor_reduce(g_rank[:], g_more[:], AX.X, ALU.add))
                step(nc.vector.tensor_scalar(g_rank[:], g_rank[:], float(TOP_GROUPS), None, ALU.is_lt))
                step(nc.vector.tensor_tensor(sc[:].rearrange("p t (g i) -> p t g i", g=GROUPS),
                                             sc[:].rearrange("p t (g i) -> p t g i", g=GROUPS),
                                             g_rank[:].unsqueeze(3).broadcast_to([P, TB, GROUPS, PER_GROUP]), ALU.mult))
                other = sc[:].unsqueeze(2).broadcast_to([P, TB, EXP, EXP])
                own = sc[:].unsqueeze(3).broadcast_to([P, TB, EXP, EXP])
                step(nc.vector.tensor_tensor(e_more[:], other, own, ALU.is_gt))
                step(nc.vector.tensor_tensor(e_tie[:], other, own, ALU.is_equal))
                step(nc.vector.tensor_tensor(e_tie[:], e_tie[:], tri_e[:].unsqueeze(1).broadcast_to([P, TB, EXP, EXP]), ALU.mult))
                step(nc.vector.tensor_tensor(e_more[:], e_more[:], e_tie[:], ALU.add))
                step(nc.vector.tensor_reduce(e_rank[:], e_more[:], AX.X, ALU.add))
                chosen = sel[:, bass.ds(j * TB, TB), :]
                step(nc.vector.tensor_scalar(chosen, e_rank[:], float(TOP), None, ALU.is_lt))
                step(nc.vector.tensor_tensor(w_top[:], sc[:], chosen, ALU.mult))
                step(nc.vector.tensor_reduce(total[:], w_top[:], AX.X, ALU.add))
                step(nc.vector.tensor_scalar(total[:], total[:], 1e-20, None, ALU.add))
                step(nc.vector.reciprocal(rc[:], total[:]))
                step(nc.vector.tensor_tensor(cw[:, bass.ds(j * TB, TB), :], w_top[:], spread(rc[:], EXP), ALU.mult))
                assert done == RANKS

            dve.sem_inc(rank_step, RANKS)
            nc.vector.memset(zero_rows[:], 0.0).then_inc(zero_set, 1)
            dve.wait_ge(consts_in, 16 * 5)
            nc.vector.tensor_copy(ids_f[:], ids_i[:]).then_inc(mask_step, 1)
            dve.wait_ge(mask_step, 1)
            nc.vector.tensor_scalar(mask[:], ids_f[:], row_scale[:, 0:1], row_scale[:, 1:2], ALU.is_equal, ALU.mult) \
                .then_inc(mask_step, 1)
            dve.wait_ge(mask_step, 2)
            adapt(0)
            with dve.Fori(1, NBLK) as j:
                adapt(j)
                rank(j - 1)
            rank(NBLK - 1)


def shared(nc, keep, x1_d, d, list_d, out_d):
    ctx = ExitStack()

    def sb(name, shape, dt=F32):
        return ctx.enter_context(nc.sbuf_tensor(name, shape, dt))

    def ps(name, shape):
        return ctx.enter_context(nc.psum_tensor(name, shape, F32))

    def sem(name):
        return ctx.enter_context(nc.semaphore(name))

    x2T, sel, cw, table = keep["x2T"], keep["sel"], keep["cw"], keep["table"]
    sup_T, sdn_T = keep["sup_T"], keep["sdn_T"]
    res = sb("res2", [P, TB, DM])
    gs = sb("sgs", [P, RING, BLK])
    a = sb("sa", [P, KS, BLK])
    pad_list = sb("pad_list", [P, LIST_TILES, 2], I32)
    pad_rows = sb("pad_rows", [P, DM])
    tokens = sb("tokens", [P, TILES], I32)
    strict = sb("strict", [P, P])
    ones = sb("ones", [P, P])
    restart = sb("restart", [P, EXP, TILES])
    steps = sb("steps", [P, TILES])
    numbers = sb("numbers", [1, LIST_TILES])
    before = sb("before", [P, EXP, TILES])
    upto = sb("upto", [P, EXP, TILES])
    more = sb("more", [P, EXP, TILES])
    tiles = sb("tiles", [P, EXP])
    ends = sb("ends", [P, EXP])
    starts = sb("starts", [P, EXP])
    place = sb("place", [P, TILES, EXP])
    best = sb("best", [P, TILES, 8])
    match = sb("match", [P, TILES, TOP, EXP])
    pairs = sb("pairs", [P, TILES, TOP, 2], I32)
    slot_i = sb("slot_i", [P, TILES, TOP], I32)
    t_cmp = sb("t_cmp", [1, LIST_TILES, EXP])
    t_exp = sb("t_exp", [1, 1 + LIST_TILES])
    t_new = sb("t_new", [1, LIST_TILES])
    t_flip = sb("t_flip", [1, LIST_TILES])
    t_slot = sb("t_slot", [1, LIST_TILES])
    t_first = sb("t_first", [1, 1 + LIST_TILES])
    t_tmp = sb("t_tmp", [1, LIST_TILES])

    gp = [ps(f"gp{i}", [P, BLK]) for i in range(RING)]
    up = [ps(f"up{i}", [P, BLK]) for i in range(RING)]
    yp = [ps(f"yp{i}", [P, DM]) for i in range(RING)]
    within = ps("within", [P, TILES, EXP])
    totals = ps("totals", [P, TILES, EXP])

    consts2 = sem("consts2")
    res_full = sem("res2_full")
    out_stored = sem("out_stored")
    pads_stored = sem("pads_stored")
    pads_set = sem("pads_set")
    g_full = sem("g_full")
    u_full = sem("u_full")
    silu_done = sem("silu_done")
    a_done = sem("a_done")
    y_full = sem("y_full")
    y_out = sem("y_out")
    counts_full = sem("counts_full")
    slot_step = sem("slot_step")
    slots_ready = sem("slots_ready")
    listed = sem("listed")

    x1_blk = x1_d.rearrange("(k t p) f -> k p t f", t=TB, p=P)
    out_blk = out_d[0:TOK].rearrange("(k t p) f -> k p t f", t=TB, p=P)
    list_rows = list_d.rearrange("(i p) c -> p i c", p=P)
    N_CONST = 7

    with ctx, nc.Block() as block:
        @block.sync
        def _(sp):
            sp.dma_start(pad_list[:], d["pad_list"]).then_inc(consts2, 16)
            sp.dma_start(tokens[:], d["tokens"]).then_inc(consts2, 16)
            sp.dma_start(strict[:], d["strict"]).then_inc(consts2, 16)
            sp.dma_start(ones[:], d["ones"]).then_inc(consts2, 16)
            sp.dma_start(restart[:], d["restart"]).then_inc(consts2, 16)
            sp.dma_start(steps[:], d["steps"]).then_inc(consts2, 16)
            sp.dma_start(numbers[:], d["numbers"]).then_inc(consts2, 16)
            sp.wait_ge(consts2, 16 * N_CONST)
            sp.dma_start(list_rows, pad_list[:]).then_inc(pads_stored, 16)
            sp.wait_ge(pads_set, 1)
            sp.dma_start(out_d[TOK:TOK + P], pad_rows[:]).then_inc(pads_stored, 16)
            sp.sem_inc(out_stored, 16)
            with sp.Fori(0, NBLK) as j:
                sp.wait_ge(out_stored, 16 * (j + 1))
                sp.dma_start(res[:], x1_blk[bass.ds(j + 1, 1)].rearrange("o p t f -> (o p) t f")).then_inc(res_full, 16)
                sp.wait_ge(y_out, TB * (j + 1))
                sp.dma_start(out_blk[bass.ds(j, 1)].rearrange("o p t f -> (o p) t f"), res[:]).then_inc(out_stored, 16)
            sp.wait_ge(out_stored, 16 * (NBLK + 1))
            sp.wait_ge(pads_stored, 32)

        @block.tensor
        def _(pe):
            def expert(j):
                for f in range(KS):
                    at = j * KS + f
                    tokens_j = bass.ds(j * BLK, BLK)
                    if f >= RING:
                        pe.wait_ge(a_done, at - RING + 1)
                    else:
                        pe.wait_ge(a_done, j * KS)
                    for k in range(KM):
                        mm = nc.tensor.matmul(gp[f % RING][:], sup_T[:, k, f * P:(f + 1) * P], x2T[:, k, tokens_j],
                                              start=(k == 0), stop=(k == KM - 1))
                    mm.then_inc(g_full, 1)
                    for k in range(KM):
                        mm = nc.tensor.matmul(up[f % RING][:], sup_T[:, k, SPAD + f * P:SPAD + (f + 1) * P],
                                              x2T[:, k, tokens_j], start=(k == 0), stop=(k == KM - 1))
                    mm.then_inc(u_full, 1)
                for t in range(TB):
                    pe.wait_ge(y_out, j * TB + (t - RING + 1 if t >= RING else 0))
                    for f in range(KS):
                        if t == 0:
                            pe.wait_ge(a_done, j * KS + f + 1)
                        mm = nc.tensor.matmul(yp[t % RING][:], a[:, f, t * P:(t + 1) * P], sdn_T[:, f, :],
                                              start=(f == 0), stop=(f == KS - 1))
                    mm.then_inc(y_full, 1)

            expert(0)
            pe.wait_ge(consts2, 16 * N_CONST)
            nc.tensor.matmul(within[:], strict[:], sel[:], start=True, stop=True).then_inc(counts_full, 1)
            nc.tensor.matmul(totals[:], ones[:], sel[:], start=True, stop=True).then_inc(counts_full, 1)
            with pe.Fori(1, NBLK) as j:
                expert(j)

        @block.scalar
        def _(act):
            def expert(j):
                for f in range(KS):
                    at = j * KS + f
                    act.wait_ge(g_full, at + 1)
                    if f >= RING:
                        act.wait_ge(a_done, at - RING + 1)
                    else:
                        act.wait_ge(a_done, j * KS)
                    nc.scalar.activation(gs[:, f % RING, :], gp[f % RING][:], ACT.Silu).then_inc(silu_done, 1)

            expert(0)
            with act.Fori(1, NBLK) as j:
                expert(j)

        @block.vector
        def _(dve):
            def expert(j):
                for f in range(KS):
                    at = j * KS + f
                    dve.wait_ge(silu_done, at + 1)
                    dve.wait_ge(u_full, at + 1)
                    nc.vector.tensor_tensor(a[:, f, :], gs[:, f % RING, :], up[f % RING][:], ALU.mult) \
                        .then_inc(a_done, 1)
                dve.wait_ge(res_full, 16 * (j + 1))
                for t in range(TB):
                    dve.wait_ge(y_full, j * TB + t + 1)
                    nc.vector.tensor_tensor(res[:, t, :], yp[t % RING][:], res[:, t, :], ALU.add).then_inc(y_out, 1)

            def slots():
                done = 0

                def step(op):
                    nonlocal done
                    op.then_inc(slot_step, 1)
                    done += 1
                    dve.wait_ge(slot_step, done)

                dve.wait_ge(consts2, 16 * N_CONST)
                dve.wait_ge(counts_full, 2)
                by_expert = totals[:].rearrange("p t e -> p e t")
                step(nc.vector.tensor_copy(before[:], by_expert))
                step(nc.vector.tensor_tensor_scan(upto[:].rearrange("p e t -> p (e t)"), restart[:].rearrange("p e t -> p (e t)"),
                                                  before[:].rearrange("p e t -> p (e t)"), 0.0, ALU.mult, ALU.add))
                step(nc.vector.tensor_tensor(before[:], upto[:], before[:], ALU.subtract))
                step(nc.vector.tensor_tensor(more[:], upto[:, :, TILES - 1:TILES].broadcast_to([P, EXP, TILES]),
                                             steps[:].unsqueeze(1).broadcast_to([P, EXP, TILES]), ALU.is_gt))
                step(nc.vector.tensor_reduce(tiles[:], more[:], AX.X, ALU.add))
                step(nc.vector.tensor_tensor_scan(ends[:], ones[:, 0:EXP], tiles[:], 0.0, ALU.mult, ALU.add))
                step(nc.vector.tensor_tensor(starts[:], ends[:], tiles[:], ALU.subtract))
                step(nc.vector.tensor_tensor(place[:], within[:], before[:].rearrange("p e t -> p t e"), ALU.add))
                step(nc.vector.scalar_tensor_tensor(out=place[:], in0=starts[:].unsqueeze(1).broadcast_to([P, TILES, EXP]),
                                                    scalar=float(P), in1=place[:], op0=ALU.mult, op1=ALU.add))
                step(nc.vector.scalar_tensor_tensor(out=place[:], in0=place[:], scalar=1.0, in1=sel[:],
                                                    op0=ALU.add, op1=ALU.mult))
                for t in range(TILES):
                    step(nc.vector.max(best[:, t, :], place[:, t, :]))
                step(nc.vector.tensor_tensor(match[:], place[:].unsqueeze(2).broadcast_to([P, TILES, TOP, EXP]),
                                             best[:, :, 0:TOP].unsqueeze(3).broadcast_to([P, TILES, TOP, EXP]), ALU.is_equal))
                step(nc.vector.tensor_tensor(match[:], match[:], cw[:].unsqueeze(2).broadcast_to([P, TILES, TOP, EXP]), ALU.mult))
                step(nc.vector.tensor_reduce(pairs[:, :, :, 1].bitcast(F32), match[:], AX.X, ALU.add))
                step(nc.vector.tensor_copy(pairs[:, :, :, 0], tokens[:].unsqueeze(2).broadcast_to([P, TILES, TOP])))
                nc.vector.tensor_scalar(slot_i[:], best[:, :, 0:TOP], -1.0, None, ALU.add).then_inc(slots_ready, 1)
                step(nc.vector.tensor_tensor(t_cmp[:], ends[0:1, :].unsqueeze(1).broadcast_to([1, LIST_TILES, EXP]),
                                             numbers[:].unsqueeze(2).broadcast_to([1, LIST_TILES, EXP]), ALU.is_le))
                step(nc.vector.memset(t_exp[:, 0:1], -1.0))
                step(nc.vector.tensor_reduce(t_exp[:, 1:], t_cmp[:], AX.X, ALU.add))
                step(nc.vector.tensor_scalar(t_exp[:, 1:], t_exp[:, 1:], float(EXP - 1), None, ALU.min))
                step(nc.vector.tensor_tensor(t_new[:], t_exp[:, 1:], t_exp[:, 0:LIST_TILES], ALU.not_equal))
                step(nc.vector.tensor_scalar(t_flip[:], t_new[:], -2.0, 1.0, ALU.mult, ALU.add))
                step(nc.vector.tensor_tensor_scan(t_slot[:], t_flip[:], t_new[:], 1.0, ALU.mult, ALU.add))
                step(nc.vector.tensor_tensor(t_tmp[:], t_new[:], numbers[:], ALU.mult))
                step(nc.vector.memset(t_first[:, 0:1], 0.0))
                step(nc.vector.tensor_tensor_scan(t_first[:, 1:], ones[0:1, 0:LIST_TILES], t_tmp[:], 0.0, ALU.mult, ALU.max))
                step(nc.vector.tensor_tensor(t_tmp[:], t_new[:], t_first[:, 0:LIST_TILES], ALU.mult))
                step(nc.vector.tensor_tensor_scan(t_flip[:], ones[0:1, 0:LIST_TILES], t_tmp[:], 0.0, ALU.mult, ALU.max))
                step(nc.vector.tensor_copy(table[:, 0, :], t_exp[:, 1:]))
                step(nc.vector.tensor_copy(table[:, 1, :], t_new[:]))
                step(nc.vector.tensor_copy(table[:, 2, :], t_slot[:]))
                step(nc.vector.tensor_copy(table[:, 3, :], t_flip[:]))
                step(nc.vector.tensor_tensor(table[:, 4, :], numbers[:], ends[0:1, EXP - 1:EXP].broadcast_to([1, LIST_TILES]),
                                             ALU.is_lt))
                step(nc.vector.memset(table[:, 5, 0:GROUP], 0))
                step(nc.vector.tensor_tensor(table[:, 5, GROUP:], table[:, 4, 0:LIST_TILES - GROUP], table[:, 4, GROUP:],
                                             ALU.subtract))

            nc.vector.memset(pad_rows[:], 0.0).then_inc(pads_set, 1)
            expert(0)
            slots()
            with dve.Fori(1, NBLK) as j:
                expert(j)

        @block.gpsimd
        def _(pool):
            pool.wait_ge(pads_stored, 32)
            pool.wait_ge(slots_ready, 1)
            for t in range(TILES):
                for k in range(TOP):
                    nc.gpsimd.indirect_dma_start(
                        out=list_d, out_offset=bass.IndirectOffsetOnAxis(ap=slot_i[:, t, k:k + 1], axis=0),
                        in_=pairs[:, t, k, :], in_offset=None).then_inc(listed, 16)
            pool.wait_ge(listed, 16 * TILES * TOP)


def experts(nc, keep, up_d, dn_d, x2_d, list_d, out_d):
    ctx = ExitStack()

    def sb(name, shape, dt=F32):
        return ctx.enter_context(nc.sbuf_tensor(name, shape, dt))

    def ps(name, shape):
        return ctx.enter_context(nc.psum_tensor(name, shape, F32))

    def sem(name):
        return ctx.enter_context(nc.semaphore(name))

    ident, table = keep["ident"], keep["table"]
    w_up = sb("w_up", [P, RING, KM, 2 * INNER])
    w_dn = sb("w_dn", [P, RING, KI, DM])
    slots = sb("slots", [P, LISTS, 2], I32)
    xg = sb("xg", [P, RING, DM])
    xT = sb("xT", [P, RING, DM])
    gs = sb("gs", [P, RING, INNER])
    a = sb("a", [P, RING, INNER])
    aT = sb("aT", [P, RING, KI * P])
    y = sb("y", [P, YS, DM])

    xT_ps = ps("xT_ps", [P, DM])
    gp = [ps(f"egp{i}", [P, INNER]) for i in range(RING)]
    up = [ps(f"eup{i}", [P, INNER]) for i in range(RING)]
    aT_ps = ps("aT_ps", [P, KI * P])
    yp = [ps(f"eyp{i}", [P, DM]) for i in range(RING)]

    w_full = [sem(f"w_full{s}") for s in range(WSEMS)]
    slots_full = [sem(f"slots_full{s}") for s in range(LISTS)]
    xg_full = [sem(f"xg_full{s}") for s in range(RING)]
    y_zero = sem("y_zero")
    gathers = sem("gathers")
    scatters = sem("scatters")
    added = sem("added")
    xT_full = sem("xT_full")
    xT_out = sem("xT_out")
    up_full = sem("up_full")
    silu_done = sem("esilu_done")
    a_done = sem("ea_done")
    aT_full = sem("aT_full")
    aT_out = sem("aT_out")
    y_full = sem("ey_full")
    y_out = sem("ey_out")
    Y0 = RING + 1

    list_tiles = list_d.rearrange("(i p) c -> i p c", p=P)

    def run(engine, tile):
        with engine.Fori(0, SURE_TURNS) as j:
            for r in range(TURN):
                tile(j, r)
        for first in GROUPS_MORE:
            filled = engine.value_load(table[0:1, 4, first:first + 1], min_val=0, max_val=1)
            with engine.If(filled):
                for i in range(first, first + GROUP):
                    tile(i // TURN, i % TURN)

    def end(engine, last_steps):
        for count in range(SURE_TURNS * TURN, RUN_TILES + 1, GROUP):
            ended_here = engine.value_load(table[0:1, 5, count:count + 1], min_val=0, max_val=1)
            with engine.If(ended_here):
                last_steps(count)

    with ctx, nc.Block() as block:
        @block.sync
        def _(sp):
            def load_slots(i, r):
                sp.dma_start(slots[:, r % LISTS, :], list_tiles[bass.ds(i, 1)].rearrange("o p c -> (o p) c")) \
                    .then_inc(slots_full[r % LISTS], 16)

            def load_weights(i, r):
                at = bass.ds(i, 1)
                expert = sp.value_load(table[0:1, 0, at], min_val=0, max_val=EXP - 1)
                starts = sp.value_load(table[0:1, 1, at], min_val=0, max_val=1)
                slot = sp.value_load(table[0:1, 2, at], min_val=0, max_val=RING - 1)
                last_run = sp.value_load(table[0:1, 3, at], min_val=0, max_val=LIST_TILES)
                sp.wait_ge(y_full, last_run + 1)
                sp.dma_start(w_up[:, bass.ds(slot, 1)].rearrange("p o k f -> p (o k f)"),
                             up_d[bass.ds(expert, 1)].rearrange("o p k f -> (o p) (k f)"), cond=starts) \
                    .then_inc(w_full[r % WSEMS], 16)
                sp.dma_start(w_dn[:, bass.ds(slot, 1)].rearrange("p o k f -> p (o k f)"),
                             dn_d[bass.ds(expert, 1)].rearrange("o p k f -> (o p) (k f)"), cond=starts) \
                    .then_inc(w_full[r % WSEMS], 16)

            for r in range(LISTS - LAG, LISTS):
                load_slots(RUN_TILES + r - (LISTS - LAG), r)
            for r in range(LISTS - LAG):
                load_slots(r, r)
            for r in range(WSEMS):
                load_weights(r, r)
            def tile(j, r):
                i = j * TURN + r
                sp.wait_ge(added, 16 * (i + 2))
                load_slots(i + LISTS - LAG, r + LISTS - LAG)
                sp.wait_ge(up_full, i + 1)
                load_weights(i + WSEMS, r + WSEMS)

            run(sp, tile)

            def last_steps(count):
                sp.wait_ge(added, 16 * (count + LAG + 1))
                for r in range(WSEMS):
                    sp.wait_ge(w_full[r], 32 * (count // WSEMS + 1))
                for r in range(LISTS):
                    loads = sum(i % LISTS == r for i in range(-LAG, count + LISTS - LAG))
                    sp.wait_ge(slots_full[r], 16 * loads)

            end(sp, last_steps)

        @block.tensor
        def _(pe):
            def x_turned(s, gathered, before):
                pe.wait_ge(xg_full[s], 16 * gathered)
                if before is not None:
                    pe.wait_ge(xT_out, before)
                for k in range(KM):
                    mm = nc.tensor.transpose(xT_ps[:, k * P:(k + 1) * P], xg[:, s, k * P:(k + 1) * P], ident[:])
                mm.then_inc(xT_full, 1)

            def go_up(i, r, s):
                slot = bass.ds(pe.value_load(table[0:1, 2, bass.ds(i, 1)], min_val=0, max_val=RING - 1), 1)
                pe.wait_ge(xT_out, i + 1)
                for half, bank in ((0, gp), (1, up)):
                    for k in range(KM):
                        mm = nc.tensor.matmul(bank[s][:], xT[:, s, k * P:(k + 1) * P],
                                              w_up[:, slot, k, half * INNER:(half + 1) * INNER].rearrange("p o f -> p (o f)"),
                                              start=(k == 0), stop=(k == KM - 1))
                mm.then_inc(up_full, 1)

            def a_turned(i, s):
                pe.wait_ge(a_done, i + 2)
                pe.wait_ge(aT_out, i + 1)
                for c in range(KI):
                    n = width(c, INNER)
                    mm = nc.tensor.transpose(aT_ps[0:n, c * P:(c + 1) * P], a[:, s, c * P:c * P + n], ident[:])
                mm.then_inc(aT_full, 1)

            def go_down(i, s):
                slot = bass.ds(pe.value_load(table[0:1, 2, bass.ds(i, 1)], min_val=0, max_val=RING - 1), 1)
                pe.wait_ge(y_out, i + 1 + Y0 - RING)
                pe.wait_ge(aT_out, i + 2)
                for c in range(KI):
                    n = width(c, INNER)
                    mm = nc.tensor.matmul(yp[s][:], aT[0:n, s, c * P:(c + 1) * P],
                                          w_dn[0:n, slot, c, :].rearrange("p o f -> p (o f)"),
                                          start=(c == 0), stop=(c == KI - 1))
                mm.then_inc(y_full, 1)

            pe.sem_inc(y_full, 1)
            x_turned(0, 1, None)
            x_turned(1, 1, 1)
            pe.wait_ge(w_full[0], 32)
            go_up(0, 0, 0)

            def tile(j, r):
                i = j * TURN + r
                s = r % RING
                a_turned(i, s)
                x_turned(s, j * (TURN // RING) + r // RING + 2, i + 2)
                pe.wait_ge(w_full[(r + 1) % WSEMS], j * (32 * TURN // WSEMS) + 32 * ((r + 1) // WSEMS + 1))
                pe.wait_ge(silu_done, i + 1)
                pe.wait_ge(a_done, i + 1)
                go_up(i + 1, r + 1, (r + 1) % RING)
                go_down(i, s)

            run(pe, tile)

        @block.scalar
        def _(act):
            def silu(i, s):
                act.wait_ge(up_full, i + 1)
                if not isinstance(i, int) or i:
                    act.wait_ge(a_done, i)
                nc.scalar.activation(gs[:, s, :], gp[s][:], ACT.Silu).then_inc(silu_done, 1)

            act.sem_inc(y_out, Y0)
            act.sem_inc(silu_done, 1)
            silu(0, 0)

            def tile(j, r):
                i = j * TURN + r
                silu(i + 1, (r + 1) % RING)
                act.wait_ge(y_full, i + 2)
                act.wait_ge(added, 16 * (i + 1))
                nc.scalar.mul(y[:, r % YS, :], yp[r % RING][:], slots[:, r, 1:2].bitcast(F32)).then_inc(y_out, 1)

            run(act, tile)

        @block.vector
        def _(dve):
            def x_out(i, s):
                dve.wait_ge(xT_full, i + 1)
                nc.vector.tensor_copy(xT[:, s, :], xT_ps[:]).then_inc(xT_out, 1)

            def swiglu(i, s):
                dve.wait_ge(silu_done, i + 2)
                nc.vector.tensor_tensor(a[:, s, :], gs[:, s, :], up[s][:], ALU.mult).then_inc(a_done, 1)

            dve.sem_inc(a_done, 1)
            dve.sem_inc(aT_out, 1)
            for s in range(YS - LAG, YS):
                nc.vector.memset(y[:, s, :], 0.0).then_inc(y_zero, 1)
            x_out(0, 0)
            x_out(1, 1)
            swiglu(0, 0)

            def tile(j, r):
                i = j * TURN + r
                s = r % RING
                dve.wait_ge(aT_full, i + 1)
                whole, n = (KI - 1) * P, width(KI - 1, INNER)
                nc.vector.tensor_copy(aT[:, s, 0:whole], aT_ps[:, 0:whole])
                nc.vector.tensor_copy(aT[0:n, s, whole:], aT_ps[0:n, whole:]).then_inc(aT_out, 1)
                x_out(i + 2, s)
                swiglu(i + 1, (r + 1) % RING)

            run(dve, tile)

        @block.gpsimd
        def _(pool):
            def gather(s, r, loaded, turned):
                pool.wait_ge(slots_full[r], loaded)
                if turned is not None:
                    pool.wait_ge(xT_full, turned)
                pool.sem_inc(gathers, 1)
                nc.gpsimd.indirect_dma_start(out=xg[:, s, :], out_offset=None, in_=x2_d,
                                             in_offset=bass.IndirectOffsetOnAxis(ap=slots[:, r, 0:1], axis=0)) \
                    .then_inc(xg_full[s], 16)

            def add_rows(r):
                nc.gpsimd.indirect_dma_start(out=out_d, out_offset=bass.IndirectOffsetOnAxis(ap=slots[:, r % LISTS, 0:1], axis=0),
                                             in_=y[:, r % YS, :], in_offset=None, compute_op=ALU.add).then_inc(added, 16)

            def add(i, r):
                pool.wait_ge(y_out, i + Y0 - LAG + 1)
                pool.wait_ge(added, i * 16 + 16)
                pool.sem_inc(scatters, 1)
                add_rows(r)

            pool.wait_ge(y_zero, LAG)
            for r in range(LISTS - LAG, LISTS):
                pool.wait_ge(slots_full[r], 16)
            add_rows(LISTS - 1)
            for s in range(RING):
                gather(s, s, 16, None)

            def tile(j, r):
                i = j * TURN + r
                ahead = r + RING
                loads = 1 + ahead // LISTS + (1 if ahead % LISTS >= LISTS - LAG else 0)
                gather(r % RING, ahead % LISTS, 16 * (j + loads), i + 1)
                add(i, r + LISTS - LAG)

            run(pool, tile)

            def last_steps(count):
                for i in range(count, count + LAG):
                    add(i, i % LISTS + LISTS - LAG)

            end(pool, last_steps)


def layer(nc, d, out_d):
    bt_d = nc.dram_tensor("bt_scratch", [NBLK + 1, NST, BLK], F32, kind="Internal").ap()
    rows_d = nc.dram_tensor("rows_scratch", [ROWS, SEQ * SEQ + SEQ], F32, kind="Internal").ap()
    x1_d = nc.dram_tensor("x1_scratch", [BLK + TOK, DM], F32, kind="Internal").ap()
    x2_d = nc.dram_tensor("x2_scratch", [TOK + P, DM], F32, kind="Internal").ap()
    list_d = nc.dram_tensor("list_scratch", [LIST_TILES * P, 2], I32, kind="Internal").ap()
    with ExitStack() as ctx:
        mamba(nc, ctx, d["x_pad"], d["subjects"], d["cond_w"], d["cond_b"], rows_d, d["in_T"], d["xp_T"], d["dt_T"], d["out_T"], d["chan"],
              d["ident"], bt_d, x1_d)
    with ExitStack() as ctx:
        keep = {name: ctx.enter_context(nc.sbuf_tensor(name + "_kept", shape, dt)) for name, shape, dt in (
            ("ident", [P, P], F32), ("x2T", [P, KM, TOK], F32), ("sel", [P, TILES, EXP], F32),
            ("cw", [P, TILES, EXP], F32), ("sup_T", [P, KM, 2 * SPAD], F32), ("sdn_T", [P, KS, DM], F32), ("table", [1, 6, LIST_TILES], I32))}
        mix(nc, keep, x1_d, d["adapters"], d, x2_d)
        shared(nc, keep, x1_d, d, list_d, out_d)
        experts(nc, keep, d["up_T"], d["dn_T"], x2_d, list_d, out_d)


def layouts(inputs):
    def get(name):
        return np.asarray(inputs[name])

    def turned(w):
        chunks = -(-w.shape[1] // P)
        padded = np.zeros((chunks * P, w.shape[0]), w.dtype)
        padded[:w.shape[1]] = w.T
        return padded.reshape(chunks, P, w.shape[0]).transpose(1, 0, 2)

    def lower(n):
        return np.broadcast_to(np.tril(np.ones((n, n), np.float32), -1), (P, n, n))

    x = get("x")
    no_rows = np.zeros((BB,) + x.shape[1:], x.dtype)
    subjects = get("itok_B_0_7")
    per_channel = np.concatenate([get("L0_attn_A_log"), get("L0_attn_conv1d_w"), get("L0_attn_dt_proj_bias")[:, None],
                                  get("L0_attn_D_param")[:, None]], 1)
    gate, up = np.split(get("L0_ffn_shared_up_w"), 2)
    rows = np.zeros((SPAD - SINNER, DM), gate.dtype)
    row_adapter = np.repeat(np.arange(NADAPT, dtype=np.float32), LRANK)
    pad_list = np.zeros((P, LIST_TILES, 2), np.int32)
    pad_list[:, :, 0] = TOK + np.arange(P)[:, None]
    restart = np.ones((P, EXP, TILES), np.float32)
    restart[:, :, 0] = 0
    arrays = {
        "x_pad": np.concatenate([no_rows, x, no_rows, no_rows]),
        "subjects": np.concatenate([subjects, np.zeros(2 * BB, subjects.dtype)])[:, None],
        "cond_w": get("L0_cond_weights").reshape(SUBJ, SEQ * SEQ),
        "cond_b": get("fside_8xS_0"),
        "in_T": turned(get("L0_attn_in_proj_w")),
        "xp_T": turned(get("L0_attn_x_proj_w")),
        "dt_T": get("L0_attn_dt_proj_w").T,
        "out_T": turned(get("L0_attn_out_proj_w")),
        "chan": per_channel.reshape(DT, P, -1).transpose(1, 0, 2),
        "ident": np.eye(P, dtype=np.float32),
        "adapters": get("itok_B_0_6")[None],
        "row_scale": np.stack([row_adapter, np.repeat(get("L0_cond2_scalings"), LRANK)], 1),
        "tri_g": lower(GROUPS),
        "tri_e": lower(EXP),
        "a_T": turned(get("L0_cond2_A").reshape(NADAPT * LRANK, DM)),
        "w_T": turned(get("L0_cond2_W")),
        "b_T": get("L0_cond2_Bm").transpose(0, 2, 1).reshape(NADAPT * LRANK, DM),
        "gate_T": turned(get("L0_ffn_gate_w")),
        "sup_T": np.concatenate([turned(np.concatenate([gate, rows])), turned(np.concatenate([up, rows]))], 2),
        "sdn_T": turned(get("L0_ffn_shared_down_w")),
        "pad_list": pad_list,
        "tokens": np.arange(TOK, dtype=np.int32).reshape(TILES, P).T,
        "strict": np.triu(np.ones((P, P), np.float32), 1),
        "ones": np.ones((P, P), np.float32),
        "restart": restart,
        "steps": np.broadcast_to(P * np.arange(TILES, dtype=np.float32), (P, TILES)),
        "numbers": np.arange(LIST_TILES, dtype=np.float32)[None],
        "up_T": np.stack([turned(w) for w in get("L0_ffn_expert_up_w")]),
        "dn_T": np.stack([turned(w) for w in get("L0_ffn_expert_down_w")]),
    }
    return {f"in_{name}": np.ascontiguousarray(a) for name, a in arrays.items()}


def kernel(**inputs):
    import concourse.bacc as bacc
    from concourse.bass_utils import run_bass_kernel_spmd

    nc = bacc.Bacc("TRN2", target_bir_lowering=False, num_devices=1)
    arrays = layouts(inputs)
    d = {name[3:]: nc.dram_tensor(name, a.shape, mybir.dt.from_np(a.dtype), kind="ExternalInput").ap()
         for name, a in arrays.items()}
    out_d = nc.dram_tensor("out", [TOK + P, DM], F32, kind="ExternalOutput").ap()
    layer(nc, d, out_d)
    r = run_bass_kernel_spmd(nc, [arrays], core_ids=[0])
    return r.results[0]["out"][:TOK].reshape(BATCH, SEQ, DM)
```

```python
from contextlib import ExitStack

import numpy as np
import concourse.bass as bass
from concourse import mybir
from concourse.alu_op_type import AluOpType as ALU

F32, I32 = mybir.dt.float32, mybir.dt.int32
ACT = mybir.ActivationFunctionType
AX = mybir.AxisListType

P = 128
LOG_EXP = "natural_log_exp_and_others"
BATCH, SEQ, DM = 32, 64, 512
TOK = BATCH * SEQ
DIN, NST, RANK, TAPS, SUBJ = 1024, 16, 128, 4, 8
BLK = 512
NBLK = TOK // BLK
BB = BLK // SEQ
TB = BLK // P
KM = DM // P
DT = DIN // P
HALVES = 2
HT = DT // HALVES
STEPS = HALVES * NST
SCANS = STEPS * HT
SUMS = STEPS * TB
RING = 2

BESIDE = [
    [["turn1"], ["z4"], ["z5", "dt4"], ["z6", "ln4"],
     ["z7", "dt5"], ["out0", "ln5"], ["out1", "cond0"], ["out2", "dt6"],
     ["out3", "cond1", "ln6"], ["out4"], ["out5", "cond2", "dt7"], ["out6", "ln7"],
     ["out7", "cond3", "skip0"], ["x0", "skip1"], ["x1", "skip2"], ["x2", "skip3"]],
    [["turn0", "x3"], ["x4"], ["x5"], ["x6"],
     ["x7"], ["silu"], ["rank0", "gate0"], ["rank1", "gate1"],
     ["dt0", "bc0", "gate2"], ["bc1", "ln0", "gate3"], ["ct", "dt1"], ["ln1", "z0"],
     ["dt2", "z1"], ["ln2", "dt3", "z2"], ["ln3", "z3"], []],
]
LINE = [pieces for half in BESIDE for pieces in half]
ROWS = BATCH + 2 * BB
CONDS = BB // RING
AHEAD = [f"cond{c}" for c in range(CONDS)] + [f"x{e}" for e in range(DT)] + [
    "silu", "rank0", "rank1", "dt0", "ln0", "bc0", "bc1", "dt1", "ln1", "ct", "dt2", "ln2", "dt3", "ln3"] + [
    f"z{e}" for e in range(HT)]
AFTER = ["turn1"] + [f"out{i}" for i in range(2 * TB)]
NEXT = set(AHEAD)


def name_and_number(piece):
    name = piece.rstrip("0123456789")
    return name, int(piece[len(name):] or 0)


EMPTIED_BY_ACT = {"cond", "x", "rank", "bc", "dt", "z"}
EMPTIED_BY_DVE = {"turn", "out", "ct"}
HALVED = {"rank", "bc", "out"}
BANKS = 2


class Use:

    def __init__(self, uses, by_act):
        self.number = len(uses)
        self.by_act = by_act
        self.place = sum(use.by_act == by_act for use in uses)
        self.bank = self.number % BANKS
        self.last = uses[-BANKS] if len(uses) >= BANKS else None


def uses_of(pieces):
    uses, of = [], {}
    for piece in pieces:
        name, i = name_and_number(piece)
        if name not in EMPTIED_BY_ACT | EMPTIED_BY_DVE:
            continue
        if name in HALVED and i % 2:
            of[piece] = of[f"{name}{i - 1}"]
            continue
        of[piece] = []
        for _ in range(HT if name == "turn" else 1):
            uses.append(Use(uses, name in EMPTIED_BY_ACT))
            of[piece].append(uses[-1])
    return uses, of


def count(uses, by_act):
    return sum(use.by_act == by_act for use in uses)


def step_of(piece):
    return next(m for m, pieces in enumerate(LINE) if piece in pieces)


BODY = [piece for pieces in LINE for piece in pieces]
USES_AHEAD, AHEAD_USE = uses_of(AHEAD)
USES_BODY, BODY_USE = uses_of(BODY)
_, AFTER_USE = uses_of(AFTER)


class Place:

    def __init__(self, section, j, piece):
        ahead = section == "ahead"
        self.block = 0 if ahead else j + 1 if piece in NEXT else j
        self.uses = {"ahead": AHEAD_USE, "body": BODY_USE, "after": AFTER_USE}[section].get(piece, [])

        def before(in_body, in_front):
            return 0 if ahead else j * in_body + in_front

        self.full_before = before(len(USES_BODY), len(USES_AHEAD))
        self.act_before = before(count(USES_BODY, True), count(USES_AHEAD, True))
        self.dve_before = before(count(USES_BODY, False), count(USES_AHEAD, False))
        if self.uses:
            use = self.uses[0]
            self.bank = use.bank
            self.full = self.full_before + use.number
            if use.by_act:
                self.act = self.act_before + use.place
            else:
                self.dve = self.dve_before + use.place


def mamba(nc, ctx, x_pad, itok, cond_w, cond_b, rows_d, in_wT, xp_wT, dt_wT, out_wT, chan, ident_d, bt_d, x1_d):
    NCH = NST + TAPS + 2
    W_PARTS = 8
    A0, W0, DTB, DSK = 0, NST, NST + TAPS, NST + TAPS + 1

    def sb(name, shape, dt=F32):
        return ctx.enter_context(nc.sbuf_tensor(name, shape, dt))

    def ps(name, shape):
        return ctx.enter_context(nc.psum_tensor(name, shape, F32))

    def sem(name):
        return ctx.enter_context(nc.semaphore(name))

    w_in = sb("w_in", [P, KM, 2 * DIN])
    w_xp = sb("w_xp", [P, DT, RANK + 2 * NST])
    w_dt = sb("w_dt", [RANK, DIN])
    w_out = sb("w_out", [P, DT, DM])
    ch = sb("ch", [P, DT, NCH])
    a_neg = sb("a_neg", [P, DT, NST])
    ident = sb("ident", [P, P])
    itok_sb = sb("itok_sb", [ROWS, 1], I32)
    row_b = sb("row_b", [ROWS, SEQ])
    x_in = sb("x_in", [SEQ + 1, RING, DM])
    w_sel = sb("w_sel", [SEQ + 1, RING, SEQ])
    hid = sb("hid", [P, KM, BLK])
    xpad = sb("xpad", [P, RING, BB, SEQ + TAPS - 1])
    xc = sb("xc", [P, DT, BLK])
    skip = sb("skip", [P, DT, BLK])
    zs = sb("zs", [P, DT, BLK])
    rank = sb("rank", [RANK, BLK])
    c_next = sb("c_next", [P, TB, NST])
    c_now = sb("c_now", [P, TB, NST])
    b_all = sb("b_all", [P, RING, BLK])
    sp_e = sb("sp_e", [P, RING, BLK])
    sp_w = sb("sp_w", [P, RING, BLK])
    delta = sb("delta", [P, DT, BLK])
    u = sb("u", [P, DT, BLK])
    dbx = sb("dbx", [P, HT, BLK])
    h = sb("h", [P, RING, HT, BLK])
    yacc = sb("yacc", [P, TB, HT * P])
    res = sb("res", [P, RING, DM])
    bc = res[0:2 * NST, 0, :]

    da = [ps(f"da{i}", [P, BLK]) for i in range(RING)]
    hT = [ps(f"hT{t}", [P, HT * P]) for t in range(TB)]
    banks = [ps(f"bank{i}", [P, BLK]) for i in range(BANKS)]

    const_in = sem("const_in")
    w_in_full = [sem(f"w_in_full{part}") for part in range(W_PARTS)]
    w_more_full = sem("w_more_full")
    x_full = sem("x_full")
    itok_in = sem("itok_in")
    row_w_full = sem("row_w_full")
    rows_stored = sem("rows_stored")
    b_full = [sem(f"b_full{s}") for s in range(RING)]
    res_full = [sem(f"res_full{s}") for s in range(RING)]
    x1_stored = [sem(f"x1_stored{s}") for s in range(RING)]
    bt_stored = sem("bt_stored")
    set_up = sem("set_up")
    ones_set = sem("ones_set")
    a_step = sem("a_step")
    bank_full = sem("bank_full")
    act_emptied = sem("act_emptied")
    dve_emptied = sem("dve_emptied")
    conv_step = sem("conv_step")
    xc_ready = sem("xc_ready")
    zs_ready = sem("zs_ready")
    skip_ready = sem("skip_ready")
    sp_step = sem("sp_step")
    sp_ready = sem("sp_ready")
    corr_ready = sem("corr_ready")
    delta_step = sem("delta_step")
    u_ready = sem("u_ready")
    da_full = sem("da_full")
    dbx_made = sem("dbx_made")
    scan_done = sem("scan_done")
    hT_full = sem("hT_full")
    sum_done = sem("sum_done")
    c_copied = sem("c_copied")
    y_ready = [sem(f"y_ready{half}") for half in range(HALVES)]
    DBX0, SCAN0, SUM0 = RING * HT, HT, TB
    X10, SKIP0, Z0, Y0 = 16, 1, 1, HT
    N_SET = 6
    row_w = u[0:ROWS].rearrange("p d t -> p (d t)")[:, 0:SEQ * SEQ]

    x_blk = x_pad.rearrange("(k b) c f -> k b c f", b=BB)
    x_rows = x_pad.rearrange("b c f -> (b c) f").rearrange("(k t p) f -> k t p f", t=TB, p=P)
    x1_rows = x1_d.rearrange("(k t p) f -> k t p f", t=TB, p=P)

    with nc.Block() as block:
        @block.sync
        def _(sp):
            def load_b(j, m):
                if m == 0:
                    sp.wait_ge(bt_stored, 16 * (j + 1))
                sp.wait_ge(dbx_made, j * SCANS + HT * (m + 1))
                row = bt_d[bass.ds(j, 1), m % NST, :]
                sp.dma_start(b_all[:, m % RING, :], row.broadcast_to([P, BLK])).then_inc(b_full[m % RING], 16)

            def load_res(j, t):
                sp.wait_ge(x1_stored[t % RING], j * 32 + 16 * (t // RING) + X10)
                if t == 0:
                    sp.wait_ge(bt_stored, 16 * (j + 1))
                    sp.wait_ge(dve_emptied, Place("body", j, "turn1").dve_before)
                sp.dma_start(res[:, t % RING, :], x_rows[bass.ds(j, 1), t].rearrange("o p f -> (o p) f")) \
                    .then_inc(res_full[t % RING], 16)

            def store_x1(section, j, t):
                sp.wait_ge(dve_emptied, Place(section, j, f"out{2 * t}").dve + 1)
                sp.dma_start(x1_rows[bass.ds(j, 1), t].rearrange("o p f -> (o p) f"), res[:, t % RING, :]) \
                    .then_inc(x1_stored[t % RING], 16)

            for s in range(RING):
                sp.sem_inc(x1_stored[s], X10)
            sp.dma_start(itok_sb[:], itok).then_inc(itok_in, 16)
            sp.dma_start(ch[:], chan).then_inc(const_in, 16)
            sp.dma_start(ident[:], ident_d).then_inc(const_in, 16)
            sp.wait_ge(row_w_full, 32)
            sp.dma_start(rows_d[:, 0:SEQ * SEQ], row_w).then_inc(rows_stored, 16)
            sp.dma_start(rows_d[:, SEQ * SEQ:], row_b[:]).then_inc(rows_stored, 16)
            for part in range(W_PARTS):
                columns = slice(part * 2 * DIN // W_PARTS, (part + 1) * 2 * DIN // W_PARTS)
                if part < CONDS:
                    sp.wait_ge(x_full, 32 * (part + 1))
                sp.dma_start(w_in[:, :, columns], in_wT[:, :, columns]).then_inc(w_in_full[part], 16)
            sp.dma_start(w_xp[:], xp_wT).then_inc(w_more_full, 16)
            sp.dma_start(w_dt[:], dt_wT).then_inc(w_more_full, 16)
            sp.dma_start(w_out[:], out_wT).then_inc(w_more_full, 16)
            with sp.Fori(0, NBLK) as j:
                for m in range(STEPS):
                    load_b(j, m)
                    for t in range(TB):
                        if m == step_of(f"out{2 * t + 1}") + 3:
                            store_x1("body", j, t)
                        if m == (step_of(f"out{2 * (t - RING) + 1}") + 4 if t >= RING else step_of("out0") - 2):
                            load_res(j, t)
            for t in range(RING):
                load_res(NBLK, t)
            for t in range(TB):
                store_x1("after", NBLK, t)
                if t + RING < TB:
                    load_res(NBLK, t + RING)
            for s in range(RING):
                sp.wait_ge(x1_stored[s], 32 * (NBLK + 1) + X10)

        @block.tensor
        def _(pe):
            def take(at, i=0):
                use = at.uses[i]
                if use.last is None:
                    pe.wait_ge(act_emptied, at.act_before)
                    pe.wait_ge(dve_emptied, at.dve_before)
                elif use.last.by_act:
                    pe.wait_ge(act_emptied, at.act_before + use.last.place + 1)
                else:
                    pe.wait_ge(dve_emptied, at.dve_before + use.last.place + 1)
                return banks[use.bank]

            def cond(at, c):
                bank = take(at)
                pe.wait_ge(x_full, at.block * (32 * CONDS) + 32 * (c + 1))
                for s in range(RING):
                    for k in range(KM):
                        mm = nc.tensor.matmul(bank[:, (s * KM + k) * SEQ:(s * KM + k + 1) * SEQ],
                                              x_in[:, s, k * P:(k + 1) * P], w_sel[:, s, :], start=True, stop=True)
                mm.then_inc(bank_full, 1)

            def in_proj(section, j, at, e):
                bank = take(at)
                if e == 0:
                    pe.wait_ge(act_emptied, Place(section, j, f"cond{CONDS - 1}").act + 1)
                for k in range(KM):
                    mm = nc.tensor.matmul(bank[:], w_in[:, k, e * P:(e + 1) * P], hid[:, k, :],
                                          start=(k == 0), stop=(k == KM - 1))
                mm.then_inc(bank_full, 1)

            def rank_proj(at, part):
                bank = banks[at.bank]
                if part == 0:
                    pe.wait_ge(xc_ready, at.block + 1)
                    take(at)
                for d in range(part * HT, part * HT + HT):
                    mm = nc.tensor.matmul(bank[:], w_xp[:, d, 0:RANK], xc[:, d, :], start=(d == 0), stop=(d == DT - 1))
                if part == 1:
                    mm.then_inc(bank_full, 1)

            def bc_proj(at, part):
                bank = banks[at.bank]
                if part == 0:
                    take(at)
                for d in range(part * HT, part * HT + HT):
                    mm = nc.tensor.matmul(bank[0:2 * NST, :], w_xp[:, d, RANK:], xc[:, d, :],
                                          start=(d == 0), stop=(d == DT - 1))
                if part == 1:
                    mm.then_inc(bank_full, 1)

            def turn_bc(section, j, at):
                bank = take(at)
                pe.wait_ge(act_emptied, Place(section, j, "bc0").act + 1)
                for t in range(TB):
                    mm = nc.tensor.matmul(bank[:, t * 2 * NST:(t + 1) * 2 * NST], bc[:, t * P:(t + 1) * P],
                                          ident[0:2 * NST, 0:2 * NST], start=True, stop=True)
                mm.then_inc(bank_full, 1)

            def dt_proj(section, j, at, d):
                bank = take(at)
                if d == 0:
                    pe.wait_ge(act_emptied, Place(section, j, "rank0").act + 1)
                nc.tensor.matmul(bank[:], w_dt[:, d * P:(d + 1) * P], rank[:], start=True, stop=True) \
                    .then_inc(bank_full, 1)

            def turn(at, half):
                pe.wait_ge(sum_done, at.block * SUMS + SUM0 + (0 if half else SUMS // HALVES))
                for d in range(HT):
                    bank = take(at, d)
                    for t in range(TB):
                        mm = nc.tensor.transpose(bank[:, t * P:(t + 1) * P], yacc[:, t, d * P:(d + 1) * P], ident[:])
                    mm.then_inc(bank_full, 1)

            def out_proj(at, i):
                t, part = divmod(i, 2)
                bank = banks[at.bank]
                if part == 0:
                    pe.wait_ge(y_ready[0], at.block * HT + Y0)
                    pe.wait_ge(y_ready[1], at.block * HT + HT)
                    take(at)
                for d in range(part * HT, part * HT + HT):
                    mm = nc.tensor.matmul(bank[:], skip[:, d, t * P:(t + 1) * P], w_out[:, d, :],
                                          start=(d == 0), stop=(d == DT - 1))
                if part == 1:
                    mm.then_inc(bank_full, 1)

            def piece_of(section, j, piece):
                at = Place(section, j, piece)
                name, i = name_and_number(piece)
                if name == "cond":
                    cond(at, i)
                elif name == "x":
                    in_proj(section, j, at, i)
                elif name == "z":
                    in_proj(section, j, at, DT + i)
                elif name == "rank":
                    rank_proj(at, i)
                elif name == "bc":
                    bc_proj(at, i)
                elif name == "ct":
                    turn_bc(section, j, at)
                elif name == "dt":
                    dt_proj(section, j, at, i)
                elif name == "turn":
                    turn(at, i)
                elif name == "out":
                    out_proj(at, i)

            def turn_h(j, m, tiles):
                pe.wait_ge(scan_done, j * SCANS + SCAN0 + HT * (m + 1))
                for t in tiles:
                    pe.wait_ge(sum_done, j * SUMS + TB * m + t + 1)
                    for d in range(HT):
                        mm = nc.tensor.transpose(hT[t][:, d * P:(d + 1) * P], h[:, m % RING, d, t * P:(t + 1) * P],
                                                 ident[:])
                    mm.then_inc(hT_full, 1)

            pe.wait_ge(const_in, 32)
            pe.wait_ge(ones_set, 1)
            for piece in AHEAD:
                name, i = name_and_number(piece)
                if name == "x" and i % (2 * DT // W_PARTS) == 0:
                    pe.wait_ge(w_in_full[i * W_PARTS // (2 * DT)], 16)
                if piece == "rank0":
                    for part in range(W_PARTS // 2, W_PARTS):
                        pe.wait_ge(w_in_full[part], 16)
                    pe.wait_ge(w_more_full, 48)
                piece_of("ahead", 0, piece)
            with pe.Fori(0, NBLK) as j:
                for m in range(STEPS):
                    mine = [piece for piece in LINE[m] if name_and_number(piece)[0] in EMPTIED_BY_ACT | EMPTIED_BY_DVE]
                    for piece in mine[:1]:
                        piece_of("body", j, piece)
                    turn_h(j, m, range(0, TB // 2))
                    for piece in mine[1:]:
                        piece_of("body", j, piece)
                    turn_h(j, m, range(TB // 2, TB))
            for piece in AFTER:
                piece_of("after", NBLK, piece)

        @block.scalar
        def _(act):
            def load_x(block, c):
                x_rows = x_blk[bass.ds(block + 1, 1), c * RING:(c + 1) * RING].rearrange("o s c f -> c (o s) f")
                act.dma_start(x_in[0:SEQ, :, :], x_rows).then_inc(x_full, 16)
                w_rows = rows_d[bass.ds(block * BB + c * RING, RING)].rearrange("s (c l) -> c s l", l=SEQ)
                act.dma_start(w_sel[:], w_rows).then_inc(x_full, 16)

            def cond(at, c):
                act.wait_ge(bank_full, at.full + 1)
                rows = slice(c * RING * SEQ, (c + 1) * RING * SEQ)
                nc.scalar.copy(hid[:, :, rows].rearrange("p k (s l) -> p s k l", s=RING),
                               banks[at.bank][:].rearrange("p (s k l) -> p s k l", s=RING, k=KM)).then_inc(act_emptied, 1)
                if c + 1 < CONDS:
                    load_x(at.block, c + 1)
                else:
                    load_x(at.block + 1, 0)

            def conv_in(section, at, e):
                act.wait_ge(bank_full, at.full + 1)
                if section == "ahead":
                    if e >= RING:
                        act.wait_ge(conv_step, (TAPS - 1) * (e - RING + 1))
                else:
                    act.wait_ge(conv_step, at.block * ((TAPS - 1) * DT) + (TAPS - 1) * (e - RING + 1))
                    act.wait_ge(u_ready, at.block * DT)
                    act.wait_ge(skip_ready, (at.block - 1) * DT + e + 1 + SKIP0)
                rows = banks[at.bank][:].rearrange("p (b l) -> p b l", b=BB)
                nc.scalar.copy(xpad[:, e % RING, :, TAPS - 1:], rows)
                nc.scalar.mul(xc[:, e, :], banks[at.bank][:], ch[:, e, W0 + TAPS - 1:W0 + TAPS]).then_inc(act_emptied, 1)

            def silus(section, j, at):
                act.wait_ge(conv_step, (at.block + 1) * ((TAPS - 1) * DT))
                nc.scalar.activation(xc[:], xc[:], ACT.Silu).then_inc(xc_ready, 1)
                if section == "body":
                    act.wait_ge(act_emptied, Place("body", j, "z7").act + 1)
                    nc.scalar.activation(zs[:], zs[:], ACT.Silu).then_inc(zs_ready, 1)
                nc.scalar.preload_act_table_set(LOG_EXP)

            def skips(j, at, i):
                for e in (2 * i, 2 * i + 1):
                    if i == 0:
                        act.wait_ge(bank_full, Place("body", j, "out7").full + 1)
                        act.wait_ge(xc_ready, at.block + 1)
                    nc.scalar.mul(skip[:, e, :], xc[:, e, :], ch[:, e, DSK:DSK + 1]).then_inc(skip_ready, 1)

            def rank_out(at):
                act.wait_ge(bank_full, at.full + 1)
                nc.scalar.copy(rank[:], banks[at.bank][:]).then_inc(act_emptied, 1)

            def bc_out(at):
                act.wait_ge(bank_full, at.full + 1)
                act.wait_ge(x1_stored[0], at.block * 32 + X10)
                nc.scalar.copy(bc, banks[at.bank][0:2 * NST, :]).then_inc(act_emptied, 1)
                act.wait_ge(act_emptied, at.act + 1)
                act.dma_start(bt_d[bass.ds(at.block, 1)].rearrange("o n t -> (o n) t"), bc[0:NST, :]).then_inc(bt_stored, 16)

            def softplus(section, at, d):
                bias = ch[:, d, DTB:DTB + 1]
                s = d % RING
                act.wait_ge(bank_full, at.full + 1)
                if section == "body" or d >= RING:
                    act.wait_ge(corr_ready, at.block * DT + d - RING + 1)
                if section == "body":
                    act.wait_ge(da_full, at.block * SCANS - (SCANS // HALVES if d < HT else 0) + 1)
                nc.scalar.activation(sp_e[:, s, :], banks[at.bank][:], ACT.Abs, bias=bias).then_inc(sp_step, 1)
                nc.scalar.activation(delta[:, d, :], banks[at.bank][:], ACT.Relu, bias=bias).then_inc(act_emptied, 1)
                act.wait_ge(sp_step, at.block * (2 * DT) + 2 * d + 1)
                nc.scalar.activation(sp_e[:, s, :], sp_e[:, s, :], ACT.Exp, scale=-1.0).then_inc(sp_step, 1)

            def log1p(section, at, d):
                s = d % RING
                act.wait_ge(sp_step, at.block * (2 * DT) + 2 * d + 2)
                if section == "body" or d >= RING:
                    act.wait_ge(delta_step, at.block * (2 * DT) + 2 * (d - RING) + 1)
                if section == "body":
                    act.wait_ge(dbx_made, at.block * SCANS + DBX0 - (SCANS // HALVES if d < HT else 0))
                nc.scalar.activation(sp_w[:, s, :], sp_e[:, s, :], ACT.Identity, bias=1.0)
                nc.scalar.activation(u[:, d, :], sp_e[:, s, :], ACT.Ln, bias=1.0).then_inc(sp_ready, 1)

            def z_out(section, at, e):
                act.wait_ge(bank_full, at.full + 1)
                if section == "body":
                    if e < HT:
                        act.wait_ge(y_ready[0], (at.block - 1) * HT + e + 1 + Y0)
                    else:
                        act.wait_ge(y_ready[1], at.block * HT + e - HT + 1)
                nc.scalar.copy(zs[:, e, :], banks[at.bank][:]).then_inc(act_emptied, 1)

            def piece_of(section, j, piece):
                at = Place(section, j, piece)
                name, i = name_and_number(piece)
                if name == "cond":
                    cond(at, i)
                elif name == "x":
                    conv_in(section, at, i)
                elif name == "silu":
                    silus(section, j, at)
                elif name == "skip":
                    skips(j, at, i)
                elif name == "rank" and i == 1:
                    rank_out(at)
                elif name == "bc" and i == 1:
                    bc_out(at)
                elif name == "dt":
                    softplus(section, at, i)
                elif name == "ln":
                    log1p(section, at, i)
                elif name == "z":
                    z_out(section, at, i)

            def decay(j, g, n, i):
                m = g * NST + n
                d = g * HT + i
                if n == 0:
                    act.wait_ge(delta_step, j * (2 * DT) + 2 * d + 2)
                act.wait_ge(scan_done, j * SCANS + HT * m + i + 1 + SCAN0 - RING)
                rows = delta[:, d, :].rearrange("p (b l) -> p b l", b=BB)
                out = da[i % RING][:].rearrange("p (b l) -> p b l", b=BB)
                nc.scalar.activation(out[:, :, 1:], rows[:, :, 1:], ACT.Exp, scale=a_neg[:, d, n:n + 1]) \
                    .then_inc(da_full, 1)

            act.sem_inc(skip_ready, SKIP0)
            act.sem_inc(zs_ready, Z0)
            nc.scalar.preload_act_table_set(LOG_EXP)
            act.wait_ge(const_in, 32)
            nc.scalar.activation(a_neg[:], ch[:, :, A0:A0 + NST], ACT.Exp).then_inc(a_step, 1)
            act.wait_ge(a_step, 1)
            nc.scalar.mul(a_neg[:], a_neg[:], -1.0).then_inc(a_step, 1)
            act.wait_ge(rows_stored, 32)
            load_x(0, 0)
            act.wait_ge(set_up, N_SET)
            act.wait_ge(a_step, 2)
            for piece in AHEAD:
                piece_of("ahead", 0, piece)
            with act.Fori(0, NBLK) as j:
                nc.scalar.preload_act_table_set(LOG_EXP)
                for m in range(STEPS):
                    for i in range(HT):
                        decay(j, *divmod(m, NST), i)
                        if m and i % RING == RING - 1:
                            mine = [piece for piece in LINE[m - 1] if name_and_number(piece)[0] not in EMPTIED_BY_DVE | {"gate"}]
                            for piece in (mine[:1] if i == RING - 1 else mine[1:]):
                                piece_of("body", j, piece)
            act.wait_ge(bt_stored, 16 * (NBLK + 1))
            act.wait_ge(x_full, 32 * (CONDS * (NBLK + 1) + 1))

        @block.vector
        def _(dve):
            def conv(at, e):
                dve.wait_ge(act_emptied, at.act + 1)
                out = xc[:, e, :].rearrange("p (b l) -> p b l", b=BB)
                for k in range(TAPS - 1):
                    if k:
                        dve.wait_ge(conv_step, at.block * ((TAPS - 1) * DT) + (TAPS - 1) * e + k)
                    nc.vector.scalar_tensor_tensor(out=out, in0=xpad[:, e % RING, :, k:k + SEQ],
                                                   scalar=ch[:, e, W0 + k:W0 + k + 1], in1=out,
                                                   op0=ALU.mult, op1=ALU.add).then_inc(conv_step, 1)

            def correct(at, d):
                s = d % RING
                dve.wait_ge(sp_ready, at.block * DT + d + 1)
                nc.vector.scalar_tensor_tensor(out=sp_w[:, s, :], in0=sp_w[:, s, :], scalar=-1.0, in1=sp_e[:, s, :],
                                               op0=ALU.add, op1=ALU.subtract, reverse1=True).then_inc(corr_ready, 1)

            def c_out(section, at):
                dve.wait_ge(bank_full, at.full + 1)
                if section == "body":
                    dve.wait_ge(c_copied, at.block)
                both = banks[at.bank][:, 0:TB * 2 * NST].rearrange("p (t n) -> p t n", t=TB)
                nc.vector.tensor_copy(c_next[:], both[:, :, NST:]).then_inc(dve_emptied, 1)

            def make_u(at, d):
                dve.wait_ge(delta_step, at.block * (2 * DT) + 2 * d + 2)
                dve.wait_ge(xc_ready, at.block + 1)
                nc.vector.tensor_tensor(u[:, d, :], delta[:, d, :], xc[:, d, :], ALU.mult).then_inc(u_ready, 1)

            def add_skip(at, half, i):
                d = half * HT + i
                dve.wait_ge(skip_ready, at.block * DT + (0 if half else d + 1) + SKIP0)
                dve.wait_ge(bank_full, at.full + i + 1)
                nc.vector.tensor_tensor(skip[:, d, :], banks[at.uses[i].bank][:], skip[:, d, :], ALU.add).then_inc(dve_emptied, 1)
                if half:
                    dve.wait_ge(zs_ready, at.block + Z0)
                    dve.wait_ge(dve_emptied, at.dve + i + 1)
                    nc.vector.tensor_tensor(skip[:, d, :], skip[:, d, :], zs[:, d, :], ALU.mult).then_inc(y_ready[1], 1)

            def residual(at, j, t):
                s = t % RING
                dve.wait_ge(res_full[s], j * 32 + 16 * (t // RING + 1))
                dve.wait_ge(bank_full, at.full + 1)
                nc.vector.tensor_tensor(res[:, s, :], banks[at.bank][:], res[:, s, :], ALU.add).then_inc(dve_emptied, 1)

            def piece_of(section, j, piece):
                at = Place(section, j, piece)
                name, i = name_and_number(piece)
                if name == "x":
                    conv(at, i)
                elif name == "ln":
                    correct(at, i)
                elif name == "ct":
                    c_out(section, at)
                elif name == "out" and i % 2:
                    residual(at, j, i // 2)

            def scan(j, g, n, i):
                m = g * NST + n
                at = j * SCANS + HT * m + i
                dve.wait_ge(da_full, at + 1)
                dve.wait_ge(dbx_made, at + DBX0 + 1)
                nc.vector.tensor_tensor_scan(h[:, n % RING, i, :], da[i % RING][:], dbx[:, i, :], 0.0,
                                             ALU.mult, ALU.add).then_inc(scan_done, 1)

            def add_state(j, g, n, t):
                at = j * SUMS + TB * (g * NST + n) + t
                scalar = c_now[:, t, n:n + 1]
                dve.wait_ge(hT_full, at + 1)
                if n == 0:
                    dve.wait_ge(c_copied, j + 1)
                    nc.vector.tensor_scalar(yacc[:, t, :], hT[t][:], scalar, None, ALU.mult).then_inc(sum_done, 1)
                else:
                    dve.wait_ge(sum_done, at + SUM0 - TB + 1)
                    nc.vector.scalar_tensor_tensor(out=yacc[:, t, :], in0=hT[t][:], scalar=scalar, in1=yacc[:, t, :],
                                                   op0=ALU.mult, op1=ALU.add).then_inc(sum_done, 1)

            dve.sem_inc(scan_done, SCAN0)
            dve.sem_inc(sum_done, SUM0)
            for s in range(RING):
                nc.vector.memset(da[s][:].rearrange("p (b l) -> p b l", b=BB)[:, :, 0:1], 0.0).then_inc(set_up, 1)
            nc.vector.memset(xpad[:, :, :, 0:TAPS - 1], 0.0).then_inc(set_up, 1)
            nc.vector.memset(x_in[SEQ:SEQ + 1, :, :], 1.0).then_inc(ones_set, 1)
            nc.vector.memset(yacc[:], 0.0).then_inc(set_up, 1)
            dve.wait_ge(set_up, N_SET)
            for piece in AHEAD:
                piece_of("ahead", 0, piece)
                if piece.startswith("ln"):
                    make_u(Place("ahead", 0, piece), name_and_number(piece)[1])
            with dve.Fori(0, NBLK) as j:
                dve.wait_ge(dve_emptied, Place("body", j, "turn1").dve_before)
                dve.wait_ge(sum_done, j * SUMS + SUM0)
                nc.vector.tensor_copy(c_now[:], c_next[:]).then_inc(c_copied, 1)
                for m in range(STEPS):
                    g, n = divmod(m, NST)
                    for i in range(HT):
                        scan(j, g, n, i)
                        if n == 0:
                            turned = f"turn{1 - g}"
                            if i == RING - 1:
                                add_skip(Place("body", j, turned), 1 - g, 0)
                            if i >= RING:
                                add_skip(Place("body", j, turned), 1 - g, i - 1)
                        elif i % RING == RING - 1:
                            for t in range(i - RING + 1, i + 1):
                                add_state(j, g, n - 1, t)
                    if n == 0:
                        add_skip(Place("body", j, turned), 1 - g, HT - 1)
                    for piece in LINE[m]:
                        if name_and_number(piece)[0] in ("out", "ct"):
                            piece_of("body", j, piece)
                    if m:
                        for piece in LINE[m - 1]:
                            if name_and_number(piece)[0] in ("x", "ln"):
                                piece_of("body", j, piece)
                    if m >= 2:
                        for piece in LINE[m - 2]:
                            if piece.startswith("ln"):
                                make_u(Place("body", j, piece), name_and_number(piece)[1])
                    if n == NST - 1:
                        for t in range(TB):
                            add_state(j, g, n, t)
                for piece in LINE[STEPS - 2]:
                    if piece.startswith("ln"):
                        make_u(Place("body", j, piece), name_and_number(piece)[1])
            for i in range(HT):
                add_skip(Place("after", NBLK, "turn1"), 1, i)
            for piece in AFTER:
                piece_of("after", NBLK, piece)

        @block.gpsimd
        def _(pool):
            def finish_delta(at, d):
                pool.wait_ge(corr_ready, at.block * DT + d + 1)
                nc.gpsimd.tensor_tensor(u[:, d, :], u[:, d, :], sp_w[:, d % RING, :], ALU.add).then_inc(delta_step, 1)
                pool.wait_ge(delta_step, at.block * (2 * DT) + 2 * d + 1)
                nc.gpsimd.tensor_tensor(delta[:, d, :], delta[:, d, :], u[:, d, :], ALU.add).then_inc(delta_step, 1)

            def gate(j, d):
                at = Place("body", j, "turn0")
                pool.wait_ge(zs_ready, at.block + 1 + Z0)
                pool.wait_ge(dve_emptied, at.dve + d + 1)
                nc.gpsimd.tensor_tensor(skip[:, d, :], skip[:, d, :], zs[:, d, :], ALU.mult).then_inc(y_ready[0], 1)

            def piece_of(section, j, piece):
                name, i = name_and_number(piece)
                if name == "ln":
                    finish_delta(Place(section, j, piece), i)
                elif name == "gate":
                    gate(j, i)

            def inflow(j, g, n, i):
                m = g * NST + n
                d = g * HT + i
                if n == 0:
                    pool.wait_ge(u_ready, j * DT + d + 1)
                if i == 0:
                    pool.wait_ge(b_full[m % RING], j * (16 * STEPS // RING) + 16 * (m // RING + 1))
                pool.wait_ge(scan_done, j * SCANS + HT * m + i + 1)
                nc.gpsimd.tensor_tensor(dbx[:, i, :], u[:, d, :], b_all[:, m % RING, :], ALU.mult) \
                    .then_inc(dbx_made, 1)

            pool.wait_ge(itok_in, 16)
            for table, rows in ((cond_w, row_w), (cond_b, row_b[:])):
                nc.gpsimd.indirect_dma_start(out=rows, out_offset=None, in_=table,
                                             in_offset=bass.IndirectOffsetOnAxis(ap=itok_sb[:, 0:1], axis=0)) \
                    .then_inc(row_w_full, 16)
            pool.sem_inc(dbx_made, DBX0)
            pool.sem_inc(y_ready[0], Y0)
            nc.gpsimd.memset(skip[:], 0.0).then_inc(set_up, 1)
            nc.gpsimd.memset(zs[:], 0.0).then_inc(set_up, 1)
            pool.wait_ge(set_up, N_SET)
            for piece in AHEAD:
                piece_of("ahead", 0, piece)
            with pool.Fori(0, NBLK) as j:
                for m in range(STEPS):
                    for i in range(HT):
                        inflow(j, *divmod(m, NST), i)
                    for behind, name in ((1, "gate"), (2, "ln")):
                        due = LINE[m - behind] if m >= behind else []
                        if m == STEPS - 1:
                            due = due + [piece for pieces in LINE[m - behind + 1:] for piece in pieces]
                        for piece in due:
                            if piece.startswith(name):
                                piece_of("body", j, piece)


NADAPT, LRANK = 8, 16
EXP, GROUPS, TOP_GROUPS, TOP = 16, 4, 2, 4
PER_GROUP = EXP // GROUPS
INNER = 352
SINNER = 2 * INNER
KI = -(-INNER // P)
KS = -(-SINNER // P)
SPAD = KS * P
TILES = TOK // P
SLOT_TILES = (TOK * TOP - EXP) // P + EXP
TURN = 8
SURE_TURNS = TOK * TOP // P // TURN
GROUP = 4
RUN_TILES = -(-SLOT_TILES // GROUP) * GROUP
GROUPS_MORE = range(SURE_TURNS * TURN, RUN_TILES, GROUP)
LISTS, YS, WSEMS = TURN, 4, 4
LAG = 3
TILES_AHEAD = LISTS - LAG
LIST_TILES = RUN_TILES + TILES_AHEAD


F32R = mybir.dt.float32r


def width(chunk, total):
    return min(P, total - chunk * P)


def hi_part(engine, hi, x):
    return engine.tensor_copy(hi, x)


def lo_part(engine, lo, x, hi):
    return engine.tensor_tensor(lo, x, hi.bitcast(F32), ALU.subtract)


def product(nc, out, lhs, rhs, first, last):
    (lhs_hi, lhs_lo), (rhs_hi, rhs_lo) = lhs, rhs
    nc.tensor.matmul(out, lhs_hi, rhs_hi, start=first, stop=False)
    nc.tensor.matmul(out, lhs_hi, rhs_lo, start=False, stop=False)
    return nc.tensor.matmul(out, lhs_lo, rhs_hi, start=False, stop=last)


RANKS = 24
ROUTE = {"top": [P, TB], "sc": [P, TB, EXP], "total": [P, TB], "rc": [P, TB], "g_top": [P, TB, GROUPS],
         "g_more": [P, TB, GROUPS, GROUPS], "g_tie": [P, TB, GROUPS, GROUPS], "g_rank": [P, TB, GROUPS],
         "e_more": [P, TB, EXP, EXP], "e_tie": [P, TB, EXP, EXP], "e_rank": [P, TB, EXP], "w_top": [P, TB, EXP],
         "tri_g": [P, GROUPS, GROUPS], "tri_e": [P, EXP, EXP]}


def rank(nc, dve, keep, j, logits):
    top, sc, total, rc, g_top, g_more, g_tie, g_rank, e_more, e_tie, e_rank, w_top, tri_g, tri_e, sel, cw = [
        keep[name] for name in (*ROUTE, "sel", "cw")]
    rank_step = keep["rank_step"]
    base = (j + 1) * RANKS
    done = 0

    def step(op):
        nonlocal done
        op.then_inc(rank_step, 1)
        done += 1
        dve.wait_ge(rank_step, base + done)

    def spread(x, n):
        return x.unsqueeze(2).broadcast_to([P, TB, n])

    step(nc.vector.tensor_reduce(top[:], logits[:], AX.X, ALU.max))
    step(nc.vector.tensor_tensor(sc[:], logits[:], spread(top[:], EXP), ALU.subtract))
    dve.wait_ge(keep["exp_done"], j + 1)
    step(nc.vector.tensor_reduce(total[:], sc[:], AX.X, ALU.add))
    step(nc.vector.reciprocal(rc[:], total[:]))
    step(nc.vector.tensor_tensor(sc[:], sc[:], spread(rc[:], EXP), ALU.mult))
    step(nc.vector.tensor_reduce(g_top[:], sc[:].rearrange("p t (g i) -> p t g i", g=GROUPS), AX.X, ALU.max))
    other = g_top[:].unsqueeze(2).broadcast_to([P, TB, GROUPS, GROUPS])
    own = g_top[:].unsqueeze(3).broadcast_to([P, TB, GROUPS, GROUPS])
    step(nc.vector.tensor_tensor(g_more[:], other, own, ALU.is_gt))
    step(nc.vector.tensor_tensor(g_tie[:], other, own, ALU.is_equal))
    step(nc.vector.tensor_tensor(g_tie[:], g_tie[:], tri_g[:].unsqueeze(1).broadcast_to([P, TB, GROUPS, GROUPS]), ALU.mult))
    step(nc.vector.tensor_tensor(g_more[:], g_more[:], g_tie[:], ALU.add))
    step(nc.vector.tensor_reduce(g_rank[:], g_more[:], AX.X, ALU.add))
    step(nc.vector.tensor_scalar(g_rank[:], g_rank[:], float(TOP_GROUPS), None, ALU.is_lt))
    step(nc.vector.tensor_tensor(sc[:].rearrange("p t (g i) -> p t g i", g=GROUPS),
                                 sc[:].rearrange("p t (g i) -> p t g i", g=GROUPS),
                                 g_rank[:].unsqueeze(3).broadcast_to([P, TB, GROUPS, PER_GROUP]), ALU.mult))
    other = sc[:].unsqueeze(2).broadcast_to([P, TB, EXP, EXP])
    own = sc[:].unsqueeze(3).broadcast_to([P, TB, EXP, EXP])
    step(nc.vector.tensor_tensor(e_more[:], other, own, ALU.is_gt))
    step(nc.vector.tensor_tensor(e_tie[:], other, own, ALU.is_equal))
    step(nc.vector.tensor_tensor(e_tie[:], e_tie[:], tri_e[:].unsqueeze(1).broadcast_to([P, TB, EXP, EXP]), ALU.mult))
    step(nc.vector.tensor_tensor(e_more[:], e_more[:], e_tie[:], ALU.add))
    step(nc.vector.tensor_reduce(e_rank[:], e_more[:], AX.X, ALU.add))
    chosen = sel[:, bass.ds(j * TB, TB), :]
    step(nc.vector.tensor_scalar(chosen, e_rank[:], float(TOP), None, ALU.is_lt))
    step(nc.vector.tensor_tensor(w_top[:], sc[:], chosen, ALU.mult))
    step(nc.vector.tensor_reduce(total[:], w_top[:], AX.X, ALU.add))
    step(nc.vector.tensor_scalar(total[:], total[:], 1e-20, None, ALU.add))
    step(nc.vector.reciprocal(rc[:], total[:]))
    step(nc.vector.tensor_tensor(cw[:, bass.ds(j * TB, TB), :], w_top[:], spread(rc[:], EXP), ALU.mult))
    assert done == RANKS


def exps(nc, act, keep, j):
    act.wait_ge(keep["rank_step"], (j + 1) * RANKS + 2)
    nc.scalar.activation(keep["sc"][:], keep["sc"][:], ACT.Exp).then_inc(keep["exp_done"], 1)


def mix(nc, keep, x1_d, adapter_ids, d, x2_d, x2T_d):
    ctx = ExitStack()

    def sb(name, shape, dt=F32):
        return ctx.enter_context(nc.sbuf_tensor(name, shape, dt))

    def ps(name, shape):
        return ctx.enter_context(nc.psum_tensor(name, shape, F32))

    def sem(name):
        return ctx.enter_context(nc.semaphore(name))

    ident, rank_step = keep["ident"], keep["rank_step"]
    w_T = sb("w_T", [P, KM, DM])
    a_T = sb("a_T", [P, KM, NADAPT * LRANK])
    b_T = sb("b_T", [NADAPT * LRANK, DM])
    gate_T = sb("gate_T", [P, KM, EXP])
    ids_i = sb("ids_i", [P, BATCH], I32)
    ids_f = sb("ids_f", [P, BATCH])
    row_scale = sb("row_scale", [P, 2])
    mask = sb("mask", [P, BATCH])
    x1_in = sb("x1_in", [P, TB, DM])
    x1T = sb("x1T", [P, KM, BLK])
    xam = sb("xam", [P, BLK])
    x2_sb = sb("x2_sb", [P, TB, DM])
    x2T = sb("x2T", [P, KM, BLK])
    lgT = sb("lgT", [EXP, BLK])
    zero_rows = sb("zero_rows", [P, DM])
    ahead = sb("ahead", [P, RING, 2 * SPAD])

    tr = [ps(f"tr{i}", [P, BLK]) for i in range(RING)]
    xa = ps("xa", [P, BLK])
    x2p = [ps(f"x2p{i}", [P, DM]) for i in range(RING)]
    lg = ps("lg", [EXP, BLK])
    lgt = ps("lgt", [P, TB, EXP])

    consts_in = sem("consts_in")
    w_in = sem("w_in")
    ahead_full = [sem(f"ahead_full{s}") for s in range(RING)]
    ahead_hi = sem("ahead_hi")
    ahead_lo = sem("ahead_lo")
    x1_full = sem("x1_full")
    zero_set = sem("zero_set")
    zero_stored = sem("zero_stored")
    mask_step = sem("mask_step")
    x1T_full = sem("x1T_full")
    x1T_out = sem("x1T_out")
    xa_full = sem("xa_full")
    xa_out = sem("xa_out")
    x2_full = sem("x2_full")
    x2_out = sem("x2_out")
    x2_stored = sem("x2_stored")
    x2T_stored = sem("x2T_stored")
    x2T_full = sem("x2T_full")
    x2T_out = sem("x2T_out")
    lg_full = sem("lg_full")
    lg_out = sem("lg_out")
    lgt_full = sem("lgt_full")
    logits_kept = sem("logits_kept")

    x1_blk = x1_d.rearrange("(k t p) f -> k p t f", t=TB, p=P)
    x2_blk = x2_d[0:TOK].rearrange("(k t p) f -> k p t f", t=TB, p=P)

    with ctx, nc.Block() as block:
        @block.sync
        def _(sp):
            def load_x1(j):
                sp.dma_start(x1_in[:], x1_blk[bass.ds(j + 1, 1)].rearrange("o p t f -> (o p) t f")).then_inc(x1_full, 16)

            load_x1(0)
            sp.dma_start(ident[:], d["ident"]).then_inc(consts_in, 16)
            sp.dma_start(ids_i[:], adapter_ids.broadcast_to([P, BATCH])).then_inc(consts_in, 16)
            sp.dma_start(row_scale[:], d["row_scale"]).then_inc(consts_in, 16)
            sp.dma_start(keep["tri_g"][:], d["tri_g"]).then_inc(consts_in, 16)
            sp.dma_start(keep["tri_e"][:], d["tri_e"]).then_inc(consts_in, 16)
            sp.dma_start(a_T[:], d["a_T"]).then_inc(w_in, 16)
            sp.dma_start(w_T[:], d["w_T"]).then_inc(w_in, 16)
            sp.dma_start(b_T[:], d["b_T"]).then_inc(w_in, 16)
            sp.dma_start(gate_T[:], d["gate_T"]).then_inc(w_in, 16)
            sp.wait_ge(zero_set, 1)
            sp.dma_start(x2_d[TOK:TOK + P], zero_rows[:]).then_inc(zero_stored, 16)
            with sp.Fori(0, NBLK - 1) as j:
                sp.wait_ge(x1T_full, KM * (j + 1))
                load_x1(j + 1)
                sp.wait_ge(x2_out, TB * (j + 1) + 1)
                sp.dma_start(x2_blk[bass.ds(j, 1)].rearrange("o p t f -> (o p) t f"), x2_sb[:]).then_inc(x2_stored, 16)
                sp.wait_ge(x2T_out, KM * (j + 1) + 1)
                sp.dma_start(x2T_d[bass.ds(j, 1)].rearrange("o p k l -> (o p) k l"), x2T[:]).then_inc(x2T_stored, 16)
            sp.wait_ge(x2_out, TB * NBLK + 1)
            sp.dma_start(x2_blk[NBLK - 1], x2_sb[:]).then_inc(x2_stored, 16)
            sp.wait_ge(x2T_out, KM * NBLK + 1)
            sp.dma_start(x2T_d[NBLK - 1], x2T[:]).then_inc(x2T_stored, 16)
            sp.wait_ge(x2_stored, 16 * NBLK)
            sp.wait_ge(x2T_stored, 16 * NBLK)
            sp.wait_ge(zero_stored, 16)

        @block.tensor
        def _(pe):
            pe.wait_ge(consts_in, 16 * 5)
            with pe.Fori(0, NBLK) as j:
                pe.wait_ge(x1_full, 16 * (j + 1))
                for k in range(KM):
                    if k < RING:
                        pe.wait_ge(x2T_out, KM * j + 1)
                    else:
                        pe.wait_ge(x1T_out, KM * j + k - RING + 1)
                    for t in range(TB):
                        mm = nc.tensor.transpose(tr[k % RING][:, t * P:(t + 1) * P], x1_in[:, t, k * P:(k + 1) * P], ident[:])
                    mm.then_inc(x1T_full, 1)
                pe.wait_ge(w_in, 64)
                for k in range(KM):
                    pe.wait_ge(x1T_out, KM * j + k + 1)
                    mm = nc.tensor.matmul(xa[:], a_T[:, k, :], x1T[:, k, :], start=(k == 0), stop=(k == KM - 1))
                mm.then_inc(xa_full, 1)
                for t in range(TB):
                    pe.wait_ge(x2_out, TB * j + (t - RING + 1 if t >= RING else 0) + 1)
                    for k in range(KM):
                        nc.tensor.matmul(x2p[t % RING][:], x1T[:, k, t * P:(t + 1) * P], w_T[:, k, :], start=(k == 0), stop=False)
                    pe.wait_ge(xa_out, j + 1)
                    nc.tensor.matmul(x2p[t % RING][:], xam[:, t * P:(t + 1) * P], b_T[:], start=False, stop=True) \
                        .then_inc(x2_full, 1)
                pe.wait_ge(x2_out, TB * (j + 1) + 1)
                for k in range(KM):
                    if k < RING:
                        pe.wait_ge(x1T_out, KM * (j + 1))
                    else:
                        pe.wait_ge(x2T_out, KM * j + k - RING + 2)
                    for t in range(TB):
                        mm = nc.tensor.transpose(tr[k % RING][:, t * P:(t + 1) * P], x2_sb[:, t, k * P:(k + 1) * P], ident[:])
                    mm.then_inc(x2T_full, 1)
                for k in range(KM):
                    pe.wait_ge(x2T_out, KM * j + k + 2)
                    mm = nc.tensor.matmul(lg[:], gate_T[:, k, :], x2T[:, k, :],
                                          start=(k == 0), stop=(k == KM - 1))
                mm.then_inc(lg_full, 1)
                pe.wait_ge(rank_step, j * RANKS + 2)
                pe.wait_ge(lg_out, j + 1)
                for t in range(TB):
                    mm = nc.tensor.matmul(lgt[:, t, :], lgT[:, t * P:(t + 1) * P], ident[0:EXP, 0:EXP], start=True, stop=True)
                mm.then_inc(lgt_full, 1)

        @block.scalar
        def _(act):
            def block_out(j, ranked):
                for k in range(KM):
                    act.wait_ge(x1T_full, KM * j + k + 1)
                    nc.scalar.copy(x1T[:, k, :], tr[k % RING][:]).then_inc(x1T_out, 1)
                for t in range(TB):
                    act.wait_ge(x2_full, TB * j + t + 1)
                    if t == 0:
                        act.wait_ge(x2_stored, 16 * j)
                    nc.scalar.copy(x2_sb[:, t, :], x2p[t % RING][:]).then_inc(x2_out, 1)
                    if t == 0 and ranked is not None:
                        exps(nc, act, keep, ranked)
                for k in range(KM):
                    act.wait_ge(x2T_full, KM * j + k + 1)
                    if k == 0:
                        act.wait_ge(x2T_stored, 16 * j)
                    nc.scalar.copy(x2T[:, k, :], tr[k % RING][:]).then_inc(x2T_out, 1)

            def logits_out(j):
                act.wait_ge(lg_full, j + 1)
                nc.scalar.copy(lgT[:], lg[:]).then_inc(lg_out, 1)

            act.sem_inc(x2_out, 1)
            act.sem_inc(x2T_out, 1)
            block_out(0, None)
            logits_out(0)
            with act.Fori(1, NBLK) as j:
                block_out(j, j - 1)
                logits_out(j)

        @block.vector
        def _(dve):
            def adapt(j):
                dve.wait_ge(xa_full, j + 1)
                nc.vector.tensor_tensor(xam[:].rearrange("p (b l) -> p b l", b=BB), xa[:].rearrange("p (b l) -> p b l", b=BB),
                                        mask[:, bass.ds(j * BB, BB)].unsqueeze(2).broadcast_to([P, BB, SEQ]),
                                        ALU.mult).then_inc(xa_out, 1)

            dve.sem_inc(rank_step, RANKS)
            nc.vector.memset(zero_rows[:], 0.0).then_inc(zero_set, 1)
            dve.wait_ge(consts_in, 16 * 5)
            nc.vector.tensor_copy(ids_f[:], ids_i[:]).then_inc(mask_step, 1)
            dve.wait_ge(mask_step, 1)
            nc.vector.tensor_scalar(mask[:], ids_f[:], row_scale[:, 0:1], row_scale[:, 1:2], ALU.is_equal, ALU.mult) \
                .then_inc(mask_step, 1)
            dve.wait_ge(mask_step, 2)
            adapt(0)
            with dve.Fori(1, NBLK) as j:
                adapt(j)
                dve.wait_ge(lgt_full, j)
                rank(nc, dve, keep, j - 1, lgt)
            dve.wait_ge(lgt_full, NBLK)
            nc.vector.tensor_copy(keep["last_logits"][:], lgt[:]).then_inc(logits_kept, 1)
            dve.wait_ge(logits_kept, 1)

        @block.gpsimd
        def _(pool):
            sup_hi, sup_lo, sdn_hi, sdn_lo = [keep[name] for name in ("sup_hi", "sup_lo", "sdn_hi", "sdn_lo")]
            pieces = [(d["sup_T"][:, k, :], sup_hi[:, k, :], sup_lo[:, k, :]) for k in range(KM)]
            pieces += [[x.rearrange("p k f -> p (k f)") for x in (d["sdn_T"][:, at, :], sdn_hi[:, at, :], sdn_lo[:, at, :])]
                       for at in (slice(0, KS // 2), slice(KS // 2, KS))]

            def load(i):
                nc.gpsimd.dma_start(ahead[:, i % RING, :], pieces[i][0]).then_inc(ahead_full[i % RING], 16)

            load(0)
            for i, (_, hi, lo) in enumerate(pieces):
                if i:
                    pool.wait_ge(ahead_lo, i)
                if i + 1 < len(pieces):
                    load(i + 1)
                pool.wait_ge(ahead_full[i % RING], 16 * (i // RING + 1))
                hi_part(nc.gpsimd, hi, ahead[:, i % RING, :]).then_inc(ahead_hi, 1)
                pool.wait_ge(ahead_hi, i + 1)
                lo_part(nc.gpsimd, lo, ahead[:, i % RING, :], hi).then_inc(ahead_lo, 1)
            pool.wait_ge(ahead_lo, len(pieces))


def shared(nc, keep, x1_d, x2T_d, d, list_d, out_d):
    ctx = ExitStack()

    def sb(name, shape, dt=F32):
        return ctx.enter_context(nc.sbuf_tensor(name, shape, dt))

    def ps(name, shape):
        return ctx.enter_context(nc.psum_tensor(name, shape, F32))

    def sem(name):
        return ctx.enter_context(nc.semaphore(name))

    sel, cw, table = keep["sel"], keep["cw"], keep["table"]
    sup_hi, sup_lo, sdn_hi, sdn_lo = keep["sup_hi"], keep["sup_lo"], keep["sdn_hi"], keep["sdn_lo"]
    x2T = sb("x2T_in", [P, KM, BLK])
    x2_hi = sb("x2_hi", [P, KM, BLK], F32R)
    x2_lo = sb("x2_lo", [P, KM, BLK], F32R)
    res = sb("res2", [P, TB, DM])
    gs = sb("sgs", [P, RING, BLK])
    a = sb("sa", [P, BLK])
    a_hi = sb("sa_hi", [P, KS, BLK], F32R)
    a_lo = sb("sa_lo", [P, KS, BLK], F32R)
    pad_list = sb("pad_list", [P, LIST_TILES, 2], I32)
    pad_rows = sb("pad_rows", [P, DM])
    tokens = sb("tokens", [P, TILES], I32)
    strict = sb("strict", [P, P])
    ones = sb("ones", [P, P])
    restart = sb("restart", [P, EXP, TILES])
    steps = sb("steps", [P, TILES])
    numbers = sb("numbers", [1, LIST_TILES])
    before = sb("before", [P, EXP, TILES])
    upto = sb("upto", [P, EXP, TILES])
    more = sb("more", [P, EXP, TILES])
    tiles = sb("tiles", [P, EXP])
    ends = sb("ends", [P, EXP])
    starts = sb("starts", [P, EXP])
    place = sb("place", [P, TILES, EXP])
    best = sb("best", [P, TILES, 8])
    match = sb("match", [P, TILES, TOP, EXP])
    pairs = sb("pairs", [P, TILES, TOP, 2], I32)
    slot_i = sb("slot_i", [P, TILES, TOP], I32)
    t_cmp = sb("t_cmp", [1, LIST_TILES, EXP])
    t_exp = sb("t_exp", [1, 1 + LIST_TILES])
    t_new = sb("t_new", [1, LIST_TILES])
    t_before = sb("t_before", [1, LIST_TILES])
    t_first = sb("t_first", [1, 1 + LIST_TILES])
    t_tmp = sb("t_tmp", [1, LIST_TILES])

    gp = [ps(f"gp{i}", [P, BLK]) for i in range(RING)]
    up = [ps(f"up{i}", [P, BLK]) for i in range(RING)]
    yp = [ps(f"yp{i}", [P, DM]) for i in range(RING)]
    within = ps("within", [P, TILES, EXP])
    totals = ps("totals", [P, TILES, EXP])

    consts2 = sem("consts2")
    res_full = sem("res2_full")
    out_stored = sem("out_stored")
    pads_stored = sem("pads_stored")
    pads_set = sem("pads_set")
    g_full = sem("g_full")
    u_full = sem("u_full")
    silu_done = sem("silu_done")
    x2_full = sem("sx2_full")
    x2_split = sem("x2_split")
    x2_parts = sem("x2_parts")
    a_done = sem("a_done")
    a_split = sem("a_split")
    a_parts = sem("a_parts")
    y_full = sem("y_full")
    y_out = sem("y_out")
    counts_full = sem("counts_full")
    slot_step = sem("slot_step")
    slots_ready = sem("slots_ready")
    listed = sem("listed")

    x1_blk = x1_d.rearrange("(k t p) f -> k p t f", t=TB, p=P)
    out_blk = out_d[0:TOK].rearrange("(k t p) f -> k p t f", t=TB, p=P)
    list_rows = list_d.rearrange("(i p) c -> p i c", p=P)
    N_CONST = 7

    with ctx, nc.Block() as block:
        @block.sync
        def _(sp):
            def load_x2(j):
                sp.dma_start(x2T[:], x2T_d[bass.ds(j, 1)].rearrange("o p k l -> (o p) k l")).then_inc(x2_full, 16)

            load_x2(0)
            sp.dma_start(pad_list[:], d["pad_list"]).then_inc(consts2, 16)
            sp.dma_start(tokens[:], d["tokens"]).then_inc(consts2, 16)
            sp.dma_start(strict[:], d["strict"]).then_inc(consts2, 16)
            sp.dma_start(ones[:], d["ones"]).then_inc(consts2, 16)
            sp.dma_start(restart[:], d["restart"]).then_inc(consts2, 16)
            sp.dma_start(steps[:], d["steps"]).then_inc(consts2, 16)
            sp.dma_start(numbers[:], d["numbers"]).then_inc(consts2, 16)
            sp.wait_ge(consts2, 16 * N_CONST)
            sp.dma_start(list_rows, pad_list[:]).then_inc(pads_stored, 16)
            sp.wait_ge(pads_set, 1)
            sp.dma_start(out_d[TOK:TOK + P], pad_rows[:]).then_inc(pads_stored, 16)
            sp.sem_inc(out_stored, 16)

            def block_io(j, last=False):
                sp.wait_ge(out_stored, 16 * (j + 1))
                sp.dma_start(res[:], x1_blk[bass.ds(j + 1, 1)].rearrange("o p t f -> (o p) t f")).then_inc(res_full, 16)
                if not last:
                    sp.wait_ge(x2_parts, j + 1)
                    load_x2(j + 1)
                sp.wait_ge(y_out, TB * (j + 1))
                sp.dma_start(out_blk[bass.ds(j, 1)].rearrange("o p t f -> (o p) t f"), res[:]).then_inc(out_stored, 16)

            with sp.Fori(0, NBLK - 1) as j:
                block_io(j)
            block_io(NBLK - 1, last=True)
            sp.wait_ge(out_stored, 16 * (NBLK + 1))
            sp.wait_ge(pads_stored, 32)

        @block.tensor
        def _(pe):
            def expert(j):
                for f in range(KS):
                    at = j * KS + f
                    if f >= RING:
                        pe.wait_ge(a_done, at - RING + 1)
                    else:
                        pe.wait_ge(a_done, j * KS)
                    if f == 0:
                        pe.wait_ge(x2_parts, j + 1)
                    for half, bank, full in ((0, gp, g_full), (1, up, u_full)):
                        at_f = slice(half * SPAD + f * P, half * SPAD + (f + 1) * P)
                        for k in range(KM):
                            mm = product(nc, bank[f % RING][:], [part[:, k, at_f] for part in (sup_hi, sup_lo)],
                                         [x2_hi[:, k, :], x2_lo[:, k, :]], k == 0, k == KM - 1)
                        mm.then_inc(full, 1)
                for t in range(TB):
                    pe.wait_ge(y_out, j * TB + (t - RING + 1 if t >= RING else 0))
                    for f in range(KS):
                        if t == 0:
                            pe.wait_ge(a_parts, j * KS + f + 1)
                        mm = product(nc, yp[t % RING][:], [part[:, f, t * P:(t + 1) * P] for part in (a_hi, a_lo)],
                                     [part[:, f, :] for part in (sdn_hi, sdn_lo)], f == 0, f == KS - 1)
                    mm.then_inc(y_full, 1)

            expert(0)
            expert(1)
            pe.wait_ge(consts2, 16 * N_CONST)
            pe.wait_ge(keep["rank_step"], (NBLK + 1) * RANKS)
            nc.tensor.matmul(within[:], strict[:], sel[:], start=True, stop=True).then_inc(counts_full, 1)
            nc.tensor.matmul(totals[:], ones[:], sel[:], start=True, stop=True).then_inc(counts_full, 1)
            with pe.Fori(2, NBLK) as j:
                expert(j)

        @block.scalar
        def _(act):
            def expert(j):
                for f in range(KS):
                    at = j * KS + f
                    act.wait_ge(g_full, at + 1)
                    if f >= RING:
                        act.wait_ge(a_done, at - RING + 1)
                    else:
                        act.wait_ge(a_done, j * KS)
                    nc.scalar.activation(gs[:, f % RING, :], gp[f % RING][:], ACT.Silu).then_inc(silu_done, 1)

            expert(0)
            exps(nc, act, keep, NBLK - 1)
            with act.Fori(1, NBLK) as j:
                expert(j)

        @block.vector
        def _(dve):
            def split_x2(j):
                dve.wait_ge(x2_full, 16 * (j + 1))
                hi_part(nc.vector, x2_hi[:], x2T[:]).then_inc(x2_split, 1)
                dve.wait_ge(x2_split, j + 1)
                lo_part(nc.vector, x2_lo[:], x2T[:], x2_hi[:]).then_inc(x2_parts, 1)

            def expert(j, last=False):
                for f in range(KS):
                    at = j * KS + f
                    dve.wait_ge(silu_done, at + 1)
                    dve.wait_ge(u_full, at + 1)
                    if f or not isinstance(j, int) or j:
                        dve.wait_ge(a_parts, at)
                    nc.vector.tensor_tensor(a[:], gs[:, f % RING, :], up[f % RING][:], ALU.mult).then_inc(a_done, 1)
                    dve.wait_ge(a_done, at + 1)
                    hi_part(nc.vector, a_hi[:, f, :], a[:]).then_inc(a_split, 1)
                    dve.wait_ge(a_split, at + 1)
                    lo_part(nc.vector, a_lo[:, f, :], a[:], a_hi[:, f, :]).then_inc(a_parts, 1)
                if not last:
                    split_x2(j + 1)
                dve.wait_ge(res_full, 16 * (j + 1))
                for t in range(TB):
                    dve.wait_ge(y_full, j * TB + t + 1)
                    nc.vector.tensor_tensor(res[:, t, :], yp[t % RING][:], res[:, t, :], ALU.add).then_inc(y_out, 1)

            done = 0

            def step(op):
                nonlocal done
                op.then_inc(slot_step, 1)
                done += 1
                dve.wait_ge(slot_step, done)

            def slots():
                dve.wait_ge(consts2, 16 * N_CONST)
                dve.wait_ge(counts_full, 2)
                by_expert = totals[:].rearrange("p t e -> p e t")
                step(nc.vector.tensor_copy(before[:], by_expert))
                step(nc.vector.tensor_tensor_scan(upto[:].rearrange("p e t -> p (e t)"), restart[:].rearrange("p e t -> p (e t)"),
                                                  before[:].rearrange("p e t -> p (e t)"), 0.0, ALU.mult, ALU.add))
                step(nc.vector.tensor_tensor(before[:], upto[:], before[:], ALU.subtract))
                step(nc.vector.tensor_tensor(more[:], upto[:, :, TILES - 1:TILES].broadcast_to([P, EXP, TILES]),
                                             steps[:].unsqueeze(1).broadcast_to([P, EXP, TILES]), ALU.is_gt))
                step(nc.vector.tensor_reduce(tiles[:], more[:], AX.X, ALU.add))
                step(nc.vector.tensor_tensor_scan(ends[:], ones[:, 0:EXP], tiles[:], 0.0, ALU.mult, ALU.add))
                step(nc.vector.tensor_tensor(starts[:], ends[:], tiles[:], ALU.subtract))
                step(nc.vector.tensor_tensor(place[:], within[:], before[:].rearrange("p e t -> p t e"), ALU.add))
                step(nc.vector.scalar_tensor_tensor(out=place[:], in0=starts[:].unsqueeze(1).broadcast_to([P, TILES, EXP]),
                                                    scalar=float(P), in1=place[:], op0=ALU.mult, op1=ALU.add))
                step(nc.vector.scalar_tensor_tensor(out=place[:], in0=place[:], scalar=1.0, in1=sel[:],
                                                    op0=ALU.add, op1=ALU.mult))
                for t in range(TILES):
                    step(nc.vector.max(best[:, t, :], place[:, t, :]))
                step(nc.vector.tensor_tensor(match[:], place[:].unsqueeze(2).broadcast_to([P, TILES, TOP, EXP]),
                                             best[:, :, 0:TOP].unsqueeze(3).broadcast_to([P, TILES, TOP, EXP]), ALU.is_equal))
                step(nc.vector.tensor_tensor(match[:], match[:], cw[:].unsqueeze(2).broadcast_to([P, TILES, TOP, EXP]), ALU.mult))
                step(nc.vector.tensor_reduce(pairs[:, :, :, 1].bitcast(F32), match[:], AX.X, ALU.add))
                step(nc.vector.tensor_copy(pairs[:, :, :, 0], tokens[:].unsqueeze(2).broadcast_to([P, TILES, TOP])))
                nc.vector.tensor_scalar(slot_i[:], best[:, :, 0:TOP], -1.0, None, ALU.add).then_inc(slots_ready, 1)

            def slot_tiles():
                step(nc.vector.tensor_tensor(t_cmp[:], ends[0:1, :].unsqueeze(1).broadcast_to([1, LIST_TILES, EXP]),
                                             numbers[:].unsqueeze(2).broadcast_to([1, LIST_TILES, EXP]), ALU.is_le))
                step(nc.vector.memset(t_exp[:, 0:1], -1.0))
                step(nc.vector.tensor_reduce(t_exp[:, 1:], t_cmp[:], AX.X, ALU.add))
                step(nc.vector.tensor_scalar(t_exp[:, 1:], t_exp[:, 1:], float(EXP - 1), None, ALU.min))
                step(nc.vector.tensor_tensor(t_new[:], t_exp[:, 1:], t_exp[:, 0:LIST_TILES], ALU.not_equal))
                step(nc.vector.tensor_tensor(t_tmp[:], t_new[:], numbers[:], ALU.mult))
                step(nc.vector.memset(t_first[:, 0:1], 0.0))
                step(nc.vector.tensor_tensor_scan(t_first[:, 1:], ones[0:1, 0:LIST_TILES], t_tmp[:], 0.0, ALU.mult, ALU.max))
                step(nc.vector.tensor_tensor(t_tmp[:], t_new[:], t_first[:, 0:LIST_TILES], ALU.mult))
                step(nc.vector.tensor_tensor_scan(t_before[:], ones[0:1, 0:LIST_TILES], t_tmp[:], 0.0, ALU.mult, ALU.max))
                step(nc.vector.tensor_copy(table[:, 0, :], t_exp[:, 1:]))
                step(nc.vector.tensor_copy(table[:, 1, :], t_new[:]))
                step(nc.vector.tensor_copy(table[:, 3, :], t_before[:]))
                step(nc.vector.tensor_tensor(table[:, 4, :], numbers[:], ends[0:1, EXP - 1:EXP].broadcast_to([1, LIST_TILES]),
                                             ALU.is_lt))
                step(nc.vector.tensor_tensor_scan(table[:, 2, :], ones[0:1, 0:LIST_TILES], t_new[:], 0.0, ALU.mult, ALU.add))
                step(nc.vector.memset(table[:, 5, 0:GROUP], 0))
                step(nc.vector.tensor_tensor(table[:, 5, GROUP:], table[:, 4, 0:LIST_TILES - GROUP], table[:, 4, GROUP:],
                                             ALU.subtract))

            nc.vector.memset(pad_rows[:], 0.0).then_inc(pads_set, 1)
            split_x2(0)
            expert(0)
            rank(nc, dve, keep, NBLK - 1, keep["last_logits"])
            expert(1)
            slots()
            for j in range(2, NBLK):
                expert(j, last=j == NBLK - 1)
                if j == 2:
                    slot_tiles()

        @block.gpsimd
        def _(pool):
            pool.wait_ge(pads_stored, 32)
            pool.wait_ge(slots_ready, 1)
            for t in range(TILES):
                for k in range(TOP):
                    nc.gpsimd.indirect_dma_start(
                        out=list_d, out_offset=bass.IndirectOffsetOnAxis(ap=slot_i[:, t, k:k + 1], axis=0),
                        in_=pairs[:, t, k, :], in_offset=None).then_inc(listed, 16)
            pool.wait_ge(listed, 16 * TILES * TOP)


def experts(nc, keep, up_d, dn_d, x2_d, list_d, out_d):
    ctx = ExitStack()

    def sb(name, shape, dt=F32):
        return ctx.enter_context(nc.sbuf_tensor(name, shape, dt))

    def ps(name, shape):
        return ctx.enter_context(nc.psum_tensor(name, shape, F32))

    def sem(name):
        return ctx.enter_context(nc.semaphore(name))

    ident, table = keep["ident"], keep["table"]
    w_up = sb("w_up", [P, KM, 2 * INNER])
    w_dn = sb("w_dn", [P, KI, DM])
    w_up_hi = sb("w_up_hi", [P, RING, KM, 2 * INNER], F32R)
    w_up_lo = sb("w_up_lo", [P, RING, KM, 2 * INNER], F32R)
    w_dn_hi = sb("w_dn_hi", [P, RING, KI, DM], F32R)
    w_dn_lo = sb("w_dn_lo", [P, RING, KI, DM], F32R)
    slots = sb("slots", [P, LISTS, 2], I32)
    xg = sb("xg", [P, RING, DM])
    xT_hi = sb("xT_hi", [P, RING, DM], F32R)
    xT_lo = sb("xT_lo", [P, RING, DM], F32R)
    gs = sb("gs", [P, RING, INNER])
    a = sb("a", [P, RING, INNER])
    aT_hi = sb("aT_hi", [P, RING, KI * P], F32R)
    aT_lo = sb("aT_lo", [P, RING, KI * P], F32R)
    y = sb("y", [P, YS, DM])

    xT_ps = ps("xT_ps", [P, DM])
    gp = [ps(f"egp{i}", [P, INNER]) for i in range(RING)]
    up = [ps(f"eup{i}", [P, INNER]) for i in range(RING)]
    aT_ps = ps("aT_ps", [P, KI * P])
    yp = [ps(f"eyp{i}", [P, DM]) for i in range(RING)]

    w_full = [sem(f"w_full{s}") for s in range(WSEMS)]
    slots_full = [sem(f"slots_full{s}") for s in range(LISTS)]
    xg_full = [sem(f"xg_full{s}") for s in range(RING)]
    gate_split = sem("gate_split")
    up_split = sem("up_split")
    dn_split = sem("dn_split")
    gate_ready = sem("gate_ready")
    up_ready = sem("up_ready")
    dn_ready = sem("dn_ready")
    y_zero = sem("y_zero")
    gathers = sem("gathers")
    scatters = sem("scatters")
    added = sem("added")
    xT_full = sem("xT_full")
    xT_split = sem("xT_split")
    xT_out = sem("xT_out")
    up_full = sem("up_full")
    silu_done = sem("esilu_done")
    a_done = sem("ea_done")
    aT_full = sem("aT_full")
    aT_split = sem("aT_split")
    aT_out = sem("aT_out")
    y_full = sem("ey_full")
    y_out = sem("ey_out")
    Y0 = RING + 1

    list_tiles = list_d.rearrange("(i p) c -> i p c", p=P)

    def slot_of(run):
        return bass.ds((run + 1) % RING, 1)

    def weights(j, r):
        return w_full[r % WSEMS], j * (32 * TURN // WSEMS) + 32 * (r // WSEMS + 1)

    def run_tiles(engine, tile, last_steps=None):
        counts = [*GROUPS_MORE, RUN_TILES] if last_steps else []
        filled, ended = [[engine.value_load(table[0:1, row, at:at + 1], min_val=0, max_val=1) for at in tiles]
                         for row, tiles in ((4, GROUPS_MORE), (5, counts))]
        with engine.Fori(0, SURE_TURNS) as j:
            for r in range(TURN):
                tile(j, r)
        for first, group_filled in zip(GROUPS_MORE, filled):
            with engine.If(group_filled):
                for i in range(first, first + GROUP):
                    tile(i // TURN, i % TURN)
        for count, ended_here in zip(counts, ended):
            with engine.If(ended_here):
                last_steps(count)

    with ctx, nc.Block() as block:
        @block.sync
        def _(sp):
            def load_slots(i, r):
                sp.dma_start(slots[:, r % LISTS, :], list_tiles[bass.ds(i, 1)].rearrange("o p c -> (o p) c")) \
                    .then_inc(slots_full[r % LISTS], 16)

            def load_weights(i, r):
                at = bass.ds(i, 1)
                expert = sp.value_load(table[0:1, 0, at], min_val=0, max_val=EXP - 1)
                starts = sp.value_load(table[0:1, 1, at], min_val=0, max_val=1)
                run = sp.value_load(table[0:1, 2, at], min_val=1, max_val=EXP)
                for ready in (gate_ready, up_ready, dn_ready):
                    sp.wait_ge(ready, run)
                sp.dma_start(w_up[:], up_d[bass.ds(expert, 1)].rearrange("o p k f -> (o p) k f"), cond=starts) \
                    .then_inc(w_full[r % WSEMS], 16)
                sp.dma_start(w_dn[:], dn_d[bass.ds(expert, 1)].rearrange("o p k f -> (o p) k f"), cond=starts) \
                    .then_inc(w_full[r % WSEMS], 16)

            for r in range(TILES_AHEAD, LISTS):
                load_slots(RUN_TILES + r - TILES_AHEAD, r)
            for r in range(TILES_AHEAD):
                load_slots(r, r)
            for r in range(WSEMS):
                load_weights(r, r)

            def tile(j, r):
                i = j * TURN + r
                sp.wait_ge(added, 16 * (i + 2))
                load_slots(i + TILES_AHEAD, r + TILES_AHEAD)
                sp.wait_ge(up_full, i + 1)
                load_weights(i + WSEMS, r + WSEMS)

            def last_steps(count):
                sp.wait_ge(added, 16 * (count + LAG + 1))
                for r in range(WSEMS):
                    sp.wait_ge(w_full[r], 32 * (count // WSEMS + 1))
                for r in range(LISTS):
                    loads = sum(i % LISTS == r for i in range(-LAG, count + TILES_AHEAD))
                    sp.wait_ge(slots_full[r], 16 * loads)

            run_tiles(sp, tile, last_steps)

        @block.tensor
        def _(pe):
            def x_turned(s, gathered, before):
                pe.wait_ge(xg_full[s], 16 * gathered)
                if before is not None:
                    pe.wait_ge(xT_out, before)
                for k in range(KM):
                    mm = nc.tensor.transpose(xT_ps[:, k * P:(k + 1) * P], xg[:, s, k * P:(k + 1) * P], ident[:])
                mm.then_inc(xT_full, 1)

            def run_of(i):
                return pe.value_load(table[0:1, 2, bass.ds(i, 1)], min_val=1, max_val=EXP)

            def go_up(i, s, run):
                slot = slot_of(run)
                pe.wait_ge(xT_out, i + 1)
                for half, bank, ready in ((0, gp, gate_ready), (1, up, up_ready)):
                    pe.wait_ge(ready, run + 1)
                    for k in range(KM):
                        x = [part[:, s, k * P:(k + 1) * P] for part in (xT_hi, xT_lo)]
                        w = [part[:, slot, k, half * INNER:(half + 1) * INNER].rearrange("p o f -> p (o f)")
                             for part in (w_up_hi, w_up_lo)]
                        mm = product(nc, bank[s][:], x, w, k == 0, k == KM - 1)
                mm.then_inc(up_full, 1)

            def a_turned(i, s):
                pe.wait_ge(a_done, i + 2)
                pe.wait_ge(aT_out, i + 1)
                for c in range(KI):
                    n = width(c, INNER)
                    mm = nc.tensor.transpose(aT_ps[0:n, c * P:(c + 1) * P], a[:, s, c * P:c * P + n], ident[:])
                mm.then_inc(aT_full, 1)

            def go_down(i, s, run):
                slot = slot_of(run)
                pe.wait_ge(y_out, i + 1 + Y0 - RING)
                pe.wait_ge(dn_ready, run + 1)
                pe.wait_ge(aT_out, i + 2)
                for c in range(KI):
                    n = width(c, INNER)
                    a_c = [part[0:n, s, c * P:(c + 1) * P] for part in (aT_hi, aT_lo)]
                    w = [part[0:n, slot, c, :].rearrange("p o f -> p (o f)") for part in (w_dn_hi, w_dn_lo)]
                    mm = product(nc, yp[s][:], a_c, w, c == 0, c == KI - 1)
                mm.then_inc(y_full, 1)

            pe.sem_inc(y_full, 1)
            x_turned(0, 1, None)
            x_turned(1, 1, 1)
            go_up(0, 0, run_of(0))
            runs = {}

            def tile(j, r):
                i = j * TURN + r
                s = r % RING
                runs[r + 1] = run_of(i + 1)
                a_turned(i, s)
                x_turned(s, j * (TURN // RING) + r // RING + 2, i + 2)
                pe.wait_ge(*weights(j, r + 1))
                pe.wait_ge(silu_done, i + 1)
                pe.wait_ge(a_done, i + 1)
                go_up(i + 1, (r + 1) % RING, runs[r + 1])
                if r == 0 or isinstance(i, int) and r % GROUP == 0:
                    runs[r] = run_of(i)
                go_down(i, s, runs[r])

            run_tiles(pe, tile)

        @block.scalar
        def _(act):
            def silu(i, s):
                act.wait_ge(up_full, i + 1)
                if not isinstance(i, int) or i:
                    act.wait_ge(a_done, i)
                nc.scalar.activation(gs[:, s, :], gp[s][:], ACT.Silu).then_inc(silu_done, 1)

            act.sem_inc(y_out, Y0)
            act.sem_inc(silu_done, 1)
            silu(0, 0)

            def tile(j, r):
                i = j * TURN + r
                silu(i + 1, (r + 1) % RING)
                act.wait_ge(y_full, i + 2)
                act.wait_ge(added, 16 * (i + 1))
                nc.scalar.mul(y[:, r % YS, :], yp[r % RING][:], slots[:, r, 1:2].bitcast(F32)).then_inc(y_out, 1)

            run_tiles(act, tile)

        @block.vector
        def _(dve):
            def x_out(i, s):
                dve.wait_ge(xT_full, i + 1)
                hi_part(nc.vector, xT_hi[:, s, :], xT_ps[:]).then_inc(xT_split, 1)
                dve.wait_ge(xT_split, i + 1)
                lo_part(nc.vector, xT_lo[:, s, :], xT_ps[:], xT_hi[:, s, :]).then_inc(xT_out, 1)

            def a_out(i, s):
                dve.wait_ge(aT_full, i + 1)
                chunks = [(P, slice(0, (KI - 1) * P)), (width(KI - 1, INNER), slice((KI - 1) * P, KI * P))]
                for n, at in chunks:
                    mask = hi_part(nc.vector, aT_hi[0:n, s, at], aT_ps[0:n, at])
                mask.then_inc(aT_split, 1)
                dve.wait_ge(aT_split, i + 1)
                for n, at in chunks:
                    less = lo_part(nc.vector, aT_lo[0:n, s, at], aT_ps[0:n, at], aT_hi[0:n, s, at])
                less.then_inc(aT_out, 1)

            def weight_parts(i):
                run = dve.value_load(table[0:1, 2, bass.ds(i, 1)], min_val=1, max_val=EXP)
                last_run = dve.value_load(table[0:1, 3, bass.ds(i, 1)], min_val=0, max_val=LIST_TILES)
                slot = slot_of(run)
                gate, up_w = [[part[:, :, half * INNER:(half + 1) * INNER] for part in (
                    w_up, *(ring[:, slot].rearrange("p o k f -> p (o k) f") for ring in (w_up_hi, w_up_lo)))]
                    for half in range(2)]
                dn = [w_dn[:], *(ring[:, slot].rearrange("p o k f -> p (o k) f") for ring in (w_dn_hi, w_dn_lo))]
                return run, last_run, gate, up_w, dn

            def upper_weights(parts, loaded):
                run, last_run, gate, up_w, dn = parts
                dve.wait_ge(*loaded)
                dve.wait_ge(y_full, last_run + 1)
                for (whole, hi, lo), split in ((gate, gate_split), (up_w, up_split), (dn, dn_split)):
                    hi_part(nc.vector, hi, whole).then_inc(split, 1)

            def lower_weights(parts):
                run, last_run, gate, up_w, dn = parts
                for (whole, hi, lo), split, ready in ((up_w, up_split, up_ready), (dn, dn_split, dn_ready)):
                    dve.wait_ge(split, run)
                    lo_part(nc.vector, lo, whole, hi).then_inc(ready, 1)

            def starts(i):
                return dve.value_load(table[0:1, 1, bass.ds(i, 1)], min_val=0, max_val=1)

            def swiglu(i, s):
                dve.wait_ge(silu_done, i + 2)
                nc.vector.tensor_tensor(a[:, s, :], gs[:, s, :], up[s][:], ALU.mult).then_inc(a_done, 1)

            dve.sem_inc(a_done, 1)
            dve.sem_inc(aT_out, 1)
            dve.sem_inc(up_ready, 1)
            dve.sem_inc(dn_ready, 1)
            for s in range(YS - LAG, YS):
                nc.vector.memset(y[:, s, :], 0.0).then_inc(y_zero, 1)
            x_out(0, 0)
            x_out(1, 1)
            upper_weights(weight_parts(0), (w_full[0], 32))
            lower_weights(weight_parts(0))
            run_starts, parts = starts(1), weight_parts(1)
            with dve.If(run_starts):
                upper_weights(parts, (w_full[1], 32))
            swiglu(0, 0)
            with dve.If(run_starts):
                lower_weights(parts)

            def tile(j, r):
                i = j * TURN + r
                s = r % RING
                run_starts, parts = starts(i + 2), weight_parts(i + 2)
                a_out(i, s)
                x_out(i + 2, s)
                with dve.If(run_starts):
                    upper_weights(parts, weights(j, r + 2))
                swiglu(i + 1, (r + 1) % RING)
                with dve.If(run_starts):
                    lower_weights(parts)

            run_tiles(dve, tile)

        @block.gpsimd
        def _(pool):
            def gather(s, r, loaded, turned):
                pool.wait_ge(slots_full[r], loaded)
                if turned is not None:
                    pool.wait_ge(xT_full, turned)
                pool.sem_inc(gathers, 1)
                nc.gpsimd.indirect_dma_start(out=xg[:, s, :], out_offset=None, in_=x2_d,
                                             in_offset=bass.IndirectOffsetOnAxis(ap=slots[:, r, 0:1], axis=0)) \
                    .then_inc(xg_full[s], 16)

            def split_gate(i):
                run = pool.value_load(table[0:1, 2, bass.ds(i, 1)], min_val=1, max_val=EXP)
                slot = slot_of(run)
                hi, lo = [part[:, slot, :, 0:INNER].rearrange("p o k f -> p (o k) f") for part in (w_up_hi, w_up_lo)]
                pool.wait_ge(gate_split, run)
                lo_part(nc.gpsimd, lo, w_up[:, :, 0:INNER], hi).then_inc(gate_ready, 1)

            def add_rows(r):
                nc.gpsimd.indirect_dma_start(out=out_d, out_offset=bass.IndirectOffsetOnAxis(ap=slots[:, r % LISTS, 0:1], axis=0),
                                             in_=y[:, r % YS, :], in_offset=None, compute_op=ALU.add).then_inc(added, 16)

            def add(i, r):
                pool.wait_ge(y_out, i + Y0 - LAG + 1)
                pool.wait_ge(added, i * 16 + 16)
                pool.sem_inc(scatters, 1)
                add_rows(r)

            pool.sem_inc(gate_ready, 1)
            pool.wait_ge(y_zero, LAG)
            for r in range(TILES_AHEAD, LISTS):
                pool.wait_ge(slots_full[r], 16)
            add_rows(LISTS - 1)
            for s in range(RING):
                gather(s, s, 16, None)

            def tile(j, r):
                i = j * TURN + r
                ahead = r + RING
                loads = 1 + ahead // LISTS + (1 if ahead % LISTS >= TILES_AHEAD else 0)
                gather(r % RING, ahead % LISTS, 16 * (j + loads), i + 1)
                starts = pool.value_load(table[0:1, 1, bass.ds(i, 1)], min_val=0, max_val=1)
                with pool.If(starts):
                    split_gate(i)
                add(i, r + TILES_AHEAD)

            def last_steps(count):
                for i in range(count, count + LAG):
                    add(i, i % LISTS + TILES_AHEAD)

            run_tiles(pool, tile, last_steps)


def layer(nc, d, out_d):
    bt_d = nc.dram_tensor("bt_scratch", [NBLK + 1, NST, BLK], F32, kind="Internal").ap()
    rows_d = nc.dram_tensor("rows_scratch", [ROWS, SEQ * SEQ + SEQ], F32, kind="Internal").ap()
    x1_d = nc.dram_tensor("x1_scratch", [BLK + TOK, DM], F32, kind="Internal").ap()
    x2_d = nc.dram_tensor("x2_scratch", [TOK + P, DM], F32, kind="Internal").ap()
    x2T_d = nc.dram_tensor("x2T_scratch", [NBLK, P, KM, BLK], F32, kind="Internal").ap()
    list_d = nc.dram_tensor("list_scratch", [LIST_TILES * P, 2], I32, kind="Internal").ap()
    with ExitStack() as ctx:
        mamba(nc, ctx, d["x_pad"], d["subjects"], d["cond_w"], d["cond_b"], rows_d, d["in_T"], d["xp_T"], d["dt_T"], d["out_T"], d["chan"],
              d["ident"], bt_d, x1_d)
    with ExitStack() as ctx:
        def held(ctx, shapes):
            return {name: ctx.enter_context(nc.sbuf_tensor(name + "_kept", shape, dt)) for name, shape, dt in shapes}

        keep = held(ctx, (("ident", [P, P], F32), ("table", [1, 6, LIST_TILES], I32)))
        with ExitStack() as ffn_ctx:
            keep.update(held(ffn_ctx, (
                ("sel", [P, TILES, EXP], F32), ("cw", [P, TILES, EXP], F32),
                ("sup_hi", [P, KM, 2 * SPAD], F32R), ("sup_lo", [P, KM, 2 * SPAD], F32R), ("sdn_hi", [P, KS, DM], F32R), ("sdn_lo", [P, KS, DM], F32R))))
            keep.update(held(ffn_ctx, [(name, shape, F32) for name, shape in (*ROUTE.items(), ("last_logits", [P, TB, EXP]))]))
            keep.update({name: ffn_ctx.enter_context(nc.semaphore(name)) for name in ("rank_step", "exp_done")})
            mix(nc, keep, x1_d, d["adapters"], d, x2_d, x2T_d)
            shared(nc, keep, x1_d, x2T_d, d, list_d, out_d)
        experts(nc, keep, d["up_T"], d["dn_T"], x2_d, list_d, out_d)


def layouts(inputs):
    def get(name):
        return np.asarray(inputs[name])

    def turned(w):
        chunks = -(-w.shape[1] // P)
        padded = np.zeros((chunks * P, w.shape[0]), w.dtype)
        padded[:w.shape[1]] = w.T
        return padded.reshape(chunks, P, w.shape[0]).transpose(1, 0, 2)

    def lower(n):
        return np.broadcast_to(np.tril(np.ones((n, n), np.float32), -1), (P, n, n))

    x = get("x")
    no_rows = np.zeros((BB,) + x.shape[1:], x.dtype)
    subjects = get("itok_B_0_7")
    per_channel = np.concatenate([get("L0_attn_A_log"), get("L0_attn_conv1d_w"), get("L0_attn_dt_proj_bias")[:, None],
                                  get("L0_attn_D_param")[:, None]], 1)
    gate, up = np.split(get("L0_ffn_shared_up_w"), 2)
    rows = np.zeros((SPAD - SINNER, DM), gate.dtype)
    row_adapter = np.repeat(np.arange(NADAPT, dtype=np.float32), LRANK)
    pad_list = np.zeros((P, LIST_TILES, 2), np.int32)
    pad_list[:, :, 0] = TOK + np.arange(P)[:, None]
    restart = np.ones((P, EXP, TILES), np.float32)
    restart[:, :, 0] = 0
    arrays = {
        "x_pad": np.concatenate([no_rows, x, no_rows, no_rows]),
        "subjects": np.concatenate([subjects, np.zeros(2 * BB, subjects.dtype)])[:, None],
        "cond_w": get("L0_cond_weights").reshape(SUBJ, SEQ * SEQ),
        "cond_b": get("fside_8xS_0"),
        "in_T": turned(get("L0_attn_in_proj_w")),
        "xp_T": turned(get("L0_attn_x_proj_w")),
        "dt_T": get("L0_attn_dt_proj_w").T,
        "out_T": turned(get("L0_attn_out_proj_w")),
        "chan": per_channel.reshape(DT, P, -1).transpose(1, 0, 2),
        "ident": np.eye(P, dtype=np.float32),
        "adapters": get("itok_B_0_6")[None],
        "row_scale": np.stack([row_adapter, np.repeat(get("L0_cond2_scalings"), LRANK)], 1),
        "tri_g": lower(GROUPS),
        "tri_e": lower(EXP),
        "a_T": turned(get("L0_cond2_A").reshape(NADAPT * LRANK, DM)),
        "w_T": turned(get("L0_cond2_W")),
        "b_T": get("L0_cond2_Bm").transpose(0, 2, 1).reshape(NADAPT * LRANK, DM),
        "gate_T": turned(get("L0_ffn_gate_w")),
        "sup_T": np.concatenate([turned(np.concatenate([gate, rows])), turned(np.concatenate([up, rows]))], 2),
        "sdn_T": turned(get("L0_ffn_shared_down_w")),
        "pad_list": pad_list,
        "tokens": np.arange(TOK, dtype=np.int32).reshape(TILES, P).T,
        "strict": np.triu(np.ones((P, P), np.float32), 1),
        "ones": np.ones((P, P), np.float32),
        "restart": restart,
        "steps": np.broadcast_to(P * np.arange(TILES, dtype=np.float32), (P, TILES)),
        "numbers": np.arange(LIST_TILES, dtype=np.float32)[None],
        "up_T": np.stack([turned(w) for w in get("L0_ffn_expert_up_w")]),
        "dn_T": np.stack([turned(w) for w in get("L0_ffn_expert_down_w")]),
    }
    return {f"in_{name}": np.ascontiguousarray(a) for name, a in arrays.items()}


def kernel(**inputs):
    import concourse.bacc as bacc
    from concourse.bass_utils import run_bass_kernel_spmd

    nc = bacc.Bacc("TRN2", target_bir_lowering=False, num_devices=1)
    arrays = layouts(inputs)
    d = {name[3:]: nc.dram_tensor(name, a.shape, mybir.dt.from_np(a.dtype), kind="ExternalInput").ap()
         for name, a in arrays.items()}
    out_d = nc.dram_tensor("out", [TOK + P, DM], F32, kind="ExternalOutput").ap()
    layer(nc, d, out_d)
    r = run_bass_kernel_spmd(nc, [arrays], core_ids=[0])
    return r.results[0]["out"][:TOK].reshape(BATCH, SEQ, DM)
```
